# Optimizing a Trainium2 kernel written in Bass

```python
import numpy as np
import jax
import jax.numpy as jnp

def _softmax(x, axis=-1):
    return jax.nn.softmax(x, axis=axis)

def _gelu(x):
    return jax.nn.gelu(x, approximate=True)

def _silu(x):
    return jax.nn.silu(x)

def _sigmoid(x):
    return jax.nn.sigmoid(x)

def _layernorm(x, axis=-1, eps=1e-05):
    m = jnp.mean(x, axis=axis, keepdims=True)
    v = jnp.var(x, axis=axis, keepdims=True)
    return (x - m) / jnp.sqrt(v + eps)

def _scatter_add(tgt, idx, src, axis=0):
    return tgt.at[idx].add(src)

def _segment_sum(src, seg, n):
    return jax.ops.segment_sum(src, seg, n)
kernel_name = 'mk_gps_d2_gnn_r32_5e556d'

def setup_inputs(seed: int=0):
    np.random.seed(seed)
    _w = jnp.asarray

    def _rec_inputs():
        import jax
        import jax.numpy as jnp
        _gk = jax.random.key(seed)
        x = -0.0002117 + 1 * jax.random.normal(jax.random.fold_in(_gk, 1), (3125, 256), jnp.float32)
        src = jax.random.randint(jax.random.fold_in(_gk, 2), (50000,), 0, 3125, jnp.int32)
        dst = jax.random.randint(jax.random.fold_in(_gk, 3), (50000,), 0, 3125, jnp.int32)
        _o = jnp.argsort(dst, stable=True)
        src = src[_o]
        dst = dst[_o]
        edge_type_8 = jax.random.randint(jax.random.fold_in(_gk, 13), (50000,), 0, 8, jnp.int32)
        return (x, src, dst, edge_type_8)
    x, src, dst, edge_type_8 = _rec_inputs()

    def _L0_gnn_setup():
        import jax, jax.numpy as jnp
        import numpy as np
        N = 3125
        E = 100000
        IN_DIM = 256

        def _edge_vals(rows):
            deg = jnp.zeros((N,), dtype=jnp.float32).at[rows].add(1.0)
            deg = jnp.where(deg == 0, 1.0, deg)
            return 1.0 / deg[rows]

        def _layer(x, rows, cols, vals, W, b):
            neigh = jax.ops.segment_sum(vals[:, None] * x[cols], rows, num_segments=N)
            cat = jnp.concatenate([x, neigh], axis=1)
            return jax.nn.relu(cat @ W.T + b)
        key = jax.random.key(seed)
        k1, k2, k3, k4, k5 = jax.random.split(key, 5)
        features = jax.random.normal(k1, (N, IN_DIM), dtype=jnp.float32)
        rows = jax.random.randint(k2, (E,), 0, N, dtype=jnp.int64)
        cols = jax.random.randint(k3, (E,), 0, N, dtype=jnp.int64)
        s0 = 1.0 / np.sqrt(2 * IN_DIM)
        W0 = jax.random.normal(k4, (256, 2 * IN_DIM), dtype=jnp.float32) * s0
        b0 = jnp.zeros((256,), dtype=jnp.float32)
        s1 = 1.0 / np.sqrt(2 * 256)
        W1 = jax.random.normal(k5, (256, 2 * 256), dtype=jnp.float32) * s1
        b1 = jnp.zeros((256,), dtype=jnp.float32)
        return {'features': features, 'rows': rows, 'cols': cols, 'W0': W0, 'b0': b0, 'W1': W1, 'b1': b1}
    _L0_gnn_all = _L0_gnn_setup()
    _L0_gnn_in = {k: v for k, v in _L0_gnn_all.items() if k in ('W0', 'b0', 'W1', 'b1')}
    del _L0_gnn_all

    def _L0_mix_setup():
        import jax, jax.numpy as jnp
        import numpy as np
        D_MODEL = 256
        NUM_HEADS = 8
        DEPTH = D_MODEL // NUM_HEADS
        B, L = (32, 128)

        def _feature_map(x):
            return jax.nn.elu(x) + 1.0
        key = jax.random.key(seed)
        ks = jax.random.split(key, 9)
        sc = 1.0 / np.sqrt(D_MODEL)
        return {'x': jax.random.normal(ks[0], (B, L, D_MODEL), dtype=jnp.float32), 'wq': jax.random.normal(ks[1], (D_MODEL, D_MODEL), dtype=jnp.float32) * sc, 'bq': jnp.zeros((D_MODEL,), dtype=jnp.float32), 'wk': jax.random.normal(ks[2], (D_MODEL, D_MODEL), dtype=jnp.float32) * sc, 'bk': jnp.zeros((D_MODEL,), dtype=jnp.float32), 'wv': jax.random.normal(ks[3], (D_MODEL, D_MODEL), dtype=jnp.float32) * sc, 'bv': jnp.zeros((D_MODEL,), dtype=jnp.float32), 'wo': jax.random.normal(ks[4], (D_MODEL, D_MODEL), dtype=jnp.float32) * sc, 'bo': jnp.zeros((D_MODEL,), dtype=jnp.float32)}
    _L0_mix_all = _L0_mix_setup()
    _L0_mix_in = {k: v for k, v in _L0_mix_all.items() if k in ('wq', 'bq', 'wk', 'bk', 'wv', 'bv', 'wo', 'bo')}
    del _L0_mix_all

    def _L0_ffn_setup():
        import jax, jax.numpy as jnp
        import numpy as np
        BN_EPS = 0.001

        def _bn(h, g, b, m, v):
            return g * (h - m) * jax.lax.rsqrt(v + BN_EPS) + b
        key = jax.random.key(seed)
        ks = jax.random.split(key, 8)
        B, F, Df = (256, 64, 256)
        E, H, D = (8, 256, 256)
        s1 = 1.0 / np.sqrt(Df)
        s2 = 1.0 / np.sqrt(H)
        return {'x': jax.random.normal(ks[0], (B, F, Df), jnp.float32), 'Wr': jax.random.normal(ks[1], (Df, E), jnp.float32) * s1, 'br': jnp.zeros((E,), jnp.float32), 'W1': jax.random.normal(ks[2], (E, Df, H), jnp.float32) * s1, 'b1': jnp.zeros((E, H), jnp.float32), 'g1': jnp.ones((E, H), jnp.float32), 'be1': jnp.zeros((E, H), jnp.float32), 'm1': jnp.zeros((E, H), jnp.float32), 'v1': jnp.ones((E, H), jnp.float32), 'W2': jax.random.normal(ks[3], (E, H, H), jnp.float32) * s2, 'b2': jnp.zeros((E, H), jnp.float32), 'g2': jnp.ones((E, H), jnp.float32), 'be2': jnp.zeros((E, H), jnp.float32), 'm2': jnp.zeros((E, H), jnp.float32), 'v2': jnp.ones((E, H), jnp.float32), 'Wo': jax.random.normal(ks[4], (E, H, D), jnp.float32) * s2, 'bo': jnp.zeros((E, D), jnp.float32)}
    _L0_ffn_all = _L0_ffn_setup()
    _L0_ffn_in = {k: v for k, v in _L0_ffn_all.items() if k in ('Wr', 'br', 'W1', 'b1', 'g1', 'be1', 'm1', 'v1', 'W2', 'b2', 'g2', 'be2', 'm2', 'v2', 'Wo', 'bo')}
    del _L0_ffn_all

    def _L1_gnn_setup():
        import jax, jax.numpy as jnp
        import numpy as np
        NUM_NODES = 50000
        NUM_EDGES = 25000
        IN_DIM = 256
        OUT_DIM = 256
        NUM_RELATIONS = 8
        key = jax.random.key(seed)
        k1, k2, k3, k4 = jax.random.split(key, 4)
        node_repr = jax.random.normal(k1, (NUM_NODES, IN_DIM), dtype=jnp.float32)
        edge_index = jax.random.randint(k2, (2, NUM_EDGES), 0, NUM_NODES, dtype=jnp.int64)
        edge_types = jax.random.randint(k3, (NUM_EDGES,), 0, NUM_RELATIONS, dtype=jnp.int64)
        limit = float(np.sqrt(6.0 / (IN_DIM + OUT_DIM)))
        weight = jax.random.uniform(k4, (NUM_RELATIONS, OUT_DIM, IN_DIM), dtype=jnp.float32, minval=-limit, maxval=limit)
        bias = jnp.zeros((OUT_DIM,), dtype=jnp.float32)
        return {'node_repr': node_repr, 'weight': weight, 'bias': bias, 'edge_index': edge_index, 'edge_types': edge_types}
    _L1_gnn_all = _L1_gnn_setup()
    _L1_gnn_in = {k: v for k, v in _L1_gnn_all.items() if k in ('weight', 'bias')}
    del _L1_gnn_all

    def _L1_mix_setup():
        import jax, jax.numpy as jnp
        import numpy as np
        HEADS = 8
        DIM_HEAD = 64
        EPS = 1e-05

        def _inst_norm(t):
            mu = jnp.mean(t, axis=-1, keepdims=True)
            var = jnp.var(t, axis=-1, keepdims=True)
            return (t - mu) / jnp.sqrt(var + EPS)
        key = jax.random.key(seed)
        k1, k2, k3, k4 = jax.random.split(key, 4)
        b, n, dim = (4, 256, 256)
        inner = HEADS * DIM_HEAD
        x = jax.random.normal(k1, (b, n, dim), dtype=jnp.float32)
        w_qkv = jax.random.normal(k2, (dim, 3 * inner), dtype=jnp.float32) * (1.0 / DIM_HEAD)
        w_out = jax.random.normal(k3, (inner, dim), dtype=jnp.float32) * dim ** (-0.5)
        b_out = jax.random.normal(k4, (dim,), dtype=jnp.float32) * 0.01
        return {'x': x, 'w_qkv': w_qkv, 'w_out': w_out, 'b_out': b_out}
    _L1_mix_all = _L1_mix_setup()
    _L1_mix_in = {k: v for k, v in _L1_mix_all.items() if k in ('w_qkv', 'w_out', 'b_out')}
    del _L1_mix_all

    def _L1_ffn_setup():
        import jax, jax.numpy as jnp
        import numpy as np
        D_MODEL = 256
        EXPERT_DIM = 512
        NUM_EXPERTS = 8
        TOP_K = 2
        SEQ_LEN = 64
        BATCH = 2
        key = jax.random.key(seed)
        ks = jax.random.split(key, 8)
        s = 0.02
        x = jax.random.normal(ks[0], (SEQ_LEN, BATCH, D_MODEL), dtype=jnp.float32)
        Wg = jax.random.normal(ks[1], (D_MODEL, NUM_EXPERTS), dtype=jnp.float32) * s
        bg = jax.random.normal(ks[2], (NUM_EXPERTS,), dtype=jnp.float32) * s
        bias = jnp.zeros((NUM_EXPERTS,), dtype=jnp.float32)
        W1 = jax.random.normal(ks[3], (NUM_EXPERTS, D_MODEL, EXPERT_DIM), dtype=jnp.float32) * s
        b1 = jax.random.normal(ks[4], (NUM_EXPERTS, EXPERT_DIM), dtype=jnp.float32) * s
        W2 = jax.random.normal(ks[5], (NUM_EXPERTS, EXPERT_DIM, D_MODEL), dtype=jnp.float32) * s
        b2 = jax.random.normal(ks[6], (NUM_EXPERTS, D_MODEL), dtype=jnp.float32) * s
        return {'x': x, 'Wg': Wg, 'bg': bg, 'bias': bias, 'W1': W1, 'b1': b1, 'W2': W2, 'b2': b2}
    _L1_ffn_all = _L1_ffn_setup()
    _L1_ffn_in = {k: v for k, v in _L1_ffn_all.items() if k in ('Wg', 'bg', 'bias', 'W1', 'b1', 'W2', 'b2')}
    del _L1_ffn_all
    return {'x': x, 'src': src, 'dst': dst, 'edge_type_8': edge_type_8, 'L0_gnn_W0': _L0_gnn_in['W0'], 'L0_gnn_b0': _L0_gnn_in['b0'], 'L0_gnn_W1': _L0_gnn_in['W1'], 'L0_gnn_b1': _L0_gnn_in['b1'], 'L0_mix_wq': _L0_mix_in['wq'], 'L0_mix_bq': _L0_mix_in['bq'], 'L0_mix_wk': _L0_mix_in['wk'], 'L0_mix_bk': _L0_mix_in['bk'], 'L0_mix_wv': _L0_mix_in['wv'], 'L0_mix_bv': _L0_mix_in['bv'], 'L0_mix_wo': _L0_mix_in['wo'], 'L0_mix_bo': _L0_mix_in['bo'], 'L0_ffn_Wr': _L0_ffn_in['Wr'], 'L0_ffn_br': _L0_ffn_in['br'], 'L0_ffn_W1': _L0_ffn_in['W1'], 'L0_ffn_b1': _L0_ffn_in['b1'], 'L0_ffn_g1': _L0_ffn_in['g1'], 'L0_ffn_be1': _L0_ffn_in['be1'], 'L0_ffn_m1': _L0_ffn_in['m1'], 'L0_ffn_v1': _L0_ffn_in['v1'], 'L0_ffn_W2': _L0_ffn_in['W2'], 'L0_ffn_b2': _L0_ffn_in['b2'], 'L0_ffn_g2': _L0_ffn_in['g2'], 'L0_ffn_be2': _L0_ffn_in['be2'], 'L0_ffn_m2': _L0_ffn_in['m2'], 'L0_ffn_v2': _L0_ffn_in['v2'], 'L0_ffn_Wo': _L0_ffn_in['Wo'], 'L0_ffn_bo': _L0_ffn_in['bo'], 'L1_gnn_weight': _L1_gnn_in['weight'], 'L1_gnn_bias': _L1_gnn_in['bias'], 'L1_mix_w_qkv': _L1_mix_in['w_qkv'], 'L1_mix_w_out': _L1_mix_in['w_out'], 'L1_mix_b_out': _L1_mix_in['b_out'], 'L1_ffn_Wg': _L1_ffn_in['Wg'], 'L1_ffn_bg': _L1_ffn_in['bg'], 'L1_ffn_bias': _L1_ffn_in['bias'], 'L1_ffn_W1': _L1_ffn_in['W1'], 'L1_ffn_b1': _L1_ffn_in['b1'], 'L1_ffn_W2': _L1_ffn_in['W2'], 'L1_ffn_b2': _L1_ffn_in['b2']}

def reference(x, src, dst, edge_type_8, L0_gnn_W0, L0_gnn_b0, L0_gnn_W1, L0_gnn_b1, L0_mix_wq, L0_mix_bq, L0_mix_wk, L0_mix_bk, L0_mix_wv, L0_mix_bv, L0_mix_wo, L0_mix_bo, L0_ffn_Wr, L0_ffn_br, L0_ffn_W1, L0_ffn_b1, L0_ffn_g1, L0_ffn_be1, L0_ffn_m1, L0_ffn_v1, L0_ffn_W2, L0_ffn_b2, L0_ffn_g2, L0_ffn_be2, L0_ffn_m2, L0_ffn_v2, L0_ffn_Wo, L0_ffn_bo, L1_gnn_weight, L1_gnn_bias, L1_mix_w_qkv, L1_mix_w_out, L1_mix_b_out, L1_ffn_Wg, L1_ffn_bg, L1_ffn_bias, L1_ffn_W1, L1_ffn_b1, L1_ffn_W2, L1_ffn_b2):
    import jax
    import jax.numpy as jnp

    def _L0_gnn_ref(features, rows, cols, W0, b0, W1, b1):
        import jax, jax.numpy as jnp
        import numpy as np
        N = 3125
        E = 100000
        IN_DIM = 256

        def _edge_vals(rows):
            deg = jnp.zeros((N,), dtype=jnp.float32).at[rows].add(1.0)
            deg = jnp.where(deg == 0, 1.0, deg)
            return 1.0 / deg[rows]

        def _layer(x, rows, cols, vals, W, b):
            neigh = jax.ops.segment_sum(vals[:, None] * x[cols], rows, num_segments=N)
            cat = jnp.concatenate([x, neigh], axis=1)
            return jax.nn.relu(cat @ W.T + b)
        vals = _edge_vals(rows)
        x = _layer(features, rows, cols, vals, W0, b0)
        x = _layer(x, rows, cols, vals, W1, b1)
        return x

    def _L0_mix_ref(x, wq, bq, wk, bk, wv, bv, wo, bo):
        import jax, jax.numpy as jnp
        import numpy as np
        D_MODEL = 256
        NUM_HEADS = 8
        DEPTH = D_MODEL // NUM_HEADS
        B, L = (32, 128)

        def _feature_map(x):
            return jax.nn.elu(x) + 1.0
        b, l, _ = x.shape
        q = (x @ wq + bq).reshape(b, l, NUM_HEADS, DEPTH)
        k = (x @ wk + bk).reshape(b, l, NUM_HEADS, DEPTH)
        v = (x @ wv + bv).reshape(b, l, NUM_HEADS, DEPTH)
        q = _feature_map(q)
        k = _feature_map(k)
        kv = jnp.einsum('blhd,blhe->bhde', k, v)
        k_sum = jnp.sum(k, axis=1)
        qkv = jnp.einsum('blhd,bhde->blhe', q, kv)
        normalizer = jnp.einsum('blhd,bhd->blh', q, k_sum) + 1e-06
        out = qkv / normalizer[..., None]
        out = out.reshape(b, l, D_MODEL)
        return out @ wo + bo

    def _L0_ffn_ref(x, Wr, br, W1, b1, g1, be1, m1, v1, W2, b2, g2, be2, m2, v2, Wo, bo):
        import jax, jax.numpy as jnp
        import numpy as np
        BN_EPS = 0.001

        def _bn(h, g, b, m, v):
            return g * (h - m) * jax.lax.rsqrt(v + BN_EPS) + b
        feat = jnp.mean(x, axis=0)
        w = jax.nn.softmax(feat @ Wr + br, axis=-1)
        h = jnp.einsum('bfd,edh->bfeh', x, W1) + b1
        h = jax.nn.relu(_bn(h, g1, be1, m1, v1))
        h = jnp.einsum('bfeh,ehk->bfek', h, W2) + b2
        h = jax.nn.relu(_bn(h, g2, be2, m2, v2))
        y = jnp.einsum('bfeh,ehd->bfed', h, Wo) + bo
        return jnp.einsum('bfed,fe->bfd', y, w)

    def _L1_gnn_ref(node_repr, weight, bias, edge_index, edge_types):
        import jax, jax.numpy as jnp
        import numpy as np
        NUM_NODES = 50000
        NUM_EDGES = 25000
        IN_DIM = 256
        OUT_DIM = 256
        NUM_RELATIONS = 8
        h_all = jnp.einsum('ni,roi->rno', node_repr, weight)
        src, dst = (edge_index[0], edge_index[1])
        msgs = h_all[edge_types, src]
        messages = jax.ops.segment_sum(msgs, dst, num_segments=node_repr.shape[0])
        return messages + bias

    def _L1_mix_ref(x, w_qkv, w_out, b_out):
        import jax, jax.numpy as jnp
        import numpy as np
        HEADS = 8
        DIM_HEAD = 64
        EPS = 1e-05

        def _inst_norm(t):
            mu = jnp.mean(t, axis=-1, keepdims=True)
            var = jnp.var(t, axis=-1, keepdims=True)
            return (t - mu) / jnp.sqrt(var + EPS)
        b, n, dim = x.shape
        qkv = x @ w_qkv
        q, k, v = jnp.split(qkv, 3, axis=-1)
        to_heads = lambda t: t.reshape(b, n, HEADS, DIM_HEAD).transpose(0, 2, 1, 3)
        q, k, v = (to_heads(q), to_heads(k), to_heads(v))
        k = _inst_norm(k)
        v = _inst_norm(v)
        dots = jnp.einsum('bhnd,bhne->bhde', k, v)
        out = jnp.einsum('bhnd,bhde->bhne', q, dots) * (1.0 / n)
        out = out.transpose(0, 2, 1, 3).reshape(b, n, HEADS * DIM_HEAD)
        return out @ w_out + b_out

    def _L1_ffn_ref(x, Wg, bg, bias, W1, b1, W2, b2):
        import jax, jax.numpy as jnp
        import numpy as np
        D_MODEL = 256
        EXPERT_DIM = 512
        NUM_EXPERTS = 8
        TOP_K = 2
        SEQ_LEN = 64
        BATCH = 2
        x_flat = x.reshape(-1, D_MODEL)
        gate_logits = x_flat @ Wg + bg + bias
        topk_vals, topk_idx = jax.lax.top_k(gate_logits, TOP_K)
        topk_w = jax.nn.softmax(topk_vals, axis=-1)
        combine = (jax.nn.one_hot(topk_idx, NUM_EXPERTS, dtype=x.dtype) * topk_w[..., None]).sum(axis=1)
        h = jax.nn.relu(jnp.einsum('td,edh->teh', x_flat, W1) + b1)
        y = jnp.einsum('teh,ehd->ted', h, W2) + b2
        out = jnp.einsum('ted,te->td', y, combine)
        return out.reshape(x.shape)
    edge_index = jnp.stack([src, dst])
    xn = _layernorm(x, axis=-1)
    x = x + _L0_gnn_ref(xn, src, dst, L0_gnn_W0, L0_gnn_b0, L0_gnn_W1, L0_gnn_b1) + _L0_mix_ref(xn[None], L0_mix_wq, L0_mix_bq, L0_mix_wk, L0_mix_bk, L0_mix_wv, L0_mix_bv, L0_mix_wo, L0_mix_bo)[0]
    x = x + _L0_ffn_ref(_layernorm(x, axis=-1)[None], L0_ffn_Wr, L0_ffn_br, L0_ffn_W1, L0_ffn_b1, L0_ffn_g1, L0_ffn_be1, L0_ffn_m1, L0_ffn_v1, L0_ffn_W2, L0_ffn_b2, L0_ffn_g2, L0_ffn_be2, L0_ffn_m2, L0_ffn_v2, L0_ffn_Wo, L0_ffn_bo)[0]
    xn = _layernorm(x, axis=-1)
    x = x + _L1_gnn_ref(xn, L1_gnn_weight, L1_gnn_bias, edge_index, edge_type_8) + _L1_mix_ref(xn[None], L1_mix_w_qkv, L1_mix_w_out, L1_mix_b_out)[0]
    x = x + _L1_ffn_ref(_layernorm(x, axis=-1)[None], L1_ffn_Wg, L1_ffn_bg, L1_ffn_bias, L1_ffn_W1, L1_ffn_b1, L1_ffn_W2, L1_ffn_b2)[0]
    return x

_drawn_inputs = setup_inputs


def setup_inputs(seed=0):
    import zlib

    import numpy as np

    out = dict(_drawn_inputs(seed))
    spreads = {'L0_gnn_b0': (0.0, 0.1),
     'L0_gnn_b1': (0.0, 0.1),
     'L0_mix_bq': (0.0, 0.8),
     'L0_mix_bk': (0.0, 0.8),
     'L0_mix_bv': (0.0, 0.1),
     'L0_mix_bo': (0.0, 0.1),
     'L0_ffn_br': (0.0, 0.1),
     'L0_ffn_b1': (0.0, 0.307),
     'L0_ffn_g1': (1.0, 0.2),
     'L0_ffn_be1': (0.0, 0.307),
     'L0_ffn_m1': (0.0, 0.304),
     'L0_ffn_v1': (1.0, 0.588),
     'L0_ffn_b2': (0.0, 0.1),
     'L0_ffn_g2': (1.0, 0.2),
     'L0_ffn_be2': (0.0, 0.1),
     'L0_ffn_m2': (0.0, 0.1),
     'L0_ffn_v2': (1.0, 0.2),
     'L0_ffn_bo': (0.0, 0.1),
     'L1_gnn_bias': (0.0, 0.345),
     'L1_ffn_bias': (0.0, 0.8)}
    factors = {'L0_mix_wq': 8.0,
     'L0_mix_wk': 4.383,
     'L1_mix_b_out': 8.0,
     'L1_ffn_Wg': 3.777,
     'L1_ffn_bg': 8.0,
     'L1_ffn_W1': 4.11,
     'L1_ffn_b1': 8.0,
     'L1_ffn_W2': 3.358,
     'L1_ffn_b2': 8.0}
    for name, (base, spread) in spreads.items():
        noise = np.random.default_rng([zlib.crc32(name.encode()), seed]).standard_normal(out[name].shape)
        drawn = base * np.exp(spread * noise) if base else spread * noise
        out[name] = jnp.asarray(drawn.astype(out[name].dtype))
    for name, factor in factors.items():
        out[name] = (out[name] * factor).astype(out[name].dtype)
    return out
```

```python
from contextlib import ExitStack

import concourse.bass as bass
from concourse import mybir

P = 128
N = 3125
D = 256
E = 50000
NT = (N + P - 1) // P
LAST = N - (NT - 1) * P
GT = 4
NG = NT // GT
EP = 125
EC = E // EP
CH = 16
HALF = CH // 2
NCH = (E + NT * (P - 1)) // P
TURNS = (NCH + CH - 1) // CH
SLOTS = TURNS * CH
ROW = D + 4
DS = D + 2
NE = 8
HW = 512
HEAD0 = D // NE
HEAD1 = HW // NE
PSB = 4
COLS = 4
LN_EPS = 1e-5
BN_EPS = 1e-3

F32 = mybir.dt.float32
F16 = mybir.dt.float16
I32 = mybir.dt.int32
U32 = mybir.dt.uint32
ALU = mybir.AluOpType
ACT = mybir.ActivationFunctionType
AX = mybir.AxisListType
ds = bass.ds


class Steps:

    def __init__(self, eng, sem):
        self.eng, self.sem, self.base = eng, sem, 0
        self.t = self.per = self.k = 0

    def did(self, ins):
        ins.then_inc(self.sem, 1)
        self.k += 1

    def count(self):
        return self.t * self.per + (self.base + self.k)

    def wait(self):
        self.eng.wait_ge(self.sem, self.count())

    def link(self, ins):
        self.did(ins)
        self.wait()

    def turn(self, t, per):
        if not self.per:
            self.base, self.k = self.base + self.k, 0
        assert not self.per or self.k == self.per, (self.k, self.per)
        self.t, self.per, self.k = t, per, 0

    def ended(self, turns):
        assert self.k == self.per, (self.k, self.per)
        self.base, self.t, self.per, self.k = self.base + turns * self.per, 0, 0, 0


def tiles(eng):
    with eng.Fori(0, NT // 2) as i:
        for s in range(2):
            yield i * 2 + s, s
    yield NT - 1, 0


def groups(eng):
    with eng.Fori(0, NG) as g:
        yield g, GT
    yield NG, NT - NG * GT


def program(nc, T, out, stop=None):
    with ExitStack() as ctx:
        def sb(name, shape, dt=F32):
            return ctx.enter_context(nc.sbuf_tensor(name, shape, dt))

        def sem(name):
            return ctx.enter_context(nc.semaphore(name))

        def dram(name, shape):
            return nc.dram_tensor(name, shape, F32, kind="Internal").ap()

        bank = [ctx.enter_context(nc.psum_tensor(f"bank{i}", [P, 512], F32)) for i in range(8)]

        table0 = dram("table0", (NT * P, ROW))
        table1 = dram("table1", (NT * P, ROW))
        hall = dram("hall", (NE * N, D))

        X = sb("X", [P, NT * D])
        XN = sb("XN", [P, NT * ROW])
        AGG = sb("AGG", [P, (NT + 1) * DS])
        STAT = sb("STAT", [P, NT * 6])
        MV = sb("MV", [P, 8, NT])
        IDX = [sb(f"IDX{i}", [P, SLOTS], I32) for i in range(2)]
        LOC = [sb(f"LOC{i}", [P, SLOTS]) for i in range(2)]
        TIL = [sb(f"TIL{i}", [P, SLOTS], I32) for i in range(2)]
        idxb = sb("idxb", [P, CH], I32)
        ident = sb("ident", [P, P])
        tri = sb("tri", [P, P])
        trin = sb("trin", [P, P])
        ones = sb("ones", [P, P])
        zeros = sb("zeros", [P, 512])
        iotai = sb("iotai", [P, SLOTS], I32)
        iota = sb("iota", [P, SLOTS])
        iota16 = sb("iota16", [P, SLOTS], F16)
        bias = sb("bias", [P, 9, D])
        small = sb("small", [P, 256])
        WA = sb("WA", [P, 16384])
        RA = sb("RA", [P, 7296])

        def view(arena, at, shape):
            n = 1
            for k in shape:
                n *= k
            v = arena[:, at:at + n]
            if len(shape) == 2:
                return v.rearrange("p (a b) -> p a b", b=shape[1])
            if len(shape) == 3:
                return v.rearrange("p (a b c) -> p a b c", b=shape[1], c=shape[2])
            return v

        w1 = view(WA, 0, (NE, 2, D))
        w2 = view(WA, 4096, (NE, 2, D))
        wo = view(WA, 8192, (NE, 2, D))
        gw = [view(WA, 12288 + 1024 * i, (4, D)) for i in range(2)]
        wkv0 = view(WA, 14336, (2, 512))
        wq0 = view(WA, 15360, (2, D))
        wo0 = view(WA, 15872, (2, D))
        wr = view(WA, 0, (2, NE * D))
        wkv1 = view(WA, 4096, (2, 2 * HW))
        wqT1 = view(WA, 6144, (4, D))
        wout1 = view(WA, 7168, (4, D))
        DT = view(WA, 8192, (4, P))
        MP = view(WA, 8704, (4, D))
        WEFF = view(WA, 9728, (2, D))
        v1 = view(WA, 0, (NE, 2, HW))
        v2 = view(WA, 8192, (NE, 4, D))
        bo_e = sb("bo_e", [NE, D])
        b2_e = sb("b2_e", [NE, D])
        wr0 = sb("wr0", [P, 2, NE])
        wg1 = sb("wg1", [P, 2, NE])
        gate_b = sb("gate_b", [P, 3, NE])
        bn = sb("bn", [P, 10, 2 * NE])
        sc = sb("sc", [P, 4, 2 * NE])
        hb = sb("hb", [P, NE * 4])
        bq = sb("bq", [P, 2])
        kvbd = sb("kvbd", [P, 2, D + NE])

        oh = view(WA, 0, (NT, EC))
        zrow = WA[:, 10000:10400]
        pos = WA[:, 10400:10800]
        scan = [WA[:, 10800:11200], WA[:, 11200:11600]]
        tmpf = [WA[:, 11600 + 400 * i:12000 + 400 * i] for i in range(6)]
        tmpi = [WA[:, 14000 + 400 * i:14400 + 400 * i].bitcast(I32) for i in range(5)]
        edges = [RA[:, 400 * i:400 * i + 400].bitcast(I32) for i in range(3)]
        permA = [RA[:, 1200 + 128 * s:1328 + 128 * s].bitcast(F16) for s in range(COLS)]
        permR = [RA[:, 1712 + 208 * s:1920 + 208 * s].bitcast(F16) for s in range(COLS)]
        cnt = small[:, 0:NT]
        z16 = RA[:, 2600:2664].bitcast(F16)
        ring = view(RA, 0, (CH, ROW))
        hot = view(RA, CH * ROW, (CH, P))
        xin = [RA[:, 256 * s:256 * s + 256] for s in range(2)]
        xT = [view(RA, 512 + 256 * s, (2, P)) for s in range(2)]
        kb = [RA[:, 1024 + 256 * s:1280 + 256 * s] for s in range(2)]
        eb = [RA[:, 1536 + 256 * s:1792 + 256 * s] for s in range(2)]
        mb = [RA[:, 2048 + 256 * s:2304 + 256 * s] for s in range(2)]
        kf = [RA[:, 2560 + 256 * s:2816 + 256 * s] for s in range(2)]
        vb = [RA[:, 3072 + 258 * s:3330 + 258 * s] for s in range(2)]
        of = [RA[:, 3600 + 256 * s:3856 + 256 * s] for s in range(2)]
        oT = [view(RA, 4112 + 256 * s, (2, P)) for s in range(2)]
        nr = [RA[:, 4624 + 16 * s:4640 + 16 * s] for s in range(2)]
        cT = [view(RA, 4656 + 512 * s, (4, P)) for s in range(2)]
        nb = [RA[:, 5680 + 256 * s:5936 + 256 * s] for s in range(2)]
        ho = [RA[:, 1024 + 2048 * s:3072 + 2048 * s] for s in range(2)]
        sq = RA[:, 5120:6144]
        kc = RA[:, 6144:6656]
        vc = RA[:, 6656:7168]
        rs = RA[:, 7168:7232]
        xg = view(RA, 0, (2, GT * P))
        xgin = view(RA, 1024, (GT, D))
        h1 = [view(RA, 2048 + 1024 * s, (2, GT * P)) for s in range(2)]
        h2 = [view(RA, 4096 + 1024 * s, (2, GT * P)) for s in range(2)]
        rt = view(RA, 6144, (8, GT * NE))
        wT = RA[0:NE, 6400:6400 + GT * P]
        hw = [view(RA, 2048 + 2048 * s, (4, GT * P)) for s in range(2)]
        rt1 = view(RA, 6144, (10, GT * NE))
        wT1 = RA[0:NE, 6500:6500 + GT * P]

        def xt(t):
            return X[:, ds(t * D, D)]

        consts = sem("consts")
        pool_step, dve_step, act_step = sem("pool_step"), sem("dve_step"), sem("act_step")
        phase = sem("phase")
        x_in = sem("x_in")
        edges_in = sem("edges_in")
        w_in = sem("w_in")
        w2_in = sem("w2_in")
        w3_in = sem("w3_in")
        stored = sem("stored")
        hall_stored = [sem(f"hall_stored{s}") for s in range(2)]
        out_stored = sem("out_stored")
        x_pad = sem("x_pad")
        var_ready, std_ready = sem("var_ready"), sem("std_ready")
        counts_ready, prefix_ready = sem("counts_ready"), sem("prefix_ready")
        nch_ready, chend_ready, ge_ready, til_ready = (sem(n) for n in ("nch_ready", "chend_ready", "ge_ready", "til_ready"))
        perm_ready, perm_used, perm_done = sem("perm_ready"), sem("perm_used"), sem("perm_done")
        idx_ready, hot_ready = sem("idx_ready"), sem("hot_ready")
        gathered = [sem(f"gathered{s}") for s in range(CH)]
        summed = sem("summed")
        added = sem("added")
        class Barrier:
            def __init__(self, eng):
                self.eng, self.n = eng, 0

            def __call__(self):
                self.n += 1
                self.eng.drain().then_inc(phase, 1)
                self.eng.wait_ge(phase, 5 * self.n)

        S = {n: sem(n) for n in (
            "c1_in c1_T c1_xT c1_p c1_v c1_kb c1_e c1_kf c1_kv kv_done "
            "c2_in c2_T c2_xT c2_q c2_qb c2_e c2_qf c2_n c2_o c2_oT c2_oTs c2_y c2_x "
            "d_in d_nb d_T d_cT d_y d_u "
            "f_in f_T f_xT f_r f_rm f_re f_w f_wT f_wTs f_b f_bx f_l1 f_h1 f_l2 f_h2 f_y f_acc "
            "wkv_c g_in g_T g_xT g_kvp g_h g_ha g_hd g_sq g_var g_std g_kc g_vc g_dt g_dtr g_mp g_mps g_we g_wes "
            "i_in i_T i_xT i_y i_x "
            "j_in j_T j_xT j_r j_d j_e j_oh j_w j_wT j_wTs j_b j_bx j_l1 j_h1 j_y j_acc").split()}
        CREDIT = {
            "act": {"c1_in": 2, "c1_xT": 2, "c1_e": 2, "c2_in": 2, "c2_xT": 2, "c2_oTs": 2, "d_in": 2, "d_cT": 2,
                    "f_h1": 2, "f_h2": 2, "g_vc": 1, "g_ha": 1, "j_xT": 1, "g_xT": 2, "i_xT": 2, "j_h1": 2},
            "pe": {"c1_T": 2, "c1_p": 2, "c1_kv": 2, "c2_T": 2, "c2_q": 2, "c2_n": 2, "c2_oT": 2, "c2_y": 2,
                   "d_T": 2, "d_y": 2, "f_l2": 3, "f_T": 1, "g_dt": 1, "j_T": 1, "f_l1": 1, "j_l1": 1, "f_y": 2, "g_T": 2, "i_T": 2, "i_y": 2, "j_y": 2},
            "dve": {"c1_v": 2, "c1_kf": 2, "c2_qf": 2, "c2_o": 2, "c2_x": 2, "d_nb": 2, "d_u": 2, "g_in": 2, "i_in": 2,
                    "g_var": 1, "f_bx": 1, "f_acc": 1, "g_kc": 1, "g_hd": 1, "j_bx": 1, "j_acc": 1,
                    "i_x": 2},
        }
        FREE, READY = 1, 3

        def wait_alone(eng, signal, value):
            if not isinstance(value, int):
                value = eng.to_reg(value)
                eng.wait_ge(consts, 6)
            eng.wait_ge(signal, value)

        block = ctx.enter_context(nc.Block())

        @block.sync
        def _(sp):
            barrier = Barrier(sp)
            for s in range(2):
                sp.sem_inc(hall_stored[s], 16)
            sp.wait_ge(x_pad, 1)
            sp.dma_start(X[:, 0:(NT - 1) * D].rearrange("p (t d) -> p t d", d=D),
                         T["x"][0:(NT - 1) * P, :].rearrange("(t p) d -> p t d", p=P)).then_inc(x_in, 16)
            sp.dma_start(X[0:LAST, (NT - 1) * D:NT * D], T["x"][(NT - 1) * P:N, :]).then_inc(x_in, 16)
            for i, n in enumerate(("src", "dst", "edge_type_8")):
                sp.dma_start(edges[i][0:EP, :], T[n].rearrange("(p c) -> p c", c=EC)).then_inc(edges_in, 16)
            for i, n in enumerate(("L0_mix_bk", "L0_mix_bv", "L0_mix_bo", "L0_gnn_b0", "L0_gnn_b1", "L1_gnn_bias", "L1_mix_b_out")):
                sp.dma_start(bias[:, i, :], T[n].partition_broadcast(P)).then_inc(w_in, 16)
            sp.dma_start(bq[:, :], T["bq"]).then_inc(w_in, 16)
            for i, n in enumerate(("L0_ffn_br", "L1_ffn_bg", "L1_ffn_bias")):
                sp.dma_start(gate_b[:, i, :], T[n].partition_broadcast(P)).then_inc(w_in, 16)
            sp.dma_start(bn[:, :, :], T["bn"]).then_inc(w_in, 16)
            sp.dma_start(hb[:, :], T["hb"]).then_inc(w_in, 16)
            sp.dma_start(bo_e[:, :], T["L0_ffn_bo"]).then_inc(w_in, 16)
            sp.dma_start(b2_e[:, :], T["L1_ffn_b2"]).then_inc(w_in, 16)
            sp.dma_start(wr0[:, :, :], T["L0_ffn_Wr"].rearrange("(k p) n -> p k n", p=P)).then_inc(w_in, 16)
            sp.dma_start(wg1[:, :, :], T["L1_ffn_Wg"].rearrange("(k p) n -> p k n", p=P)).then_inc(w_in, 16)
            barrier()
            sp.dma_start(table0.rearrange("(t p) d -> p t d", p=P),
                         XN[:, :].rearrange("p (t d) -> p t d", d=ROW)).then_inc(stored, 16)
            sp.wait_ge(stored, 16)
            barrier()
            for e in range(NE):
                for dst, n in ((w1, "L0_ffn_W1"), (w2, "L0_ffn_W2"), (wo, "L0_ffn_Wo")):
                    sp.dma_start(dst[:, e, :, :], T[n][e].rearrange("(k p) n -> p k n", p=P)).then_inc(w2_in, 16)
            for dst, n in ((gw[0], "W0T"), (gw[1], "W1T"), (wkv0[:, :, 0:D], "L0_mix_wk"), (wkv0[:, :, D:2 * D], "L0_mix_wv"),
                           (wq0, "L0_mix_wq"), (wo0, "L0_mix_wo")):
                sp.dma_start(dst, T[n].rearrange("(k p) n -> p k n", p=P)).then_inc(w2_in, 16)
            sp.wait_ge(w2_in, 16 * (3 * NE + 6))
            barrier()
            barrier()
            barrier()
            barrier()
            barrier()
            sp.dma_start(table1.rearrange("(t p) d -> p t d", p=P),
                         XN[:, :].rearrange("p (t d) -> p t d", d=ROW)).then_inc(stored, 16)
            sp.wait_ge(stored, 32)
            barrier()
            barrier()
            barrier()
            barrier()
            for dst, n in ((wr, "WrT"), (wkv1, "wkv"), (wqT1, "wqT"), (wout1, "L1_mix_w_out")):
                sp.dma_start(dst, T[n].rearrange("(k p) n -> p k n", p=P)).then_inc(w3_in, 16)
            sp.wait_ge(w3_in, 64)
            barrier()
            hall_v = hall.rearrange("(r n) d -> n r d", n=N)
            for t, s in tiles(sp):
                rows = LAST if isinstance(t, int) else P
                sp.wait_ge(S["g_ha"], t * 2 + 2 + 1)
                sp.wait_ge(S["g_hd"], t * 2 + 2 + 1)
                if rows == P:
                    src = hall_v[ds(t * P, P), :, :]
                else:
                    src = hall_v[(NT - 1) * P:N, :, :]
                sp.dma_start(src, ho[s][0:rows, :].rearrange("p (r d) -> p r d", r=NE)).then_inc(hall_stored[s], 16)
            sp.wait_ge(hall_stored[0], 16 * 14)
            sp.wait_ge(hall_stored[1], 16 * 13)
            barrier()
            barrier()
            barrier()
            for e in range(NE):
                sp.dma_start(v1[:, e, :, :], T["L1_ffn_W1"][e].rearrange("(k p) n -> p k n", p=P)).then_inc(w3_in, 16)
                sp.dma_start(v2[:, e, :, :], T["L1_ffn_W2"][e].rearrange("(k p) n -> p k n", p=P)).then_inc(w3_in, 16)
            sp.wait_ge(w3_in, 64 + 16 * 2 * NE)
            barrier()
            barrier()
            sp.dma_start(out[0:(NT - 1) * P, :].rearrange("(t p) d -> p t d", p=P),
                         X[:, 0:(NT - 1) * D].rearrange("p (t d) -> p t d", d=D)).then_inc(out_stored, 16)
            sp.dma_start(out[(NT - 1) * P:N, :], X[0:LAST, (NT - 1) * D:NT * D]).then_inc(out_stored, 16)
            sp.wait_ge(out_stored, 32)

        @block.gpsimd
        def _(pool):
            barrier = Barrier(pool)
            pool.memset(X[:, (NT - 1) * D:NT * D], 0.0).then_inc(x_pad, 1)
            pool.memset(ident[:, :], 0.0).then_inc(pool_step, 1)
            pool.memset(ones[:, :], 1.0).then_inc(pool_step, 1)
            pool.memset(zeros[:, :], 0.0).then_inc(consts, 1)
            pool.memset(XN[:, :], 1.0).then_inc(consts, 1)
            pool.iota(iotai[:, :], pattern=[[1, SLOTS]], base=0, channel_multiplier=0).then_inc(consts, 1)
            pool.wait_ge(pool_step, 2)
            pool.affine_select(out=ident[:, :], in_=ident[:, :], compare_op=ALU.not_equal, fill=1.0, base=0,
                               pattern=[[-1, P]], channel_multiplier=1).then_inc(consts, 1)
            pool.affine_select(out=tri[:, :], in_=ones[:, :], compare_op=ALU.is_gt, fill=0.0, base=0,
                               pattern=[[1, P]], channel_multiplier=-1).then_inc(consts, 1)
            pool.affine_select(out=trin[:, :], in_=ones[:, :], compare_op=ALU.is_ge, fill=0.0, base=0,
                               pattern=[[1, P]], channel_multiplier=-1).then_inc(consts, 1)
            for _ in range(5):
                barrier()

            def gather(layer, table, cols):
                with pool.Fori(0, TURNS) as i:
                    for h in range(2):
                        wait_alone(pool, idx_ready, i * 2 + (2 * TURNS * layer + h + 1))
                        for s in range(h * HALF, (h + 1) * HALF):
                            pool.indirect_dma_start(out=ring[:, s, 0:cols], out_offset=None, in_=table,
                                                    in_offset=bass.IndirectOffsetOnAxis(ap=idxb[:, s:s + 1], axis=0)
                                                    ).then_inc(gathered[s], 16)

            gather(0, table0[:, :], ROW)
            barrier()
            barrier()
            barrier()
            gather(1, table1[:, :], ROW)
            for _ in range(5):
                barrier()
            gather(2, hall[:, :], D)
            for _ in range(4):
                barrier()

        @block.vector
        def _(dve):
            barrier = Barrier(dve)
            st = Steps(dve, dve_step)
            for name, k in CREDIT["dve"].items():
                dve.sem_inc(S[name], k)
            dve.sem_inc(added, PSB)

            def stats(n):
                with dve.Fori(0, NT) as t:
                    st.turn(t, 1)
                    st.did(dve.bn_stats(STAT[:, ds(t * 6, 6)], xt(t)))
                st.ended(NT)
                st.wait()
                f = STAT[:, :].rearrange("p (t c) -> p c t", c=6)
                st.did(dve.tensor_tensor(MV[:, 2, :], f[:, 1, :], f[:, 4, :], ALU.add))
                st.did(dve.tensor_tensor(MV[:, 3, :], f[:, 1, :], f[:, 4, :], ALU.subtract))
                st.link(dve.tensor_tensor(MV[:, 4, :], f[:, 2, :], f[:, 5, :], ALU.add))
                st.did(dve.tensor_scalar(MV[:, 0, :], MV[:, 2, :], 0.5, None, ALU.mult))
                st.link(dve.scalar_tensor_tensor(MV[:, 5, :], MV[:, 3, :], 0.25, MV[:, 3, :], ALU.mult, ALU.mult))
                st.link(dve.scalar_tensor_tensor(MV[:, 6, :], MV[:, 4, :], 1.0 / D, MV[:, 5, :], ALU.mult, ALU.add))
                dve.tensor_scalar(MV[:, 7, :], MV[:, 6, :], LN_EPS, None, ALU.add).then_inc(var_ready, 1)
                dve.wait_ge(std_ready, n)
                st.link(dve.reciprocal(MV[:, 1, :], MV[:, 2, :]))

            def norm(dst, t):
                return dve.tensor_scalar(dst, xt(t), MV[:, 0, ds(t, 1)], MV[:, 1, ds(t, 1)], ALU.subtract, ALU.mult)

            dve.wait_ge(consts, 6)
            st.did(dve.tensor_copy(iota[:, :], iotai[:, :]))
            st.link(dve.tensor_copy(iota16[:, :], iotai[:, :]))
            dve.wait_ge(x_in, 32)
            stats(1)
            with dve.Fori(0, NT) as t:
                st.turn(t, 1)
                st.did(norm(XN[:, ds(t * ROW, D)], t))
            st.ended(NT)
            barrier()

            def sort(n):
                key, other = edges[n][0:EP, :], edges[1 - n][0:EP, :]
                f = [a[0:EP, :] for a in tmpf]
                g = [a[0:EP, :] for a in tmpi]
                st.did(dve.tensor_scalar(g[0], key, 7, None, ALU.logical_shift_right))
                st.did(dve.tensor_scalar(g[1], key, P - 1, None, ALU.bitwise_and))
                st.link(dve.memset(zrow, 0.0))
                st.did(dve.tensor_copy(f[0], g[0]))
                st.link(dve.tensor_copy(f[1], g[1]))
                for b in range(NT):
                    st.did(dve.tensor_scalar(oh[0:EP, b, :], f[0], float(b), 0.0, ALU.is_equal, ALU.add,
                                             accum_out=cnt[0:EP, b:b + 1]))
                st.wait()
                dve.drain().then_inc(counts_ready, 1)
                dve.wait_ge(prefix_ready, n + 1)
                ti = tmpi[2][:, 0:NT]
                c = [small[:, 32 * k:32 * k + NT] for k in range(1, 6)]
                st.link(dve.tensor_scalar(ti, bank[0][:, 32:32 + NT], float(P - 1), None, ALU.add))
                st.link(dve.tensor_scalar(tmpi[3][:, 0:NT], ti, 7, None, ALU.logical_shift_right))
                st.link(dve.tensor_copy(c[0], tmpi[3][:, 0:NT]))
                st.link(dve.tensor_tensor_scan(c[1], c[0], zrow[:, 0:NT], 0.0, ALU.add, ALU.add))
                st.link(dve.tensor_tensor(c[2], c[1], c[0], ALU.subtract))
                st.link(dve.scalar_tensor_tensor(c[3], c[2], float(P), bank[0][:, 0:NT], ALU.mult, ALU.add))
                st.link(dve.tensor_scalar(c[4], c[3], -1.0, None, ALU.add))
                st.link(dve.tensor_scalar(tmpi[2][0:NT, 40:41], bank[0][0:NT, 64:65], float(P - 1), None, ALU.add))
                st.link(dve.tensor_scalar(tmpi[3][0:NT, 40:41], tmpi[2][0:NT, 40:41], 7, None, ALU.logical_shift_right))
                dve.tensor_copy(small[0:NT, 224:225], tmpi[3][0:NT, 40:41]).then_inc(nch_ready, 1)
                dve.wait_ge(chend_ready, n + 1)
                st.link(dve.tensor_copy(small[0:NT, 225:226], bank[0][0:NT, 66:67]))
                dve.tensor_scalar(RA[0:NT, 3000:3000 + SLOTS], iota[0:NT, :], small[0:NT, 225:226], None,
                                  ALU.is_ge).then_inc(ge_ready, 1)
                dve.wait_ge(til_ready, n + 1)
                st.did(dve.tensor_copy(TIL[n][:, :], bank[1][:, 0:SLOTS]))
                st.link(dve.memset(pos, 0.0))
                for b in range(NT):
                    st.link(dve.tensor_tensor_scan(scan[b % 2][0:EP, :], oh[0:EP, b, :], zrow[0:EP, :],
                                                   c[4][0:EP, b:b + 1], ALU.add, ALU.add))
                    st.link(dve.copy_predicated(pos[0:EP, :], oh[0:EP, b, :].bitcast(I32), scan[b % 2][0:EP, :]))
                st.link(dve.tensor_copy(g[2], pos[0:EP, :]))
                st.did(dve.tensor_scalar(g[3], g[2], P - 1, None, ALU.bitwise_and))
                st.link(dve.tensor_scalar(g[4], g[2], 7, None, ALU.logical_shift_right))
                st.did(dve.tensor_copy(f[2], g[3]))
                st.did(dve.tensor_copy(f[3], g[4]))
                if n == 0:
                    st.link(dve.tensor_copy(f[4], other))
                else:
                    st.link(dve.scalar_tensor_tensor(f[4], edges[2][0:EP, :], float(N), other, ALU.mult, ALU.add))
                st.link(dve.tensor_scalar(f[5], f[4], 1.0, float(P), ALU.add, ALU.mult))
                st.link(dve.tensor_tensor(g[0], f[5], f[1], ALU.add))
                st.did(dve.tensor_scalar(g[1], g[0], 11, None, ALU.logical_shift_right))
                st.link(dve.tensor_scalar(g[2], g[0], 2047, None, ALU.bitwise_and))
                st.did(dve.tensor_copy(f[4], g[1]))
                st.link(dve.tensor_copy(f[5], g[2]))
                if n == 0:
                    st.link(dve.memset(z16, 0.0))
                with dve.Fori(0, EC // COLS) as i:
                    for s in range(COLS):
                        q, r, hi, lo = (f[k][:, ds(i * COLS + s, 1)] for k in (2, 3, 4, 5))
                        dve.wait_ge(perm_used, i * COLS + (n * EC + s + 1))
                        dve.tensor_scalar(permA[s][0:EP, 0:P], iota16[0:EP, 0:P], q, hi, ALU.is_equal, ALU.mult)
                        dve.tensor_scalar(permA[s][0:EP, P:2 * P], iota16[0:EP, 0:P], q, lo, ALU.is_equal, ALU.mult)
                        dve.tensor_scalar(permR[s][0:EP, :], iota16[0:EP, :], r, None, ALU.is_equal).then_inc(perm_ready, 1)
                dve.wait_ge(perm_done, n + 1)
                hif, lof, vf = RA[:, 3500:3500 + SLOTS], RA[:, 3916:3916 + SLOTS], RA[:, 4332:4332 + SLOTS]
                vi, ri, li = (RA[:, 4748 + SLOTS * k:4748 + SLOTS * (k + 1)].bitcast(I32) for k in range(3))
                st.link(dve.tensor_copy(lof, bank[3][:, 0:SLOTS]))
                st.link(dve.scalar_tensor_tensor(vf, bank[2][:, 0:SLOTS], 2048.0, lof, ALU.mult, ALU.add))
                st.link(dve.tensor_copy(vi, vf))
                st.did(dve.tensor_scalar(ri, vi, 7, None, ALU.logical_shift_right))
                st.did(dve.tensor_scalar(li, vi, P - 1, None, ALU.bitwise_and))
                st.link(dve.tensor_scalar(hif, vf, float(P), None, ALU.is_lt))
                st.link(dve.tensor_scalar(IDX[n][:, :], ri, -1.0, 0.0, ALU.add, ALU.max))
                st.link(dve.tensor_tensor(LOC[n][:, :], li, hif, ALU.subtract))

            dve.wait_ge(edges_in, 48)
            sort(0)
            sort(1)
            barrier()

            dve.wait_ge(w_in, 16 * 17)
            for k in range(2):
                b, g, be, m, v = (bn[:, 5 * k + j, :] for j in range(5))
                dve.tensor_scalar(sc[:, 2 * k, :], v, BN_EPS, None, ALU.add).then_inc(var_ready, 1)
                dve.wait_ge(std_ready, 2 + k)
                st.link(dve.reciprocal(sc[:, 2 * k, :], sc[:, 2 * k + 1, :]))
                st.did(dve.tensor_tensor(sc[:, 2 * k, :], sc[:, 2 * k, :], g, ALU.mult))
                st.link(dve.tensor_tensor(sc[:, 2 * k + 1, :], b, m, ALU.subtract))
                st.link(dve.tensor_tensor(sc[:, 2 * k + 1, :], sc[:, 2 * k + 1, :], sc[:, 2 * k, :], ALU.mult))
                st.link(dve.tensor_tensor(sc[:, 2 * k + 1, :], sc[:, 2 * k + 1, :], be, ALU.add))
            st.did(dve.tensor_tensor(bias[:, 7, :], bias[:, 5, :], bias[:, 6, :], ALU.add))
            st.did(dve.tensor_tensor(gate_b[:, 1, :], gate_b[:, 1, :], gate_b[:, 2, :], ALU.add))
            for s in range(2):
                st.did(dve.memset(vb[s][:, D:D + 2], 1.0))
            st.link(dve.memset(kvbd[:, :, :], 0.0))
            barrier()

            for t, s in tiles(dve):
                st.turn(t, 1)
                dve.wait_ge(S["c1_p"], t + READY)
                dve.wait_ge(S["c1_kv"], t + FREE)
                p = bank[2 + s]
                dve.tensor_tensor(kb[s], p[:, 0:D], bias[:, 0, :], ALU.add).then_inc(S["c1_kb"], 1)
                dve.tensor_tensor(vb[s][:, 0:D], p[:, D:2 * D], bias[:, 1, :], ALU.add).then_inc(S["c1_v"], 1)
                dve.wait_ge(S["c1_e"], t + READY)
                st.did(dve.tensor_scalar(mb[s], eb[s], 1.0, None, ALU.min))
                st.wait()
                dve.scalar_tensor_tensor(kf[s], kb[s], 0.0, mb[s], ALU.max, ALU.add).then_inc(S["c1_kf"], 1)
            st.ended(NT)
            dve.wait_ge(S["kv_done"], 1)
            for h in range(2):
                for a in range(4):
                    hd = 4 * h + a
                    r = slice(32 * a, 32 * a + 32)
                    st.did(dve.tensor_copy(kvbd[r, h, hd * HEAD0:(hd + 1) * HEAD0],
                                           bank[4 + h][r, hd * HEAD0:(hd + 1) * HEAD0]))
                    st.did(dve.tensor_copy(kvbd[r, h, D + hd:D + hd + 1], bank[4 + h][r, D:D + 1]))
            barrier()
            for t, s in tiles(dve):
                st.turn(t, 3)
                dve.wait_ge(S["c2_q"], t + READY)
                dve.wait_ge(S["c2_n"], t + FREE)
                p = bank[2 + s]
                for m in range(2):
                    ins = dve.tensor_scalar(kb[s][:, m * P:(m + 1) * P], p[:, m * P:(m + 1) * P], bq[:, m:m + 1], 0.0,
                                            ALU.add, ALU.max)
                ins.then_inc(S["c2_qb"], 1)
                dve.wait_ge(S["c2_e"], t + 1)
                dve.scalar_tensor_tensor(kf[s], eb[s], 1.0, kb[s], ALU.min, ALU.add).then_inc(S["c2_qf"], 1)
                dve.wait_ge(S["c2_n"], t + READY)
                n = bank[4 + s]
                st.link(dve.tensor_scalar(nr[s][:, 0:NE], n[:, D:D + NE], 1e-6, None, ALU.add))
                st.link(dve.reciprocal(nr[s][:, NE:2 * NE], nr[s][:, 0:NE]))
                dve.wait_ge(S["c2_oT"], t + FREE)
                dve.tensor_tensor(of[s].rearrange("p (h e) -> p h e", h=NE), n[:, 0:D].rearrange("p (h e) -> p h e", h=NE),
                                  nr[s][:, NE:2 * NE].unsqueeze(2).to_broadcast([P, NE, HEAD0]), ALU.mult
                                  ).then_inc(S["c2_o"], 1)
                dve.wait_ge(S["c2_y"], t + READY)
                st.link(dve.tensor_tensor(xt(t), xt(t), bank[6 + s][:, D:2 * D], ALU.add))
                dve.tensor_tensor(xt(t), xt(t), bias[:, 2, :], ALU.add).then_inc(S["c2_x"], 1)
            st.ended(NT)
            barrier()

            def refill(n, layer, i, h):
                a = h * HALF
                wait_alone(dve, summed, i * CH + (SLOTS * layer + a + HALF))
                dve.tensor_copy(idxb[:, a:a + HALF], IDX[n][:, ds(i * CH + a, HALF)]).then_inc(idx_ready, 1)
                for s in range(a, a + HALF):
                    ins = dve.tensor_scalar(hot[:, s, :], iota[:, 0:P], LOC[n][:, ds(i * CH + s, 1)], None, ALU.is_equal)
                ins.then_inc(hot_ready, 1)

            def sums(n, layer, i, h, cols):
                for s in range(h * HALF, (h + 1) * HALF):
                    tile = dve.value_load(TIL[n][0:1, ds(i * CH + s, 1)], min_val=0, max_val=NT)
                    dve.wait_ge(summed, i * CH + (SLOTS * layer + CH + s + 1))
                    dve.wait_ge(added, i * CH + (SLOTS * layer + PSB + s))
                    a = AGG[:, ds(tile * DS, cols)]
                    dve.tensor_tensor(a, a, bank[s % PSB][:, 0:cols], ALU.add).then_inc(added, 1)

            def aggregate(layer):
                n, cols = (0, DS) if layer < 2 else (1, D)
                st.link(dve.memset(AGG[:, :], 0.0))
                for h in range(2):
                    refill(n, layer, 0, h)
                with dve.Fori(0, TURNS - 1) as i:
                    for h in range(2):
                        sums(n, layer, i, h, cols)
                        refill(n, layer, i + 1, h)
                for h in range(2):
                    sums(n, layer, TURNS - 1, h, cols)

            def dense(layer):
                st.did(dve.tensor_scalar(MV[:, 2, :], AGG[:, 0:NT * DS].rearrange("p (t c) -> p c t", c=DS)[:, D, :], 1.0,
                                         None, ALU.max))
                st.wait()
                st.link(dve.reciprocal(MV[:, 3, :], MV[:, 2, :]))
                for t, s in tiles(dve):
                    st.turn(t, 1)
                    dve.wait_ge(S["d_T"], t + (NT * layer + FREE))
                    dve.tensor_scalar(nb[s], AGG[:, ds(t * DS, D)], MV[:, 3, ds(t, 1)], None, ALU.mult).then_inc(S["d_nb"], 1)
                    dve.wait_ge(S["d_y"], t + (NT * layer + READY))
                    st.did(dve.tensor_tensor(mb[s], bank[2 + s][:, 0:D], bias[:, 3 + layer, :], ALU.add))
                    st.wait()
                    if layer == 0:
                        dve.tensor_scalar(XN[:, ds(t * ROW, D)], mb[s], 0.0, None, ALU.max).then_inc(S["d_u"], 1)
                    else:
                        dve.scalar_tensor_tensor(xt(t), mb[s], 0.0, xt(t), ALU.max, ALU.add).then_inc(S["d_u"], 1)
                st.ended(NT)

            aggregate(0)
            barrier()
            dense(0)
            barrier()
            barrier()
            aggregate(1)
            barrier()
            dense(1)
            dve.wait_ge(S["d_u"], 2 + 2 * NT)
            stats(4)
            barrier()

            def x_add(g, n_tiles, e, scale, psum_banks, sig_y, sig_acc, sig_b):
                dve.wait_ge(S[sig_y], g * NE + (e + READY))
                if e == 0:
                    dve.wait_ge(S[sig_b], g + 2)
                else:
                    dve.wait_ge(S[sig_acc], g * NE + (e + 1))
                for j in range(n_tiles):
                    x_ = xt(g * GT + j)
                    ins = dve.scalar_tensor_tensor(x_, bank[psum_banks + j // 2][:, (j % 2) * D:(j % 2 + 1) * D],
                                                   scale[:, j * NE + e:j * NE + e + 1], x_, ALU.mult, ALU.add)
                ins.then_inc(S[sig_acc], 1)

            for g, T_ in groups(dve):
                st.turn(g, 4)
                dve.wait_ge(S["f_T"], g + 1)
                for j in range(T_):
                    ins = norm(xgin[:, j, :], g * GT + j)
                ins.then_inc(S["f_in"], 1)
                dve.wait_ge(S["f_r"], g + 1)
                n = T_ * NE
                v = [rt[:, k, 0:n].rearrange("p (t e) -> p t e", e=NE) for k in range(8)]
                st.link(dve.tensor_tensor(v[0], bank[6][:, 0:n].rearrange("p (t e) -> p t e", e=NE),
                                          gate_b[:, 0:1, :].to_broadcast([P, T_, NE]), ALU.add))
                st.link(dve.tensor_reduce(rt[:, 1, 0:T_], v[0], AX.X, ALU.max))
                dve.tensor_tensor(v[2], v[0], rt[:, 1, 0:T_].unsqueeze(2).to_broadcast([P, T_, NE]), ALU.subtract
                                  ).then_inc(S["f_rm"], 1)
                dve.wait_ge(S["f_re"], g + 1)
                st.link(dve.tensor_reduce(rt[:, 4, 0:T_], v[3], AX.X, ALU.add))
                st.link(dve.reciprocal(rt[:, 5, 0:T_], rt[:, 4, 0:T_]))
                dve.tensor_tensor(v[6], v[3], rt[:, 5, 0:T_].unsqueeze(2).to_broadcast([P, T_, NE]), ALU.mult
                                  ).then_inc(S["f_w"], 1)
                dve.wait_ge(S["f_wT"], g + 1)
                dve.tensor_copy(wT[:, 0:T_ * P], bank[7][0:NE, 0:T_ * P]).then_inc(S["f_wTs"], 1)
                dve.wait_ge(S["f_b"], g + 1)
                for j in range(T_):
                    x_ = xt(g * GT + j)
                    ins = dve.tensor_tensor(x_, x_, bank[6 + j // 2][:, (j % 2) * D:(j % 2 + 1) * D], ALU.add)
                ins.then_inc(S["f_bx"], 1)
                for e in range(NE):
                    x_add(g, T_, e, rt[:, 6, :], 4, "f_y", "f_acc", "f_bx")
            st.ended(NG + 1)
            dve.wait_ge(S["f_acc"], (NG + 1) * NE + 1)
            stats(5)
            barrier()
            barrier()

            st.did(dve.memset(DT[:, :, :], 0.0))
            hv = wkv1.rearrange("p k n -> p (k n)").rearrange("p (h e) -> p h e", e=HEAD1)
            st.link(dve.tensor_reduce(rs[:, 0:32], hv, AX.X, ALU.add))
            st.link(dve.tensor_scalar(rs[:, 32:64], rs[:, 0:32], 1.0 / HEAD1, None, ALU.mult))
            dve.tensor_tensor(hv, hv, rs[:, 32:64].unsqueeze(2).to_broadcast([P, 32, HEAD1]), ALU.subtract
                              ).then_inc(S["wkv_c"], 1)
            for t, s in tiles(dve):
                st.turn(t, 3)
                dve.wait_ge(S["g_T"], t + FREE)
                norm(xin[s], t).then_inc(S["g_in"], 1)
                dve.wait_ge(S["g_sq"], t + 1)
                st.link(dve.tensor_reduce(rs[:, 0:16], sq.rearrange("p (h e) -> p h e", e=HEAD1), AX.X, ALU.add))
                dve.tensor_scalar(rs[:, 16:32], rs[:, 0:16], 1.0 / HEAD1, LN_EPS, ALU.mult, ALU.add).then_inc(S["g_var"], 1)
                for q in range(2, 4):
                    dve.wait_ge(S["g_h"], t * 4 + (q + 1))
                    if q == 2:
                        dve.wait_ge(hall_stored[s], t * 8 + (16 - 8 * s))
                    dve.tensor_copy(ho[s][:, q * 512:(q + 1) * 512], bank[2 + q][:, :]).then_inc(S["g_hd"], 1)
                dve.wait_ge(S["g_std"], t + 1)
                st.link(dve.reciprocal(rs[:, 32:48], rs[:, 48:64]))
                st.link(dve.tensor_tensor(rs[:, 0:8], rs[:, 32:40], rs[:, 40:48], ALU.mult))
                dve.wait_ge(S["g_dt"], t + 1)
                dve.tensor_tensor(kc.rearrange("p (h e) -> p h e", e=HEAD1), bank[6][:, :].rearrange("p (h e) -> p h e", e=HEAD1),
                                  rs[:, 0:8].unsqueeze(2).to_broadcast([P, NE, HEAD1]), ALU.mult).then_inc(S["g_kc"], 1)
            st.ended(NT)
            dve.wait_ge(S["g_dt"], NT + 2)
            b1 = bank[1][:, :].rearrange("p (a b) -> p a b", b=P)
            st.did(dve.tensor_scalar(DT[0:64, :, 0:64], b1[0:64, :, 0:64], 1.0 / N, None, ALU.mult))
            dve.tensor_scalar(DT[64:P, :, 64:P], b1[64:P, :, 64:P], 1.0 / N, None, ALU.mult).then_inc(S["g_dtr"], 1)
            dve.wait_ge(S["g_mp"], 1)
            for h in range(2):
                ins = dve.tensor_copy(MP[:, 2 * h:2 * h + 2, :].rearrange("p a b -> p (a b)"), bank[2 + h][:, :])
            ins.then_inc(S["g_mps"], 1)
            dve.wait_ge(S["g_we"], 1)
            dve.tensor_copy(WEFF.rearrange("p a b -> p (a b)"), bank[4][:, :]).then_inc(S["g_wes"], 1)
            barrier()
            aggregate(2)
            barrier()

            for t, s in tiles(dve):
                st.turn(t, 2)
                dve.wait_ge(S["i_T"], t + FREE)
                norm(xin[s], t).then_inc(S["i_in"], 1)
                dve.wait_ge(S["i_y"], t + READY)
                st.link(dve.tensor_tensor(xt(t), xt(t), bank[2 + s][:, 0:D], ALU.add))
                st.link(dve.tensor_tensor(xt(t), xt(t), AGG[:, ds(t * DS, D)], ALU.add))
                dve.tensor_tensor(xt(t), xt(t), bias[:, 7, :], ALU.add).then_inc(S["i_x"], 1)
            st.ended(NT)
            dve.wait_ge(S["i_x"], NT + 2)
            stats(6)
            barrier()
            barrier()

            for g, T_ in groups(dve):
                st.turn(g, 7)
                dve.wait_ge(S["j_T"], g + 1)
                for j in range(T_):
                    ins = norm(xgin[:, j, :], g * GT + j)
                ins.then_inc(S["j_in"], 1)
                dve.wait_ge(S["j_r"], g + 1)
                n = T_ * NE
                r = [rt1[:, k, :] for k in range(10)]
                v = [a[:, 0:n].rearrange("p (t e) -> p t e", e=NE) for a in r]
                st.did(dve.tensor_tensor(v[0], bank[6][:, 0:n].rearrange("p (t e) -> p t e", e=NE),
                                         gate_b[:, 1:2, :].to_broadcast([P, T_, NE]), ALU.add))
                wait_alone(dve, st.sem, st.count())
                for j in range(T_):
                    ins = dve.max(r[1][:, j * NE:(j + 1) * NE], r[0][:, j * NE:(j + 1) * NE])
                st.did(ins)
                wait_alone(dve, st.sem, st.count())
                for j in range(T_):
                    ins = dve.max_index(r[2][:, j * NE:(j + 1) * NE].bitcast(U32), r[1][:, j * NE:(j + 1) * NE],
                                        r[0][:, j * NE:(j + 1) * NE])
                st.link(ins)
                st.did(dve.tensor_copy(r[3][:, 0:n], r[2][:, 0:n].bitcast(U32)))
                dve.tensor_tensor(r[4][:, 0:T_], v[1][:, :, 1], v[1][:, :, 0], ALU.subtract).then_inc(S["j_d"], 1)
                dve.wait_ge(S["j_e"], g + 1)
                st.link(dve.tensor_scalar(r[6][:, 0:T_], r[5][:, 0:T_], 1.0, None, ALU.add))
                st.link(dve.reciprocal(r[7][:, 0:T_], r[6][:, 0:T_]))
                st.link(dve.tensor_tensor(r[7][:, GT:GT + T_], r[7][:, 0:T_], r[5][:, 0:T_], ALU.mult))
                for j in range(T_):
                    dve.tensor_scalar(r[8][:, j * NE:(j + 1) * NE], iota[:, 0:NE], r[3][:, j * NE:j * NE + 1], r[7][:, j:j + 1],
                                      ALU.is_equal, ALU.mult)
                    ins = dve.tensor_scalar(r[9][:, j * NE:(j + 1) * NE], iota[:, 0:NE], r[3][:, j * NE + 1:j * NE + 2],
                                            r[7][:, GT + j:GT + j + 1], ALU.is_equal, ALU.mult)
                ins.then_inc(S["j_oh"], 1)
                dve.wait_ge(S["j_oh"], g + 1)
                dve.tensor_tensor(r[8][:, 0:n], r[8][:, 0:n], r[9][:, 0:n], ALU.add).then_inc(S["j_w"], 1)
                dve.wait_ge(S["j_wT"], g + 1)
                dve.tensor_copy(wT1[:, 0:T_ * P], bank[7][0:NE, 0:T_ * P]).then_inc(S["j_wTs"], 1)
                dve.wait_ge(S["j_b"], g + 1)
                for j in range(T_):
                    x_ = xt(g * GT + j)
                    ins = dve.tensor_tensor(x_, x_, bank[6 + j // 2][:, (j % 2) * D:(j % 2 + 1) * D], ALU.add)
                ins.then_inc(S["j_bx"], 1)
                for e in range(NE):
                    x_add(g, T_, e, rt1[:, 8, :], 4, "j_y", "j_acc", "j_bx")
            st.ended(NG + 1)
            barrier()

        @block.scalar
        def _(act):
            barrier = Barrier(act)
            for name, k in CREDIT["act"].items():
                act.sem_inc(S[name], k)

            def std(n, dst, src):
                act.wait_ge(var_ready, n)
                act.activation(dst, src, ACT.Sqrt).then_inc(std_ready, 1)

            std(1, MV[:, 2, :], MV[:, 7, :])
            barrier()
            barrier()
            std(2, sc[:, 1, :], sc[:, 0, :])
            std(3, sc[:, 3, :], sc[:, 2, :])
            barrier()
            for t, s in tiles(act):
                wait_alone(act, S["c1_T"], t + FREE)
                act.copy(xin[s], XN[:, ds(t * ROW, D)]).then_inc(S["c1_in"], 1)
                act.wait_ge(S["c1_T"], t + READY)
                act.wait_ge(S["c1_p"], t + FREE)
                act.copy(xT[s].rearrange("p a b -> p (a b)"), bank[s][:, 0:D]).then_inc(S["c1_xT"], 1)
                act.wait_ge(S["c1_kb"], t + 1)
                act.wait_ge(S["c1_kf"], t + FREE)
                act.activation(eb[s], kb[s], ACT.Exp).then_inc(S["c1_e"], 1)
            barrier()
            for t, s in tiles(act):
                wait_alone(act, S["c2_T"], t + FREE)
                act.copy(xin[s], XN[:, ds(t * ROW, D)]).then_inc(S["c2_in"], 1)
                act.wait_ge(S["c2_T"], t + READY)
                act.wait_ge(S["c2_q"], t + FREE)
                act.copy(xT[s].rearrange("p a b -> p (a b)"), bank[s][:, 0:D]).then_inc(S["c2_xT"], 1)
                act.wait_ge(S["c2_qb"], t + 1)
                act.wait_ge(S["c2_qf"], t + FREE)
                for m in range(2):
                    ins = act.activation(eb[s][:, m * P:(m + 1) * P], bank[2 + s][:, m * P:(m + 1) * P], ACT.Exp,
                                         bias=bq[:, m:m + 1])
                ins.then_inc(S["c2_e"], 1)
                act.wait_ge(S["c2_oT"], t + READY)
                act.wait_ge(S["c2_y"], t + FREE)
                act.copy(oT[s].rearrange("p a b -> p (a b)"), bank[6 + s][:, 0:D]).then_inc(S["c2_oTs"], 1)
            barrier()
            for layer in range(2):
                barrier()
                o = NT * layer
                for t, s in tiles(act):
                    wait_alone(act, S["d_T"], t + (o + FREE))
                    act.copy(xin[s], XN[:, ds(t * ROW, D)]).then_inc(S["d_in"], 1)
                    act.wait_ge(S["d_T"], t + (o + READY))
                    act.wait_ge(S["d_y"], t + (o + FREE))
                    act.copy(cT[s].rearrange("p a b -> p (a b)"), bank[s][:, :]).then_inc(S["d_cT"], 1)
                if layer == 0:
                    barrier()
                    barrier()
            std(4, MV[:, 2, :], MV[:, 7, :])
            barrier()
            for g, T_ in groups(act):
                act.wait_ge(S["f_T"], g + 2)
                act.wait_ge(S["f_l1"], g * 16 + 1)
                for k in range(2):
                    ins = act.copy(xg[:, k, 0:T_ * P], bank[k][:, 0:T_ * P])
                ins.then_inc(S["f_xT"], 1)
                act.wait_ge(S["f_rm"], g + 1)
                act.activation(rt[:, 3, 0:T_ * NE], rt[:, 2, 0:T_ * NE], ACT.Exp).then_inc(S["f_re"], 1)

                def relu(e, first):
                    lay, h, l_, wait_free = (0, h1, "f_l1", "f_l2") if first else (1, h2, "f_l2", "f_y")
                    for m in range(2):
                        if first:
                            act.wait_ge(S["f_l1"], g * 16 + (2 * e + m + 2))
                            if m == 0:
                                act.wait_ge(S["f_l2"], g * 16 + 2 * e + 1)
                        else:
                            act.wait_ge(S["f_l2"], g * 16 + (2 * e + m + 4))
                            if m == 0:
                                act.wait_ge(S["f_y"], g * NE + (e + FREE))
                        act.activation(h[e % 2][:, m, 0:T_ * P], bank[(2 if first else 0) + m][:, 0:T_ * P], ACT.Relu,
                                       bias=sc[:, 2 * lay + 1, 2 * e + m:2 * e + m + 1],
                                       scale=sc[:, 2 * lay, 2 * e + m:2 * e + m + 1]).then_inc(S["f_h1" if first else "f_h2"], 1)

                relu(0, True)
                for e in range(NE):
                    if e + 1 < NE:
                        relu(e + 1, True)
                    relu(e, False)
            std(5, MV[:, 2, :], MV[:, 7, :])
            barrier()
            barrier()
            for t, s in tiles(act):
                act.wait_ge(S["g_T"], t + READY)
                act.wait_ge(S["g_dt"], t + 1)
                act.copy(xT[s].rearrange("p a b -> p (a b)"), bank[0][:, 0:D]).then_inc(S["g_xT"], 1)
                act.wait_ge(S["g_kvp"], t + 1)
                act.wait_ge(S["g_var"], t + 1)
                for k in range(2):
                    ins = act.activation(sq[:, k * 512:(k + 1) * 512], bank[6 + k][:, :], ACT.Square)
                ins.then_inc(S["g_sq"], 1)
                act.wait_ge(S["g_dt"], t + 1)
                act.copy(vc, bank[7][:, :]).then_inc(S["g_vc"], 1)
                for q in range(2):
                    act.wait_ge(S["g_h"], t * 4 + (q + 1))
                    if q == 0:
                        act.wait_ge(hall_stored[s], t * 8 + (16 - 8 * s))
                    act.copy(ho[s][:, q * 512:(q + 1) * 512], bank[2 + q][:, :]).then_inc(S["g_ha"], 1)
                act.wait_ge(S["g_var"], t + 2)
                act.activation(rs[:, 48:64], rs[:, 16:32], ACT.Sqrt).then_inc(S["g_std"], 1)
            barrier()
            barrier()
            for t, s in tiles(act):
                act.wait_ge(S["i_T"], t + READY)
                act.wait_ge(S["i_y"], t + FREE)
                act.copy(xT[s].rearrange("p a b -> p (a b)"), bank[s][:, 0:D]).then_inc(S["i_xT"], 1)
            std(6, MV[:, 2, :], MV[:, 7, :])
            barrier()
            barrier()
            for g, T_ in groups(act):
                act.wait_ge(S["j_T"], g + 2)
                act.wait_ge(S["j_l1"], g * 32 + 1)
                for k in range(2):
                    ins = act.copy(xg[:, k, 0:T_ * P], bank[k][:, 0:T_ * P])
                ins.then_inc(S["j_xT"], 1)
                act.wait_ge(S["j_d"], g + 1)
                act.activation(rt1[:, 5, 0:T_], rt1[:, 4, 0:T_], ACT.Exp).then_inc(S["j_e"], 1)
                for e in range(NE):
                    for m in range(4):
                        act.wait_ge(S["j_l1"], g * 32 + (4 * e + m + 2))
                        if m == 0:
                            act.wait_ge(S["j_y"], g * NE + (e + FREE))
                        act.activation(hw[e % 2][:, m, 0:T_ * P], bank[2 + m % 2][:, 0:T_ * P], ACT.Relu,
                                       bias=hb[:, 4 * e + m:4 * e + m + 1]).then_inc(S["j_h1"], 1)
            barrier()

        @block.tensor
        def _(pe):
            barrier = Barrier(pe)
            for name, k in CREDIT["pe"].items():
                pe.sem_inc(S[name], k)
            pe.sem_inc(perm_used, COLS)
            pe.sem_inc(summed, CH)
            barrier()
            for n in range(2):
                pe.wait_ge(counts_ready, n + 1)
                b0 = bank[0]
                pe.matmul(b0[:, 0:NT], tri[0:EP, :], cnt[0:EP, :], start=True, stop=True)
                pe.matmul(b0[:, 32:32 + NT], ones[0:EP, :], cnt[0:EP, :], start=True, stop=True)
                pe.matmul(b0[0:NT, 64:65], cnt[0:EP, :], ones[0:EP, 0:1], start=True, stop=True).then_inc(prefix_ready, 1)
                pe.wait_ge(nch_ready, n + 1)
                pe.matmul(b0[0:NT, 66:67], trin[0:NT, 0:NT], small[0:NT, 224:225], start=True, stop=True
                          ).then_inc(chend_ready, 1)
                pe.wait_ge(ge_ready, n + 1)
                pe.matmul(bank[1][:, 0:SLOTS], ones[0:NT, :], RA[0:NT, 3000:3000 + SLOTS], start=True, stop=True
                          ).then_inc(til_ready, 1)
                pe.wait_ge(perm_ready, n * EC + 1)
                for k in range(2):
                    pe.matmul(bank[2 + k][:, 0:SLOTS], z16[0:EP, :], permR[0][0:EP, :], start=True, stop=False)
                with pe.Fori(0, EC // COLS) as i:
                    for s in range(COLS):
                        pe.wait_ge(perm_ready, i * COLS + (n * EC + s + 1))
                        for k in range(2):
                            mm = pe.matmul(bank[2 + k][:, 0:SLOTS], permA[s][0:EP, k * P:(k + 1) * P], permR[s][0:EP, :],
                                           start=False, stop=False)
                        mm.then_inc(perm_used, 1)
                for k in range(2):
                    mm = pe.matmul(bank[2 + k][:, 0:SLOTS], z16[0:EP, :], permR[0][0:EP, :], start=False, stop=True)
                mm.then_inc(perm_done, 1)
            barrier()
            barrier()

            def transpose(dst, src):
                for k in range(src.shape[-1] // P):
                    mm = pe.transpose(dst[:, k * P:(k + 1) * P], src[:, k * P:(k + 1) * P], ident[:, :])
                return mm

            for h in range(2):
                pe.matmul(bank[4 + h][:, 0:D + 2], zeros[:, 0:P], zeros[:, 0:D + 2], start=True, stop=False)
            for t, s in tiles(pe):
                rows = LAST if isinstance(t, int) else P
                pe.wait_ge(S["c1_in"], t + READY)
                pe.wait_ge(S["c1_xT"], t + FREE)
                transpose(bank[s], xin[s]).then_inc(S["c1_T"], 1)
                pe.wait_ge(S["c1_xT"], t + READY)
                pe.wait_ge(S["c1_v"], t + FREE)
                for k in range(2):
                    mm = pe.matmul(bank[2 + s][:, :], xT[s][:, k, :], wkv0[:, k, :], start=(k == 0), stop=(k == 1))
                mm.then_inc(S["c1_p"], 1)
                pe.wait_ge(S["c1_kf"], t + READY)
                for h in range(2):
                    mm = pe.matmul(bank[4 + h][:, 0:D + 2], kf[s][0:rows, h * P:(h + 1) * P], vb[s][0:rows, 0:D + 2],
                                   start=False, stop=False)
                mm.then_inc(S["c1_kv"], 1)
            for h in range(2):
                mm = pe.matmul(bank[4 + h][:, 0:D + 2], zeros[:, 0:P], zeros[:, 0:D + 2], start=False, stop=True)
            mm.then_inc(S["kv_done"], 1)
            barrier()
            for t, s in tiles(pe):
                pe.wait_ge(S["c2_in"], t + READY)
                pe.wait_ge(S["c2_xT"], t + FREE)
                transpose(bank[s], xin[s]).then_inc(S["c2_T"], 1)
                pe.wait_ge(S["c2_xT"], t + READY)
                pe.wait_ge(S["c2_qf"], t + FREE)
                for m in range(2):
                    for k in range(2):
                        mm = pe.matmul(bank[2 + s][:, m * P:(m + 1) * P], wq0[:, k, m * P:(m + 1) * P], xT[s][:, k, :],
                                       start=(k == 0), stop=(k == 1))
                mm.then_inc(S["c2_q"], 1)
                pe.wait_ge(S["c2_qf"], t + READY)
                pe.wait_ge(S["c2_o"], t + FREE)
                for m in range(2):
                    mm = pe.matmul(bank[4 + s][:, 0:D + NE], kf[s][:, m * P:(m + 1) * P], kvbd[:, m, :],
                                   start=(m == 0), stop=(m == 1))
                mm.then_inc(S["c2_n"], 1)
                pe.wait_ge(S["c2_o"], t + READY)
                pe.wait_ge(S["c2_x"], t + FREE)
                transpose(bank[6 + s], of[s]).then_inc(S["c2_oT"], 1)
                pe.wait_ge(S["c2_oTs"], t + READY)
                for k in range(2):
                    mm = pe.matmul(bank[6 + s][:, D:2 * D], oT[s][:, k, :], wo0[:, k, :], start=(k == 0), stop=(k == 1))
                mm.then_inc(S["c2_y"], 1)
            barrier()

            def aggregate(layer):
                cols = DS if layer < 2 else D
                with pe.Fori(0, TURNS) as i:
                    for s in range(CH):
                        if s % HALF == 0:
                            pe.wait_ge(hot_ready, i * 2 + (2 * TURNS * layer + s // HALF + 1))
                        pe.wait_ge(gathered[s], i * 16 + (TURNS * layer + 1) * 16)
                        pe.wait_ge(added, i * CH + (SLOTS * layer + s + 1))
                        pe.matmul(bank[s % PSB][:, 0:cols], hot[:, s, :], ring[:, s, 0:cols], start=True, stop=True
                                  ).then_inc(summed, 1)

            def dense(layer):
                o = NT * layer
                for t, s in tiles(pe):
                    pe.wait_ge(S["d_in"], t + (o + READY))
                    pe.wait_ge(S["d_nb"], t + (o + READY))
                    pe.wait_ge(S["d_cT"], t + (o + FREE))
                    transpose(bank[s], xin[s])
                    transpose(bank[s][:, D:2 * D], nb[s]).then_inc(S["d_T"], 1)
                    pe.wait_ge(S["d_cT"], t + (o + READY))
                    pe.wait_ge(S["d_u"], t + (o + FREE))
                    for k in range(4):
                        mm = pe.matmul(bank[2 + s][:, 0:D], cT[s][:, k, :], gw[layer][:, k, :], start=(k == 0), stop=(k == 3))
                    mm.then_inc(S["d_y"], 1)

            aggregate(0)
            barrier()
            dense(0)
            barrier()
            barrier()
            aggregate(1)
            barrier()
            dense(1)
            barrier()

            for g, T_ in groups(pe):
                W = T_ * P
                pe.wait_ge(S["f_in"], g + 1)
                pe.wait_ge(S["f_h2"], g * 16 + 2)
                for k in range(2):
                    for j in range(T_):
                        mm = pe.transpose(bank[k][:, j * P:(j + 1) * P], xgin[:, j, k * P:(k + 1) * P], ident[:, :])
                mm.then_inc(S["f_T"], 1)
                pe.wait_ge(S["f_xT"], g + 1)
                pe.wait_ge(S["f_bx"], g + 1)
                for j in range(T_):
                    for k in range(2):
                        mm = pe.matmul(bank[6][:, j * NE:(j + 1) * NE], xg[:, k, j * P:(j + 1) * P], wr0[:, k, :],
                                       start=(k == 0), stop=(k == 1))
                mm.then_inc(S["f_r"], 1)

                def first(e):
                    for m in range(2):
                        pe.wait_ge(S["f_h1"], g * 16 + (2 * e + m + FREE))
                        for k in range(2):
                            mm = pe.matmul(bank[2 + m][:, 0:W], w1[:, e, k, m * P:(m + 1) * P], xg[:, k, 0:W],
                                           start=(k == 0), stop=(k == 1))
                        mm.then_inc(S["f_l1"], 1)

                def second(e):
                    pe.wait_ge(S["f_h1"], g * 16 + (2 * e + 1 + READY))
                    for m in range(2):
                        pe.wait_ge(S["f_h2"], g * 16 + (2 * e + m + FREE))
                        for k in range(2):
                            mm = pe.matmul(bank[m][:, 0:W], w2[:, e, k, m * P:(m + 1) * P], h1[e % 2][:, k, 0:W],
                                           start=(k == 0), stop=(k == 1))
                        mm.then_inc(S["f_l2"], 1)

                def third(e):
                    pe.wait_ge(S["f_h2"], g * 16 + (2 * e + 1 + READY))
                    pe.wait_ge(S["f_acc"], g * NE + e + 1)
                    for j in range(T_):
                        for k in range(2):
                            mm = pe.matmul(bank[4 + j // 2][:, (j % 2) * D:(j % 2 + 1) * D], h2[e % 2][:, k, j * P:(j + 1) * P],
                                           wo[:, e, k, :], start=(k == 0), stop=(k == 1))
                    mm.then_inc(S["f_y"], 1)

                first(0)
                pe.wait_ge(S["f_w"], g + 1)
                for j in range(T_):
                    mm = pe.transpose(bank[7][0:NE, j * P:(j + 1) * P], rt[:, 6, j * NE:(j + 1) * NE], ident[:, :])
                mm.then_inc(S["f_wT"], 1)
                pe.wait_ge(S["f_wTs"], g + 1)
                for j in range(T_):
                    mm = pe.matmul(bank[6 + j // 2][:, (j % 2) * D:(j % 2 + 1) * D], wT[:, j * P:(j + 1) * P], bo_e[:, :],
                                   start=True, stop=True)
                mm.then_inc(S["f_b"], 1)
                for e in range(NE + 1):
                    if 0 < e < NE:
                        first(e)
                    if e >= 1:
                        if e < NE + 1:
                            second(e - 1)
                    if e >= 2:
                        third(e - 2)
                third(NE - 1)
            barrier()
            barrier()

            pe.wait_ge(S["wkv_c"], 1)
            pe.matmul(bank[1][:, :], zeros[:, 0:P], zeros[:, :], start=True, stop=False)
            for t, s in tiles(pe):
                rows = LAST if isinstance(t, int) else P
                pe.wait_ge(S["g_in"], t + READY)
                pe.wait_ge(S["g_xT"], t + FREE + 1)
                transpose(bank[0], xin[s]).then_inc(S["g_T"], 1)
                pe.wait_ge(S["g_xT"], t + READY)
                pe.wait_ge(S["g_kc"], t + 1)
                pe.wait_ge(S["g_vc"], t + 1)
                for b in range(2):
                    for k in range(2):
                        mm = pe.matmul(bank[6 + b][:, :], xT[s][:, k, :], wkv1[:, k, b * HW:(b + 1) * HW],
                                       start=(k == 0), stop=(k == 1))
                mm.then_inc(S["g_kvp"], 1)
                pe.wait_ge(S["g_ha"], t * 2 + 1)
                pe.wait_ge(S["g_hd"], t * 2 + 1)
                for q in range(4):
                    for k in range(2):
                        mm = pe.matmul(bank[2 + q][:, :], xT[s][:, k, :], wr[:, k, q * 512:(q + 1) * 512],
                                       start=(k == 0), stop=(k == 1))
                    mm.then_inc(S["g_h"], 1)
                pe.wait_ge(S["g_kc"], t + 2)
                pe.wait_ge(S["g_vc"], t + 2)
                for p in range(4):
                    mm = pe.matmul(bank[1][:, p * P:(p + 1) * P], vc[0:rows, p * P:(p + 1) * P], kc[0:rows, p * P:(p + 1) * P],
                                   start=False, stop=False)
                mm.then_inc(S["g_dt"], 1)
            pe.matmul(bank[1][:, :], zeros[:, 0:P], zeros[:, :], start=False, stop=True).then_inc(S["g_dt"], 1)
            pe.wait_ge(S["g_dtr"], 1)
            pe.wait_ge(S["g_ha"], 2 * NT + 1)
            pe.wait_ge(S["g_hd"], 2 * NT + 1)
            for p in range(4):
                mm = pe.matmul(bank[2 + p // 2][:, (p % 2) * D:(p % 2 + 1) * D], DT[:, p, :], wout1[:, p, :],
                               start=True, stop=True)
            mm.then_inc(S["g_mp"], 1)
            pe.wait_ge(S["g_mps"], 1)
            for m in range(2):
                for p in range(4):
                    mm = pe.matmul(bank[4][:, m * D:(m + 1) * D], wqT1[:, p, m * P:(m + 1) * P], MP[:, p, :],
                                   start=(p == 0), stop=(p == 3))
            mm.then_inc(S["g_we"], 1)
            barrier()
            aggregate(2)
            barrier()
            for t, s in tiles(pe):
                pe.wait_ge(S["i_in"], t + READY)
                pe.wait_ge(S["i_xT"], t + FREE)
                transpose(bank[s], xin[s]).then_inc(S["i_T"], 1)
                pe.wait_ge(S["i_xT"], t + READY)
                pe.wait_ge(S["i_x"], t + FREE)
                for k in range(2):
                    mm = pe.matmul(bank[2 + s][:, 0:D], xT[s][:, k, :], WEFF[:, k, :], start=(k == 0), stop=(k == 1))
                mm.then_inc(S["i_y"], 1)
            barrier()
            barrier()
            for g, T_ in groups(pe):
                W = T_ * P
                pe.wait_ge(S["j_in"], g + 1)
                pe.wait_ge(S["j_xT"], g + 1)
                for k in range(2):
                    for j in range(T_):
                        mm = pe.transpose(bank[k][:, j * P:(j + 1) * P], xgin[:, j, k * P:(k + 1) * P], ident[:, :])
                mm.then_inc(S["j_T"], 1)
                pe.wait_ge(S["j_xT"], g + 2)
                pe.wait_ge(S["j_bx"], g + 1)
                for j in range(T_):
                    for k in range(2):
                        mm = pe.matmul(bank[6][:, j * NE:(j + 1) * NE], xg[:, k, j * P:(j + 1) * P], wg1[:, k, :],
                                       start=(k == 0), stop=(k == 1))
                mm.then_inc(S["j_r"], 1)

                def first(e):
                    for m in range(4):
                        pe.wait_ge(S["j_h1"], g * 32 + (4 * e + m + FREE))
                        for k in range(2):
                            mm = pe.matmul(bank[2 + m % 2][:, 0:W], v1[:, e, k, m * P:(m + 1) * P], xg[:, k, 0:W],
                                           start=(k == 0), stop=(k == 1))
                        mm.then_inc(S["j_l1"], 1)

                def second(e):
                    pe.wait_ge(S["j_h1"], g * 32 + (4 * e + 3 + READY))
                    pe.wait_ge(S["j_acc"], g * NE + e + 1)
                    for j in range(T_):
                        for k in range(4):
                            mm = pe.matmul(bank[4 + j // 2][:, (j % 2) * D:(j % 2 + 1) * D], hw[e % 2][:, k, j * P:(j + 1) * P],
                                           v2[:, e, k, :], start=(k == 0), stop=(k == 3))
                    mm.then_inc(S["j_y"], 1)

                first(0)
                pe.wait_ge(S["j_w"], g + 1)
                for j in range(T_):
                    mm = pe.transpose(bank[7][0:NE, j * P:(j + 1) * P], rt1[:, 8, j * NE:(j + 1) * NE], ident[:, :])
                mm.then_inc(S["j_wT"], 1)
                pe.wait_ge(S["j_wTs"], g + 1)
                for j in range(T_):
                    mm = pe.matmul(bank[6 + j // 2][:, (j % 2) * D:(j % 2 + 1) * D], wT1[:, j * P:(j + 1) * P], b2_e[:, :],
                                   start=True, stop=True)
                mm.then_inc(S["j_b"], 1)
                for e in range(NE):
                    if e + 1 < NE:
                        first(e + 1)
                    second(e)
            barrier()


def kernel(**inputs):
    import numpy as _np
    import concourse.bacc as _bacc
    from concourse import mybir as _mybir
    from concourse.bass_utils import run_bass_kernel_spmd as _run

    a = {k: _np.asarray(v) for k, v in inputs.items()}
    cols = lambda v: v.reshape(-1, P).T
    laid = {k: v for k, v in a.items() if not k.startswith("L0_ffn_") or k[7:] in ("W1", "W2", "Wo", "Wr", "br", "bo")}
    for k in ("L0_gnn_W0", "L0_gnn_W1", "L1_gnn_weight", "L1_mix_w_qkv", "L1_ffn_b1"):
        del laid[k]
    laid["W0T"], laid["W1T"] = a["L0_gnn_W0"].T, a["L0_gnn_W1"].T
    laid["WrT"] = a["L1_gnn_weight"].reshape(NE * D, D).T
    laid["wkv"], laid["wqT"] = a["L1_mix_w_qkv"][:, HW:], a["L1_mix_w_qkv"][:, :HW].T
    laid["bq"] = cols(laid.pop("L0_mix_bq"))
    laid["hb"] = cols(a["L1_ffn_b1"])
    laid["bn"] = _np.stack([cols(a["L0_ffn_" + n + k]) for k in "12" for n in ("b", "g", "be", "m", "v")], 1)
    nc = _bacc.Bacc("TRN2", target_bir_lowering=False, num_devices=1)
    arrays, T = {}, {}
    for name, v in laid.items():
        v = _np.ascontiguousarray(v)
        arrays[f"in_{name}"] = v
        T[name] = nc.dram_tensor(f"in_{name}", v.shape, _mybir.dt.from_np(v.dtype), kind="ExternalInput").ap()
    out = nc.dram_tensor("out_0", (N, D), F32, kind="ExternalOutput").ap()
    program(nc, T, out)
    r = _run(nc, [arrays], core_ids=[0])
    return r.results[0]["out_0"]
```

```python
from contextlib import ExitStack

import concourse.bass as bass
from concourse import mybir

P = 128
N = 3125
D = 256
E = 50000
NT = (N + P - 1) // P
LAST = N - (NT - 1) * P
GT = 4
NG = NT // GT
EP = 125
EC = E // EP
CH = 32
PART = 8
HOTS = 16
LOADS = 8
UNIT = CH // 2
NCH = (E + NT * (P - 1)) // P
TURNS = (NCH + CH - 1) // CH
SLOTS = TURNS * CH
ROW = D + 4
DS = D + 2
NE = 8
HW = 512
HEAD0 = D // NE
HEAD1 = HW // NE
PSB = 2
COLS = 5
HCOLS = 2
SHARED = (1, 3)
CPT = 16
C0 = TURNS * CPT
assert TURNS == NT // 2 + 1 and EC - C0 == (TURNS - 1) * CPT
TOP = 2
ITEMS = TOP * NT
XCH = (TOP * N + NE * (P - 1)) // P
XB = 6
assert XCH % XB == 2
WST = 1024
BST = HW + D
OG = 5
assert NT % OG == 0
LN_EPS = 1e-5
BN_EPS = 1e-3

F32 = mybir.dt.float32
F16 = mybir.dt.float16
I32 = mybir.dt.int32
U32 = mybir.dt.uint32
ALU = mybir.AluOpType
ACT = mybir.ActivationFunctionType
AX = mybir.AxisListType
ds = bass.ds


class Steps:

    def __init__(self, eng, sem):
        self.eng, self.sem, self.base = eng, sem, 0
        self.t = self.per = self.k = 0

    def did(self, ins):
        ins.then_inc(self.sem, 1)
        self.k += 1

    def count(self):
        return self.t * self.per + (self.base + self.k)

    def wait(self, but=0):
        self.eng.wait_ge(self.sem, self.count() - but)

    def link(self, ins):
        self.did(ins)
        self.wait()

    def turn(self, t, per):
        if not self.per:
            self.base, self.k = self.base + self.k, 0
        assert not self.per or self.k == self.per, (self.k, self.per)
        self.t, self.per, self.k = t, per, 0

    def ended(self, turns):
        assert self.k == self.per, (self.k, self.per)
        self.base, self.t, self.per, self.k = self.base + turns * self.per, 0, 0, 0


def tiles(eng):
    with eng.Fori(0, NT // 2) as i:
        for s in range(2):
            yield i * 2 + s, s
    yield NT - 1, 0


def groups(eng):
    with eng.Fori(0, NG - 1) as g:
        yield g, GT, GT
    yield NG - 1, GT, NT - NG * GT
    yield NG, NT - NG * GT, 0


def turns(eng):
    with eng.Fori(0, TURNS - 1) as i:
        yield i, 2
    yield TURNS - 1, 1


def chunks(eng):
    yield 0, 0, 0, 1, 0
    with eng.Fori(0, XCH // XB) as i:
        for u in range(XB):
            yield i * XB + (1 + u), (1 + u) % 2, i * (XB // 2) + u // 2, (2 + u) % XB, i + (2 + u) // XB
    yield XCH - 1, 1, (XCH - 2) // 2, 0, 0


def beside(work, i, tiles_here, s):
    u = s // UNIT
    if u < tiles_here and s % UNIT in work:
        work[s % UNIT](i * 2 + u, u)


def program(nc, T, out, stop=None):
    with ExitStack() as ctx:
        def sb(name, shape, dt=F32):
            return ctx.enter_context(nc.sbuf_tensor(name, shape, dt))

        def sem(name):
            return ctx.enter_context(nc.semaphore(name))

        def dram(name, shape):
            return nc.dram_tensor(name, shape, F32, kind="Internal").ap()

        bank = [ctx.enter_context(nc.psum_tensor(f"bank{i}", [P, 512], F32)) for i in range(8)]

        table0 = dram("table0", (NT * P, ROW))
        table1 = dram("table1", (NT * P, D))
        hall = dram("hall", (NE * N, D))
        ys = dram("ys", (XCH * P, D))

        X = sb("X", [P, (NT + 1) * D])
        XN = sb("XN", [P, NT * ROW])
        AGG = sb("AGG", [P, (NT + 1) * DS])
        STAT = sb("STAT", [P, NT * 6])
        MV = sb("MV", [P, 8, NT + 1])
        IDX = [sb(f"IDX{i}", [P, SLOTS], I32) for i in range(2)]
        LOC = [sb(f"LOC{i}", [P, SLOTS]) for i in range(2)]
        TIL = [sb(f"TIL{i}", [P, SLOTS], I32) for i in range(2)]
        idxb = sb("idxb", [P, CH], I32)
        ident = sb("ident", [P, P])
        tri = sb("tri", [P, P])
        trin = sb("trin", [P, P])
        ones = sb("ones", [P, P])
        zeros = sb("zeros", [P, 512])
        iotai = sb("iotai", [P, SLOTS], I32)
        iota = sb("iota", [P, SLOTS])
        iota16 = sb("iota16", [P, SLOTS], F16)
        bias = sb("bias", [P, 9, D])
        small = sb("small", [P, 384])
        WA = sb("WA", [P, 16384])
        RA = sb("RA", [P, 7296])

        def view(arena, at, shape):
            n = 1
            for k in shape:
                n *= k
            v = arena[:, at:at + n]
            if len(shape) == 2:
                return v.rearrange("p (a b) -> p a b", b=shape[1])
            if len(shape) == 3:
                return v.rearrange("p (a b c) -> p a b c", b=shape[1], c=shape[2])
            return v

        w1 = view(WA, 0, (NE, 2, D))
        w2 = view(WA, 4096, (NE, 2, D))
        wo = view(WA, 8192, (NE, 2, D))
        gw = [view(WA, 12288 + 1024 * i, (4, D)) for i in range(2)]
        wkv0 = view(WA, 14336, (2, 512))
        wq0 = view(WA, 15360, (2, D))
        wo0 = view(WA, 15872, (2, D))
        wr = view(WA, 12288, (2, NE * D))
        wkv1 = view(AGG, 0, (2, 2 * HW))
        wqT1 = view(AGG, 2048, (4, D))
        wout1 = view(AGG, 3072, (4, D))
        DT = view(AGG, 4096, (4, P))
        MP = view(AGG, 4608, (4, D))
        WEFF = view(AGG, 5632, (2, D))
        v1 = view(WA, 0, (NE, 2, HW))
        v2 = view(WA, 8192, (NE, 4, D))
        bo_e = sb("bo_e", [NE, D])
        wr0 = sb("wr0", [P, 2, NE])
        wg1 = sb("wg1", [P, 2, NE])
        gate_b = sb("gate_b", [P, 3, NE])
        bn = sb("bn", [P, 10, 2 * NE])
        sc = sb("sc", [P, 4, 2 * NE])
        beyond = sb("beyond", [P, 1])
        rowi, rowf = sb("rowi", [P, 1], I32), sb("rowf", [P, 1])
        bq = sb("bq", [P, 2])
        kvbd = sb("kvbd", [P, 2, D + NE])

        pos = AGG[:, 400:800]
        scan = [AGG[:, 800:1200], AGG[:, 1200:1600], IDX[1][:, 0:EC].bitcast(F32)]
        tmpi = [AGG[:, 1600 + 400 * i:2000 + 400 * i].bitcast(I32) for i in range(5)]
        tmpf = [AGG[:, 3600 + 400 * i:4000 + 400 * i] for i in range(6)]
        moves = [AGG[:, 4400:6000], WA[:, 10368:11968]]
        rooms = [(WA, 8320, 9), (RA, 3500, 8), (AGG, 4400, 4), (AGG, 0, 1), (AGG, 6000, 1), (RA, 2560, 1), (LOC[1], 0, 1)]
        oh = [a[:, at + EC * k:at + EC * (k + 1)] for a, at, n in rooms for k in range(n)]
        assert len(oh) == NT
        minus = [[AGG[:, 3600:4000], AGG[:, 4000:4400]], [IDX[1][:, 0:EC].bitcast(F32), LOC[1][:, 0:EC]]]
        away = [RA[:, 6928 + 64 * s:6992 + 64 * s].bitcast(F16) for s in range(2)]
        edges = [RA[:, 400 * i:400 * i + 400].bitcast(I32) for i in range(3)]
        permA = [RA[:, 1200 + 128 * s:1328 + 128 * s].bitcast(F16) for s in range(COLS)]
        permR = [RA[:, 1840 + 208 * s:2048 + 208 * s].bitcast(F16) for s in range(COLS)]
        permA1 = [RA[:, 6192 + 128 * s:6320 + 128 * s].bitcast(F16) for s in range(HCOLS)]
        permR1 = [RA[:, 6448 + 208 * s:6656 + 208 * s].bitcast(F16) for s in range(HCOLS)]
        cnt = small[:, 0:NT]
        z16 = RA[:, 6864:6928].bitcast(F16)
        ring = view(WA, 0, (CH, ROW))
        hot = view(WA, CH * ROW, (HOTS, P))
        xin = [RA[:, 256 * s:256 * s + 256] for s in range(2)]
        xT = [view(RA, 512 + 256 * s, (2, P)) for s in range(2)]
        kb = [RA[:, 1024 + 256 * s:1280 + 256 * s] for s in range(2)]
        eb = [RA[:, 1536 + 256 * s:1792 + 256 * s] for s in range(2)]
        mb = [RA[:, 2048 + 256 * s:2304 + 256 * s] for s in range(2)]
        kf = [RA[:, 2560 + 256 * s:2816 + 256 * s] for s in range(2)]
        vb = [RA[:, 3072 + 258 * s:3330 + 258 * s] for s in range(2)]
        of = [RA[:, 3600 + 256 * s:3856 + 256 * s] for s in range(2)]
        oT = [view(RA, 4112 + 256 * s, (2, P)) for s in range(2)]
        nr = [RA[:, 4624 + 16 * s:4640 + 16 * s] for s in range(2)]
        cT = [view(RA, 4656 + 512 * s, (4, P)) for s in range(2)]
        nb = [RA[:, 5680 + 256 * s:5936 + 256 * s] for s in range(2)]
        ho = [RA[:, 1024 + 2048 * s:3072 + 2048 * s] for s in range(2)]
        sq = RA[:, 5120:6144]
        kc = RA[:, 6144:6656]
        vc = RA[:, 6656:7168]
        rs = RA[:, 7168:7232]
        xg = view(RA, 0, (2, GT * P))
        xgin = view(RA, 1024, (GT, D))
        h1 = [view(RA, 2048 + 1024 * s, (2, GT * P)) for s in range(2)]
        h2 = [view(RA, 4096 + 1024 * s, (2, GT * P)) for s in range(2)]
        rt = view(RA, 6144, (8, GT * NE))
        wT = RA[0:NE, 6400:6400 + GT * P]
        hs = [RA[:, 1024 + 512 * s:1536 + 512 * s] for s in range(2)]
        hT = [view(RA, 2048 + 512 * s, (4, P)) for s in range(2)]
        yo = [RA[:, 3072 + 256 * s:3328 + 256 * s] for s in range(2)]
        logits, best = view(RA, 3600, (NT, NE)), view(RA, 3800, (NT, NE))
        bestat = RA[:, 4000:4200].bitcast(U32).rearrange("p (t e) -> p t e", e=NE)
        chosen = view(RA, 4200, (TOP, NT))
        mask = view(RA, 4300, (NE, ITEMS))
        rank = [RA[:, 4700 + 50 * s:4700 + 50 * s + ITEMS] for s in range(2)]
        ipos = RA[:, 4800:4800 + ITEMS]
        slot_token = IDX[0][:, 0:XCH]
        item_slot = IDX[0][:, 64:64 + ITEMS]
        itemi = [RA[:, 5360 + 50 * k:5360 + 50 * k + ITEMS].bitcast(I32) for k in range(3)]
        itemf = [RA[:, 5520 + 50 * k:5520 + 50 * k + ITEMS] for k in range(2)]
        tokens = RA[:, 5620:5620 + NT]
        itemA = [RA[:, 4860 + P * k:4860 + P * (k + 1)] for k in range(TOP)]
        itemR = [RA[:, 5120 + 64 * k:5120 + 64 * k + XCH] for k in range(TOP)]
        xc = [RA[:, 3600 + 256 * b:3856 + 256 * b] for b in range(XB)]
        wexp, bexp = TIL[0], TIL[1]
        eb1 = view(AGG, 0, (NE, BST))
        yr = [view(XN, 0, (NT, ROW)), view(RA, 0, (NT, D))]

        def xt(t):
            return X[:, ds(t * D, D)]

        consts = sem("consts")
        pool_step, dve_step, act_step = sem("pool_step"), sem("dve_step"), sem("act_step")
        phase = sem("phase")
        x_in = sem("x_in")
        edges_in = sem("edges_in")
        w_in = sem("w_in")
        stored = sem("stored")
        hall_stored = [sem(f"hall_stored{s}") for s in range(2)]
        out_stored = sem("out_stored")
        x_pad = sem("x_pad")
        ys_stored = [sem(f"ys_stored{s}") for s in range(2)]
        var_ready, std_ready = sem("var_ready"), sem("std_ready")
        counts_ready, prefix_ready = sem("counts_ready"), sem("prefix_ready")
        nch_ready, chend_ready, ge_ready, til_ready = (sem(n) for n in ("nch_ready", "chend_ready", "ge_ready", "til_ready"))
        perm_ready, perm_used, perm_done = sem("perm_ready"), sem("perm_used"), sem("perm_done")
        moves_ready, abs_ready, place_ready = sem("moves_ready"), sem("abs_ready"), sem("place_ready")
        idx_ready, hot_ready = sem("idx_ready"), sem("hot_ready")
        gathered = [sem(f"gathered{s}") for s in range(CH)]
        summed = sem("summed")
        added = sem("added")
        class Barrier:
            def __init__(self, eng):
                self.eng, self.n = eng, 0

            def __call__(self, wait=True):
                self.n += 1
                self.eng.drain().then_inc(phase, 1)
                if wait:
                    self.eng.wait_ge(phase, 5 * self.n)

        S = {n: sem(n) for n in (
            "c1_m c2_r c2_d c1_in c1_T c1_xT c1_p c1_v c1_kb c1_e c1_kf c1_kv kv_done "
            "c2_in c2_T c2_xT c2_q c2_qb c2_e c2_qf c2_n c2_o c2_oT c2_oTs c2_y c2_x "
            "d_in d_nb d_T d_cT d_y d_u "
            "f_in f_T f_xT f_r f_rm f_re f_w f_wT f_wTs f_b f_bx f_l1 f_h1 f_l2 f_h2 f_y f_acc "
            "wkv_c g_in g_c g_T g_xT g_kvp g_h g_ha g_hd g_sq g_var g_std g_kc g_vc g_dt g_dtr g_mp g_mps g_we "
            "i_in i_T i_xT i_y i_x r_in r_d r_e items_ready e_T e_xT e_l1 e_h e_Th e_hT e_l2 e_y x_done").split()}
        CREDIT = {
            "act": {"c1_in": 2, "c1_xT": 2, "c1_e": 2, "c2_in": 2, "c2_xT": 2, "c2_oTs": 2, "d_in": 2, "d_cT": 2,
                    "f_h1": 2, "f_h2": 2, "g_vc": 1, "g_ha": 1, "g_xT": 2, "i_in": 2, "i_xT": 2, "e_xT": 2, "e_hT": 2},
            "pe": {"c1_T": 2, "c1_p": 2, "c1_kv": 2, "c2_T": 2, "c2_q": 2, "c2_n": 2, "c2_oT": 2, "c2_y": 2,
                   "d_T": 2, "d_y": 2, "f_l2": 3, "f_T": 1, "g_dt": 1, "g_h": 5, "f_l1": 1, "f_y": 2, "g_T": 2, "i_T": 2, "i_y": 2, "e_T": 2, "e_l1": 2, "e_Th": 2, "e_l2": 2},
            "dve": {"c1_v": 2, "c1_kf": 2, "c2_qf": 2, "c2_o": 2, "c2_x": 2, "d_nb": 2, "d_u": 2, "g_in": 2,
                    "g_var": 1, "f_bx": 1, "f_acc": 1, "g_kc": 1, "g_hd": 1, "e_h": 2, "e_y": 2,
                    "i_x": 2},
        }
        FREE, READY = 1, 3

        def wait_alone(eng, signal, value):
            if not isinstance(value, int):
                value = eng.to_reg(value)
                eng.wait_ge(consts, 6)
            eng.wait_ge(signal, value)

        block = ctx.enter_context(nc.Block())

        @block.sync
        def _(sp):
            barrier = Barrier(sp)
            for s in range(2):
                sp.sem_inc(hall_stored[s], 16)
            sp.wait_ge(x_pad, 1)
            sp.dma_start(X[:, 0:(NT - 1) * D].rearrange("p (t d) -> p t d", d=D),
                         T["x"][0:(NT - 1) * P, :].rearrange("(t p) d -> p t d", p=P)).then_inc(x_in, 16)
            sp.dma_start(X[0:LAST, (NT - 1) * D:NT * D], T["x"][(NT - 1) * P:N, :]).then_inc(x_in, 16)
            for i, n in enumerate(("src", "dst", "edge_type_8")):
                sp.dma_start(edges[i][0:EP, :], T[n].rearrange("(p c) -> p c", c=EC)).then_inc(edges_in, 16)
            for i, n in enumerate(("L0_mix_bk", "L0_mix_bv", "L0_mix_bo", "L0_gnn_b0", "L0_gnn_b1", "L1_gnn_bias", "L1_mix_b_out")):
                sp.dma_start(bias[:, i, :], T[n].partition_broadcast(P)).then_inc(w_in, 16)
            sp.dma_start(bq[:, :], T["bq"]).then_inc(w_in, 16)
            for i, n in enumerate(("L0_ffn_br", "L1_ffn_bg", "L1_ffn_bias")):
                sp.dma_start(gate_b[:, i, :], T[n].partition_broadcast(P)).then_inc(w_in, 16)
            sp.dma_start(bn[:, :, :], T["bn"]).then_inc(w_in, 16)
            sp.dma_start(bo_e[:, :], T["L0_ffn_bo"]).then_inc(w_in, 16)
            sp.dma_start(wr0[:, :, :], T["L0_ffn_Wr"].rearrange("(k p) n -> p k n", p=P)).then_inc(w_in, 16)
            sp.dma_start(wg1[:, :, :], T["L1_ffn_Wg"].rearrange("(k p) n -> p k n", p=P)).then_inc(w_in, 16)
            for dst, n in ((gw[0], "W0T"), (gw[1], "W1T"), (wkv0[:, :, 0:D], "L0_mix_wk"), (wkv0[:, :, D:2 * D], "L0_mix_wv"),
                           (wq0, "L0_mix_wq"), (wo0, "L0_mix_wo")):
                sp.dma_start(dst, T[n].rearrange("(k p) n -> p k n", p=P)).then_inc(w_in, 16)
            barrier()
            sp.dma_start(table0.rearrange("(t p) d -> p t d", p=P),
                         XN[:, :].rearrange("p (t d) -> p t d", d=ROW)).then_inc(stored, 16)
            sp.wait_ge(stored, 16)
            barrier()
            barrier()
            barrier()
            sp.dma_start(table1.rearrange("(t p) d -> p t d", p=P),
                         XN[:, :].rearrange("p (t d) -> p t d", d=ROW)[:, :, 0:D]).then_inc(stored, 16)
            sp.wait_ge(stored, 32)
            barrier()
            barrier()
            for e in range(NE):
                for dst, n in ((w1, "L0_ffn_W1"), (w2, "L0_ffn_W2"), (wo, "L0_ffn_Wo")):
                    sp.dma_start(dst[:, e, :, :], T[n][e].rearrange("(k p) n -> p k n", p=P)).then_inc(w_in, 16)
            sp.wait_ge(w_in, 16 * (21 + 3 * NE))
            barrier()
            for dst, n in ((wr, "WrT"), (wkv1, "wkv"), (wqT1, "wqT"), (wout1, "L1_mix_w_out")):
                sp.dma_start(dst, T[n].rearrange("(k p) n -> p k n", p=P)).then_inc(w_in, 16)
            sp.wait_ge(w_in, 16 * (25 + 3 * NE))
            barrier()
            hall_v = hall.rearrange("(r n) d -> n r d", n=N)
            for t, s in tiles(sp):
                rows = LAST if isinstance(t, int) else P
                sp.wait_ge(S["g_ha"], t * 2 + 2 + 1)
                sp.wait_ge(S["g_hd"], t * 2 + 2 + 1)
                if rows == P:
                    src = hall_v[ds(t * P, P), :, :]
                else:
                    src = hall_v[(NT - 1) * P:N, :, :]
                sp.dma_start(src, ho[s][0:rows, :].rearrange("p (r d) -> p r d", r=NE)).then_inc(hall_stored[s], 16)
            sp.wait_ge(hall_stored[0], 16 * 14)
            sp.wait_ge(hall_stored[1], 16 * 13)
            barrier()
            barrier()
            for e in range(NE):
                sp.dma_start(v1[:, e, :, :], T["L1_ffn_W1"][e].rearrange("(k p) n -> p k n", p=P)).then_inc(w_in, 16)
                sp.dma_start(v2[:, e, :, :], T["L1_ffn_W2"][e].rearrange("(k p) n -> p k n", p=P)).then_inc(w_in, 16)
                sp.dma_start(eb1[:, e, 0:HW], T["L1_ffn_b1"][e].partition_broadcast(P)).then_inc(w_in, 16)
                sp.dma_start(eb1[:, e, HW:BST], T["L1_ffn_b2"][e].partition_broadcast(P)).then_inc(w_in, 16)
            sp.wait_ge(S["r_in"], NT)
            sp.dma_start(table1.rearrange("(t p) d -> p t d", p=P),
                         XN[:, :].rearrange("p (t d) -> p t d", d=ROW)[:, :, 0:D]).then_inc(stored, 16)
            sp.wait_ge(stored, 48)
            sp.wait_ge(w_in, 16 * (25 + 7 * NE))
            barrier()
            for s in range(2):
                sp.sem_inc(ys_stored[s], 16)
            for c, s, before, _, _ in chunks(sp):
                if not (isinstance(c, int) and c == 0):
                    sp.wait_ge(S["e_y"], c + (READY - 1))
                    sp.dma_start(ys[ds(c * P - P, P), :], yo[1 - s]).then_inc(ys_stored[1 - s], 16)
            sp.wait_ge(S["e_y"], XCH - 1 + READY)
            sp.dma_start(ys[(XCH - 1) * P:XCH * P, :], yo[1]).then_inc(ys_stored[1], 16)
            for s in range(2):
                sp.wait_ge(ys_stored[s], 16 * (XCH // 2 + 1))
            barrier()
            for g in range(NT // OG):
                sp.wait_ge(S["x_done"], g + 1)
                a, b = g * OG, min((g + 1) * OG, NT - 1)
                sp.dma_start(out[a * P:b * P, :].rearrange("(t p) d -> p t d", p=P),
                             X[:, a * D:b * D].rearrange("p (t d) -> p t d", d=D)).then_inc(out_stored, 16)
            sp.dma_start(out[(NT - 1) * P:N, :], X[0:LAST, (NT - 1) * D:NT * D]).then_inc(out_stored, 16)
            sp.wait_ge(out_stored, 16 * (NT // OG + 1))

        @block.gpsimd
        def _(pool):
            barrier = Barrier(pool)
            pool.memset(X[:, (NT - 1) * D:(NT + 1) * D], 0.0).then_inc(x_pad, 1)
            pool.memset(ident[:, :], 0.0).then_inc(pool_step, 1)
            pool.memset(ones[:, :], 1.0).then_inc(pool_step, 1)
            pool.memset(zeros[:, :], 0.0).then_inc(consts, 1)
            pool.iota(rowi[:, :], pattern=[[0, 1]], base=0, channel_multiplier=1).then_inc(pool_step, 1)
            pool.memset(XN[:, :], 1.0).then_inc(consts, 1)
            pool.iota(iotai[:, :], pattern=[[1, SLOTS]], base=0, channel_multiplier=0).then_inc(consts, 1)
            pool.wait_ge(pool_step, 3)
            pool.affine_select(out=ident[:, :], in_=ident[:, :], compare_op=ALU.not_equal, fill=1.0, base=0,
                               pattern=[[-1, P]], channel_multiplier=1).then_inc(consts, 1)
            pool.affine_select(out=tri[:, :], in_=ones[:, :], compare_op=ALU.is_gt, fill=0.0, base=0,
                               pattern=[[1, P]], channel_multiplier=-1).then_inc(consts, 1)
            pool.affine_select(out=trin[:, :], in_=ones[:, :], compare_op=ALU.is_ge, fill=0.0, base=0,
                               pattern=[[1, P]], channel_multiplier=-1).then_inc(consts, 1)
            barrier()
            barrier(wait=False)
            pool.wait_ge(stored, 16)

            def gather(layer, table, cols):
                with pool.Fori(0, TURNS) as i:
                    for q in range(CH // PART):
                        wait_alone(pool, idx_ready, (i + TURNS * layer) * (CH // PART) + (q + 1))
                        for s in range(q * PART, (q + 1) * PART):
                            pool.indirect_dma_start(out=ring[:, s, 0:cols], out_offset=None, in_=table,
                                                    in_offset=bass.IndirectOffsetOnAxis(ap=idxb[:, s:s + 1], axis=0)
                                                    ).then_inc(gathered[s], 16)

            gather(0, table0[:, :], ROW)
            barrier()
            barrier()
            barrier()
            gather(1, table1[:, :], D)
            for _ in range(4):
                barrier()
            gather(2, hall[:, :], D)
            barrier()
            barrier()
            for c in range(XCH):
                if c >= XB:
                    pool.wait_ge(S["e_T"], c - XB + READY)
                pool.indirect_dma_start(out=xc[c % XB], out_offset=None, in_=table1,
                                        in_offset=bass.IndirectOffsetOnAxis(ap=slot_token[:, c:c + 1], axis=0)
                                        ).then_inc(gathered[c % XB], 16)
            barrier()
            for g in range(NT // OG):
                for t in range(g * OG, (g + 1) * OG):
                    for k in range(TOP):
                        pool.indirect_dma_start(out=yr[k][:, t, 0:D], out_offset=None, in_=ys,
                                                in_offset=bass.IndirectOffsetOnAxis(ap=item_slot[:, k * NT + t:k * NT + t + 1], axis=0)
                                                ).then_inc(gathered[g], 16)

        @block.vector
        def _(dve):
            barrier = Barrier(dve)
            st = Steps(dve, dve_step)
            for name, k in CREDIT["dve"].items():
                dve.sem_inc(S[name], k)
            dve.sem_inc(added, PSB)

            def moments(t):
                return dve.bn_stats(STAT[:, ds(t * 6, 6)], xt(t))

            def all_moments():
                with dve.Fori(0, NT // OG) as i:
                    st.turn(i, OG)
                    for j in range(OG):
                        st.did(moments(i * OG + j))
                st.ended(NT // OG)

            def stats(n):
                st.wait()
                f = STAT[:, :].rearrange("p (t c) -> p c t", c=6)
                st.did(dve.tensor_tensor(MV[:, 2, 0:NT], f[:, 1, :], f[:, 4, :], ALU.add))
                st.did(dve.tensor_tensor(MV[:, 3, 0:NT], f[:, 1, :], f[:, 4, :], ALU.subtract))
                st.link(dve.tensor_tensor(MV[:, 4, 0:NT], f[:, 2, :], f[:, 5, :], ALU.add))
                st.did(dve.tensor_scalar(MV[:, 0, 0:NT], MV[:, 2, 0:NT], 0.5, None, ALU.mult))
                st.link(dve.scalar_tensor_tensor(MV[:, 5, 0:NT], MV[:, 3, 0:NT], 0.25, MV[:, 3, 0:NT], ALU.mult, ALU.mult))
                st.link(dve.scalar_tensor_tensor(MV[:, 6, 0:NT], MV[:, 4, 0:NT], 1.0 / D, MV[:, 5, 0:NT], ALU.mult, ALU.add))
                dve.tensor_scalar(MV[:, 7, 0:NT], MV[:, 6, 0:NT], LN_EPS, None, ALU.add).then_inc(var_ready, 1)
                dve.wait_ge(std_ready, n)
                st.link(dve.reciprocal(MV[:, 1, 0:NT], MV[:, 2, 0:NT]))
                st.did(dve.scalar_tensor_tensor(MV[:, 4, 0:NT], MV[:, 0, 0:NT], -1.0, MV[:, 1, 0:NT], ALU.mult, ALU.mult))

            def norm(dst, t):
                return dve.tensor_scalar(dst, xt(t), MV[:, 0, ds(t, 1)], MV[:, 1, ds(t, 1)], ALU.subtract, ALU.mult)

            dve.wait_ge(consts, 6)
            st.did(dve.tensor_copy(iota[:, :], iotai[:, :]))
            st.did(dve.tensor_copy(iota16[:, :], iotai[:, :]))
            dve.wait_ge(pool_step, 3)
            st.did(dve.tensor_copy(rowf[:, :], rowi[:, :]))
            st.link(dve.tensor_scalar(beyond[:, :], rowi[:, :], float(LAST), 16.0, ALU.is_ge, ALU.mult))
            dve.wait_ge(x_in, 32)
            all_moments()
            stats(1)
            with dve.Fori(0, NT // OG) as i:
                st.turn(i, OG)
                for j in range(OG):
                    st.did(norm(XN[:, ds(i * OG * ROW + j * ROW, D)], i * OG + j))
            st.ended(NT // OG)
            barrier()

            def indices(n, i, q):
                dve.tensor_copy(idxb[:, q * PART:(q + 1) * PART], IDX[n][:, ds(i * CH + q * PART, PART)]
                                ).then_inc(idx_ready, 1)

            def starts(n, bins, slots):
                c = [small[:, 32 * k:32 * k + bins] for k in range(1, 6)]
                ci = [small[:, 256 + 32 * k:256 + 32 * k + bins].bitcast(I32) for k in range(2)]
                r, ri = small[0:bins, 224:226], small[0:bins, 320:322].bitcast(I32)
                st.wait()
                dve.drain().then_inc(counts_ready, 1)
                dve.wait_ge(prefix_ready, n + 1)
                st.link(dve.tensor_scalar(ci[0], bank[0][:, 32:32 + bins], float(P - 1), None, ALU.add))
                st.link(dve.tensor_scalar(ci[1], ci[0], 7, None, ALU.logical_shift_right))
                st.link(dve.tensor_copy(c[0], ci[1]))
                st.link(dve.tensor_tensor_scan(c[1], c[0], zeros[:, 0:bins], 0.0, ALU.add, ALU.add))
                st.link(dve.tensor_tensor(c[2], c[1], c[0], ALU.subtract))
                st.link(dve.scalar_tensor_tensor(c[3], c[2], float(P), bank[0][:, 0:bins], ALU.mult, ALU.add))
                st.link(dve.tensor_scalar(c[4], c[3], -1.0, None, ALU.add))
                st.link(dve.tensor_scalar(ri[:, 0:1], bank[0][0:bins, 64:65], float(P - 1), None, ALU.add))
                st.link(dve.tensor_scalar(ri[:, 1:2], ri[:, 0:1], 7, None, ALU.logical_shift_right))
                dve.tensor_copy(r[:, 0:1], ri[:, 1:2]).then_inc(nch_ready, 1)
                dve.wait_ge(chend_ready, n + 1)
                st.link(dve.tensor_copy(r[:, 1:2], bank[0][0:bins, 66:67]))
                dve.tensor_scalar(RA[0:bins, 3000:3000 + slots], iota[0:bins, 0:slots], r[:, 1:2], None,
                                  ALU.is_ge).then_inc(ge_ready, 1)
                dve.wait_ge(til_ready, n + 1)
                return c[4]

            def place(n):
                key, other = edges[n][0:EP, :], edges[1 - n][0:EP, :]
                f = [a[0:EP, :] for a in tmpf]
                m = [moves[n][0:EP, EC * k:EC * (k + 1)] for k in range(4)]
                g = [a[0:EP, :] for a in tmpi]
                st.did(dve.tensor_scalar(g[0], key, 7, None, ALU.logical_shift_right))
                st.link(dve.tensor_scalar(g[1], key, P - 1, None, ALU.bitwise_and))
                st.did(dve.tensor_copy(f[0], g[0]))
                st.link(dve.tensor_copy(f[1], g[1]))
                for b in range(NT):
                    st.did(dve.tensor_scalar(oh[b][0:EP, :], f[0], float(b), 0.0, ALU.is_equal, ALU.add,
                                             accum_out=cnt[0:EP, b:b + 1]))
                c = starts(n, NT, SLOTS)
                st.did(dve.tensor_scalar(TIL[n][:, :], bank[1][:, 0:SLOTS], float((DS, D)[n]), None, ALU.mult))
                st.link(dve.memset(pos, 0.0))

                def count(b):
                    st.did(dve.tensor_tensor_scan(scan[b % 3][0:EP, :], oh[b][0:EP, :], zeros[0:EP, 0:EC],
                                                  c[0:EP, b:b + 1], ALU.add, ALU.add))

                count(0)
                for b in range(NT):
                    if b + 1 < NT:
                        count(b + 1)
                    st.wait(but=int(b + 1 < NT))
                    st.did(dve.copy_predicated(pos[0:EP, :], oh[b][0:EP, :].bitcast(I32), scan[b % 3][0:EP, :]))
                st.wait()
                st.link(dve.tensor_copy(g[2], pos[0:EP, :]))
                st.did(dve.tensor_scalar(g[3], g[2], P - 1, None, ALU.bitwise_and))
                st.link(dve.tensor_scalar(g[4], g[2], 7, None, ALU.logical_shift_right))
                st.did(dve.tensor_copy(m[0], g[3]))
                st.did(dve.tensor_copy(m[1], g[4]))
                if n == 0:
                    st.link(dve.tensor_copy(m[2], other))
                else:
                    st.link(dve.scalar_tensor_tensor(m[2], edges[2][0:EP, :], float(N), other, ALU.mult, ALU.add))
                st.link(dve.tensor_scalar(m[3], m[2], 1.0, float(P), ALU.add, ALU.mult))
                st.link(dve.tensor_tensor(g[0], m[3], f[1], ALU.add))
                st.did(dve.tensor_scalar(g[1], g[0], 11, None, ALU.logical_shift_right))
                st.link(dve.tensor_scalar(g[2], g[0], 2047, None, ALU.bitwise_and))
                st.did(dve.tensor_copy(m[2], g[1]))
                st.link(dve.tensor_copy(m[3], g[2]))
                for k in range(2):
                    ins = dve.tensor_scalar(minus[n][k][0:EP, :], m[2 + k], -1.0, None, ALU.mult)
                ins.then_inc(moves_ready, 1)
                dve.wait_ge(moves_ready, n + 1)
                if n == 0:
                    st.link(dve.memset(z16, 0.0))

            def column(n, c, free, A, R, shared):
                q, r, hi, lo = (moves[n][0:EP, ds(c + EC * k, 1)] for k in range(4))
                dve.wait_ge(perm_used, free)
                if not shared:
                    dve.tensor_scalar(A[0:EP, 0:P], iota16[0:EP, 0:P], q, hi, ALU.is_equal, ALU.mult)
                    dve.tensor_scalar(A[0:EP, P:2 * P], iota16[0:EP, 0:P], q, lo, ALU.is_equal, ALU.mult)
                dve.tensor_scalar(R[0:EP, :], iota16[0:EP, :], r, None, ALU.is_equal).then_inc(perm_ready, 1)

            def moved(n, bank_hi, bank_lo):
                dve.wait_ge(perm_done, n + 1)
                hif, lof, vf = RA[:, 3500:3500 + SLOTS], RA[:, 3916:3916 + SLOTS], RA[:, 4332:4332 + SLOTS]
                vi, ri, li = (RA[:, 4748 + SLOTS * k:4748 + SLOTS * (k + 1)].bitcast(I32) for k in range(3))
                st.link(dve.tensor_copy(lof, bank_lo[:, 0:SLOTS]))
                st.link(dve.scalar_tensor_tensor(vf, bank_hi[:, 0:SLOTS], 2048.0, lof, ALU.mult, ALU.add))
                st.link(dve.tensor_copy(vi, vf))
                st.did(dve.tensor_scalar(ri, vi, 7, None, ALU.logical_shift_right))
                st.did(dve.tensor_scalar(li, vi, P - 1, None, ALU.bitwise_and))
                st.link(dve.tensor_scalar(hif, vf, float(P), None, ALU.is_lt))
                st.link(dve.tensor_scalar(IDX[n][:, :], ri, -1.0, 0.0, ALU.add, ALU.max))
                st.link(dve.tensor_tensor(LOC[n][:, :], li, hif, ALU.subtract))

            dve.wait_ge(edges_in, 48)
            place(0)
            with dve.Fori(0, EC // COLS) as i:
                for s in range(COLS):
                    column(0, i * COLS + s, i * COLS + (s + 1), permA[s], permR[s], s in SHARED)
            moved(0, bank[2], bank[3])
            for q in range(CH // PART):
                indices(0, 0, q)
            place(1)

            dve.wait_ge(w_in, 16 * 21)
            for k in range(2):
                b, g, be, m, v = (bn[:, 5 * k + j, :] for j in range(5))
                dve.tensor_scalar(sc[:, 2 * k, :], v, BN_EPS, None, ALU.add).then_inc(var_ready, 1)
                dve.wait_ge(std_ready, 2 + k)
                st.link(dve.reciprocal(sc[:, 2 * k, :], sc[:, 2 * k + 1, :]))
                st.did(dve.tensor_tensor(sc[:, 2 * k, :], sc[:, 2 * k, :], g, ALU.mult))
                st.link(dve.tensor_tensor(sc[:, 2 * k + 1, :], b, m, ALU.subtract))
                st.link(dve.tensor_tensor(sc[:, 2 * k + 1, :], sc[:, 2 * k + 1, :], sc[:, 2 * k, :], ALU.mult))
                st.link(dve.tensor_tensor(sc[:, 2 * k + 1, :], sc[:, 2 * k + 1, :], be, ALU.add))
            st.did(dve.tensor_tensor(bias[:, 7, :], bias[:, 5, :], bias[:, 6, :], ALU.add))
            st.did(dve.tensor_tensor(gate_b[:, 1, :], gate_b[:, 1, :], gate_b[:, 2, :], ALU.add))
            for s in range(2):
                st.did(dve.memset(vb[s][:, D:D + 2], 1.0))
            st.link(dve.memset(kvbd[:, :, :], 0.0))
            barrier()

            def onehot(n, i, s):
                dve.tensor_scalar(hot[:, s % HOTS, :], iota[:, 0:P], LOC[n][:, ds(i * CH + s, 1)], None, ALU.is_equal
                                  ).then_inc(hot_ready, 1)

            def aggregate(layer, dst, stride, cols, banks, work, after=None):
                n, parts = (0 if layer < 2 else 1), CH // PART
                if layer:
                    for q in range(parts):
                        indices(n, 0, q)
                for s in range(HOTS):
                    onehot(n, 0, s)
                for i, here in turns(dve):
                    for s in range(CH):
                        at = i * CH + (SLOTS * layer + s)
                        if s % LOADS == 0:
                            _, starts = nc.values_load_multi_w_load_instructions(
                                TIL[n][0:1, ds(i * CH + s, LOADS)], engines=[mybir.EngineType.DVE], min_val=0, max_val=NT * stride,
                                skip_runtime_bounds_check_because="the sort writes the starts of its tiles, of which there are NT + 1")
                        dve.wait_ge(summed, at + 1)
                        dve.wait_ge(added, at + PSB)
                        if after and s % UNIT == after[0] + 1 and s // UNIT < here:
                            dve.wait_ge(after[1], i * 2 + (s // UNIT + READY))
                        a = dst[:, ds(starts[s % LOADS], cols)]
                        dve.tensor_tensor(a, a, bank[banks[s % len(banks)]][:, 0:cols], ALU.add).then_inc(added, 1)
                        beside(work, i, here, s)
                        if layer < 2 and s % 2 and not (layer == 1 and here == 1):
                            c = i * CPT + (C0 * layer + s // 2)
                            column(1, c, c + (EC + COLS - HCOLS + 1), permA1[s // 2 % HCOLS], permR1[s // 2 % HCOLS], True)
                        if s + HOTS < CH:
                            onehot(n, i, s + HOTS)
                        elif here == 2:
                            onehot(n, i + 1, s + HOTS - CH)
                        if s % PART == PART - 1 and here == 2:
                            indices(n, i + 1, s // PART)

            def kv_bias(t, s):
                dve.wait_ge(S["c1_p"], t + READY)
                dve.wait_ge(S["c1_kv"], t + FREE)
                p = bank[3]
                dve.tensor_tensor(kb[s], p[:, 0:D], bias[:, 0, :], ALU.add).then_inc(S["c1_kb"], 1)
                dve.tensor_tensor(vb[s][:, 0:D], p[:, D:2 * D], bias[:, 1, :], ALU.add).then_inc(S["c1_v"], 1)

            def k_feature(t, s):
                dve.wait_ge(S["c1_e"], t + READY)
                dve.tensor_scalar(mb[s], eb[s], 1.0, None, ALU.min).then_inc(S["c1_m"], 1)
                dve.wait_ge(S["c1_m"], t + 1)
                dve.scalar_tensor_tensor(kf[s], kb[s], 0.0, mb[s], ALU.max, ALU.add).then_inc(S["c1_kf"], 1)

            def q_bias(t, s):
                dve.wait_ge(S["c2_q"], t + READY)
                dve.wait_ge(S["c2_n"], t + FREE)
                p = bank[2][:, D:2 * D]
                for m in range(2):
                    ins = dve.tensor_scalar(kb[s][:, m * P:(m + 1) * P], p[:, m * P:(m + 1) * P], bq[:, m:m + 1], 0.0,
                                            ALU.add, ALU.max)
                ins.then_inc(S["c2_qb"], 1)

            def q_feature(t, s):
                dve.wait_ge(S["c2_e"], t + 1)
                dve.scalar_tensor_tensor(kf[s], eb[s], 1.0, kb[s], ALU.min, ALU.add).then_inc(S["c2_qf"], 1)

            def q_normalise(t, s):
                dve.wait_ge(S["c2_n"], t + READY)
                n = bank[3]
                dve.tensor_scalar(nr[s][:, 0:NE], n[:, D:D + NE], 1e-6, None, ALU.add).then_inc(S["c2_d"], 1)
                wait_alone(dve, S["c2_d"], t + 1)
                dve.reciprocal(nr[s][:, NE:2 * NE], nr[s][:, 0:NE]).then_inc(S["c2_r"], 1)
                dve.wait_ge(S["c2_r"], t + 1)
                dve.wait_ge(S["c2_oT"], t + FREE)
                dve.tensor_tensor(of[s].rearrange("p (h e) -> p h e", h=NE), n[:, 0:D].rearrange("p (h e) -> p h e", h=NE),
                                  nr[s][:, NE:2 * NE].unsqueeze(2).to_broadcast([P, NE, HEAD0]), ALU.mult
                                  ).then_inc(S["c2_o"], 1)

            def q_out(t, s):
                dve.wait_ge(S["c2_y"], t + READY)
                dve.tensor_tensor(xt(t), xt(t), bank[4][:, D:2 * D], ALU.add).then_inc(S["c2_x"], 1)

            def x_plus(t, s):
                dve.wait_ge(S["i_y"], t + READY)
                dve.wait_ge(added, t * UNIT + (SLOTS * 2 + 6 + 1 + PSB))
                dve.tensor_tensor(xt(t), xt(t), bank[3][:, 0:D], ALU.add).then_inc(S["i_x"], 1)

            def dense(layer):
                if layer == 0:
                    st.link(dve.tensor_scalar(MV[:, 2, 0:NT], AGG[:, 0:NT * DS].rearrange("p (t c) -> p c t", c=DS)[:, D, :], 1.0,
                                              None, ALU.max))
                    st.did(dve.memset(MV[:, 3, NT:NT + 1], 0.0))
                    st.link(dve.reciprocal(MV[:, 3, 0:NT], MV[:, 2, 0:NT]))

                def mean(t, s, free):
                    dve.wait_ge(S["d_T"], free)
                    dve.tensor_scalar(nb[s], AGG[:, ds(t * DS, D)], MV[:, 3, ds(t, 1)], None, ALU.mult).then_inc(S["d_nb"], 1)

                o = NT * layer
                mean(0, 0, o + FREE)
                mean(1, 1, o + FREE + 1)
                for t, s in tiles(dve):
                    if layer:
                        st.turn(t, 1)
                    if not isinstance(t, int):
                        mean(t + 2, s, t + (o + FREE + 2))
                    dve.wait_ge(S["d_y"], t + (o + READY))
                    if layer == 0:
                        dve.tensor_scalar(XN[:, ds(t * ROW, D)], bank[2 + s][:, 0:D], 0.0, None, ALU.max).then_inc(S["d_u"], 1)
                    else:
                        dve.scalar_tensor_tensor(xt(t), bank[2 + s][:, 0:D], 0.0, xt(t), ALU.max, ALU.add).then_inc(S["d_u"], 1)
                        wait_alone(dve, S["d_u"], t + (o + READY))
                        st.did(moments(t))
                if layer:
                    st.ended(NT)

            st.link(dve.memset(AGG[:, :], 0.0))
            aggregate(0, AGG, DS, DS, [0, 1], {6: kv_bias, 9: k_feature})
            dve.wait_ge(S["kv_done"], 1)
            for h in range(2):
                for a in range(4):
                    hd = 4 * h + a
                    r = slice(32 * a, 32 * a + 32)
                    st.did(dve.tensor_copy(kvbd[r, h, hd * HEAD0:(hd + 1) * HEAD0],
                                           bank[4 + h][r, hd * HEAD0:(hd + 1) * HEAD0]))
                    st.did(dve.tensor_copy(kvbd[r, h, D + hd:D + hd + 1], bank[4 + h][r, D:D + 1]))
            barrier()
            dense(0)
            dve.wait_ge(S["d_nb"], NT + 1 + 2)
            st.did(dve.memset(AGG[:, :], 0.0))
            barrier()
            barrier()
            aggregate(1, AGG, DS, D, [0, 1], {3: q_bias, 5: q_feature, 9: q_normalise, 14: q_out})
            moved(1, bank[6], bank[7])
            barrier()
            dense(1)
            stats(4)
            barrier()

            def x_add(g, n_tiles, e, scale, psum_banks, sig_y, sig_acc, sig_b):
                dve.wait_ge(S[sig_y], g * NE + (e + READY))
                if e == 0:
                    dve.wait_ge(S[sig_b], g + 2)
                else:
                    dve.wait_ge(S[sig_acc], g * NE + (e + 1))
                for j in range(n_tiles):
                    x_ = xt(g * GT + j)
                    ins = dve.scalar_tensor_tensor(x_, bank[psum_banks + j // 2][:, (j % 2) * D:(j % 2 + 1) * D],
                                                   scale[:, j * NE + e:j * NE + e + 1], x_, ALU.mult, ALU.add)
                ins.then_inc(S[sig_acc], 1)

            def norm_group(g, n_tiles):
                dve.wait_ge(S["f_T"], g + 1)
                for j in range(n_tiles):
                    ins = norm(xgin[:, j, :], g * GT + j)
                ins.then_inc(S["f_in"], 1)

            norm_group(0, GT)
            for g, T_, next_T in groups(dve):
                st.turn(g, 5)
                dve.wait_ge(S["f_r"], g + 1)
                n = T_ * NE
                v = [rt[:, k, 0:n].rearrange("p (t e) -> p t e", e=NE) for k in range(8)]
                st.link(dve.tensor_tensor(v[0], bank[6][:, 0:n].rearrange("p (t e) -> p t e", e=NE),
                                          gate_b[:, 0:1, :].to_broadcast([P, T_, NE]), ALU.add))
                st.link(dve.tensor_reduce(rt[:, 1, 0:T_], v[0], AX.X, ALU.max))
                dve.tensor_tensor(v[2], v[0], rt[:, 1, 0:T_].unsqueeze(2).to_broadcast([P, T_, NE]), ALU.subtract
                                  ).then_inc(S["f_rm"], 1)
                dve.wait_ge(S["f_re"], g + 1)
                st.link(dve.tensor_reduce(rt[:, 4, 0:T_], v[3], AX.X, ALU.add))
                st.link(dve.reciprocal(rt[:, 5, 0:T_], rt[:, 4, 0:T_]))
                dve.tensor_tensor(v[6], v[3], rt[:, 5, 0:T_].unsqueeze(2).to_broadcast([P, T_, NE]), ALU.mult
                                  ).then_inc(S["f_w"], 1)
                dve.wait_ge(S["f_wT"], g + 1)
                dve.tensor_copy(wT[:, 0:T_ * P], bank[7][0:NE, 0:T_ * P]).then_inc(S["f_wTs"], 1)
                dve.wait_ge(S["f_b"], g + 1)
                for j in range(T_):
                    x_ = xt(g * GT + j)
                    ins = dve.tensor_tensor(x_, x_, bank[6 + j // 2][:, (j % 2) * D:(j % 2 + 1) * D], ALU.add)
                ins.then_inc(S["f_bx"], 1)
                if next_T:
                    norm_group(g + 1, next_T)
                for e in range(NE):
                    x_add(g, T_, e, rt[:, 6, :], 4, "f_y", "f_acc", "f_bx")
                wait_alone(dve, S["f_acc"], g * NE + (NE + 1))
                for j in range(T_):
                    ins = moments(g * GT + j)
                st.did(ins)
            st.ended(NG + 1)
            stats(5)
            barrier()

            st.did(dve.memset(DT[:, :, :], 0.0))
            hv = wkv1.rearrange("p k n -> p (k n)").rearrange("p (h e) -> p h e", e=HEAD1)
            st.link(dve.tensor_reduce(rs[:, 0:32], hv, AX.X, ALU.add))
            st.link(dve.tensor_scalar(rs[:, 32:64], rs[:, 0:32], 1.0 / HEAD1, None, ALU.mult))
            dve.tensor_tensor(hv, hv, rs[:, 32:64].unsqueeze(2).to_broadcast([P, 32, HEAD1]), ALU.subtract
                              ).then_inc(S["wkv_c"], 1)
            norm(XN[:, 0:D], 0).then_inc(S["g_in"], 1)
            for t, s in tiles(dve):
                st.turn(t, 3)
                if not isinstance(t, int):
                    norm(XN[:, ds(t * ROW + ROW, D)], t + 1).then_inc(S["g_in"], 1)
                dve.wait_ge(S["g_sq"], t + 1)
                st.link(dve.tensor_reduce(rs[:, 0:16], sq.rearrange("p (h e) -> p h e", e=HEAD1), AX.X, ALU.add))
                dve.tensor_scalar(rs[:, 16:32], rs[:, 0:16], 1.0 / HEAD1, LN_EPS, ALU.mult, ALU.add).then_inc(S["g_var"], 1)
                dve.wait_ge(S["g_std"], t + 1)
                st.link(dve.reciprocal(rs[:, 32:48], rs[:, 48:64]))
                st.link(dve.tensor_tensor(rs[:, 0:8], rs[:, 32:40], rs[:, 40:48], ALU.mult))
                dve.wait_ge(S["g_dt"], t + 1)
                dve.tensor_tensor(kc.rearrange("p (h e) -> p h e", e=HEAD1), bank[6][:, :].rearrange("p (h e) -> p h e", e=HEAD1),
                                  rs[:, 0:8].unsqueeze(2).to_broadcast([P, NE, HEAD1]), ALU.mult).then_inc(S["g_kc"], 1)
                for q in range(2, 4):
                    dve.wait_ge(S["g_h"], t * 4 + (q + 1 + 5))
                    if q == 2:
                        dve.wait_ge(hall_stored[s], t * 8 + (16 - 8 * s))
                    dve.tensor_copy(ho[s][:, q * 512:(q + 1) * 512], bank[2 + q][:, :]).then_inc(S["g_hd"], 1)
            st.ended(NT)
            dve.wait_ge(S["g_dt"], NT + 2)
            b1 = bank[1][:, :].rearrange("p (a b) -> p a b", b=P)
            st.did(dve.tensor_scalar(DT[0:64, :, 0:64], b1[0:64, :, 0:64], 1.0 / N, None, ALU.mult))
            dve.tensor_scalar(DT[64:P, :, 64:P], b1[64:P, :, 64:P], 1.0 / N, None, ALU.mult).then_inc(S["g_dtr"], 1)
            dve.wait_ge(S["g_mp"], 1)
            for h in range(2):
                ins = dve.tensor_copy(MP[:, 2 * h:2 * h + 2, :].rearrange("p a b -> p (a b)"), bank[2 + h][:, :])
            ins.then_inc(S["g_mps"], 1)
            dve.wait_ge(S["g_we"], 1)
            dve.tensor_copy(WEFF.rearrange("p a b -> p (a b)"), bank[4][:, :])
            barrier()
            aggregate(2, X, D, D, [0, 1, 4, 5], {6: x_plus}, (6, S["i_x"]))
            dve.wait_ge(added, 3 * SLOTS + PSB)
            all_moments()
            stats(6)
            barrier()

            with dve.Fori(0, NT // OG) as i:
                for j in range(OG):
                    norm(XN[:, ds(i * OG * ROW + j * ROW, D)], i * OG + j).then_inc(S["r_in"], 1)
            dve.wait_ge(S["i_y"], 2 * NT + 2)
            st.link(dve.tensor_tensor(logits, bank[2][:, 0:NT * NE].rearrange("p (t e) -> p t e", e=NE),
                                      gate_b[:, 1:2, :].to_broadcast([P, NT, NE]), ALU.add))
            for t in range(NT):
                st.did(dve.max(best[:, t, :], logits[:, t, :]))
            st.wait()
            for t in range(NT):
                st.did(dve.max_index(bestat[:, t, :], best[:, t, :], logits[:, t, :]))
            dve.tensor_tensor(MV[:, 4, 0:NT], best[:, :, 1], best[:, :, 0], ALU.subtract).then_inc(S["r_d"], 1)
            st.wait()
            for k in range(TOP):
                st.did(dve.tensor_copy(chosen[:, k, :], bestat[:, :, k]))
            st.wait()
            st.link(dve.tensor_tensor(chosen[:, :, NT - 1], chosen[:, :, NT - 1], beyond[:, :].to_broadcast([P, TOP]), ALU.add))
            dve.wait_ge(S["r_e"], 1)
            st.link(dve.tensor_scalar(MV[:, 6, 0:NT], MV[:, 5, 0:NT], 1.0, None, ALU.add))
            st.link(dve.reciprocal(MV[:, 2, 0:NT], MV[:, 6, 0:NT]))
            st.did(dve.tensor_tensor(MV[:, 3, 0:NT], MV[:, 2, 0:NT], MV[:, 5, 0:NT], ALU.mult))
            items = chosen.rearrange("p k t -> p (k t)")
            for e in range(NE):
                st.did(dve.tensor_scalar(mask[:, e, :], items, float(e), 0.0, ALU.is_equal, ALU.add, accum_out=small[:, e:e + 1]))
            c = starts(2, NE, XCH)
            st.did(dve.tensor_scalar(wexp[:, 0:XCH], bank[1][:, 0:XCH], float(NE - 1), float(WST), ALU.min, ALU.mult))
            st.did(dve.tensor_scalar(bexp[:, 0:XCH], bank[1][:, 0:XCH], float(NE - 1), float(BST), ALU.min, ALU.mult))
            st.link(dve.memset(ipos, -1.0))
            for e in range(NE):
                st.link(dve.tensor_tensor_scan(rank[e % 2], mask[:, e, :], zeros[:, 0:ITEMS], c[:, e:e + 1], ALU.add, ALU.add))
                st.link(dve.copy_predicated(ipos, mask[:, e, :].bitcast(I32), rank[e % 2]))
            st.did(dve.tensor_scalar(item_slot, ipos, 0.0, None, ALU.max))
            st.did(dve.tensor_scalar(tokens, iota[:, 0:NT], float(P), rowf[:, :], ALU.mult, ALU.add))
            st.link(dve.tensor_copy(itemi[0], ipos))
            st.did(dve.tensor_scalar(itemi[1], itemi[0], P - 1, None, ALU.bitwise_and))
            st.did(dve.tensor_scalar(itemi[2], itemi[0], 7, None, ALU.arith_shift_right))
            st.wait()
            for k in range(2):
                st.did(dve.tensor_copy(itemf[k], itemi[1 + k]))
            st.wait()
            with dve.Fori(0, NT) as t:
                for k in range(TOP):
                    q, r = (itemf[j][:, ds(t + k * NT, 1)] for j in range(2))
                    dve.wait_ge(perm_used, t * TOP + (2 * EC + k + 1 + COLS - TOP))
                    dve.tensor_scalar(itemA[k], iota[:, 0:P], q, tokens[:, ds(t, 1)], ALU.is_equal, ALU.mult)
                    dve.tensor_scalar(itemR[k], iota[:, 0:XCH], r, None, ALU.is_equal).then_inc(perm_ready, 1)
            dve.wait_ge(perm_done, 3)
            st.did(dve.tensor_copy(slot_token, bank[3][:, 0:XCH]))
            barrier()

            def out_bias(d, s, before, start):
                dve.wait_ge(S["e_l2"], d + READY)
                dve.wait_ge(ys_stored[s], before * 16 + 16)
                dve.tensor_tensor(yo[s], bank[6 + s][:, 0:D], AGG[:, ds(start + HW, D)], ALU.add).then_inc(S["e_y"], 1)

            for c, s, before, _, _ in chunks(dve):
                at, span = (0, 1) if isinstance(c, int) and c == 0 else (c - 1, 2)
                _, b = nc.values_load_multi_w_load_instructions(
                    bexp[0:1, ds(at, span)], engines=[mybir.EngineType.DVE], min_val=0, max_val=(NE - 1) * BST,
                    skip_runtime_bounds_check_because="a minimum with the last expert's start bounds it")
                dve.wait_ge(S["e_l1"], c + READY)
                dve.wait_ge(S["e_Th"], c + FREE)
                dve.tensor_tensor(hs[s], bank[2 + s][:, :], AGG[:, ds(b[-1], HW)], ALU.add).then_inc(S["e_h"], 1)
                if not (isinstance(c, int) and c == 0):
                    out_bias(c - 1, 1 - s, before, b[0])
            out_bias(XCH - 1, 1, XCH // 2 - 1, b[-1])
            barrier()

            for g in range(NT // OG):
                dve.wait_ge(gathered[g], 16 * (3 * TURNS + len(range(g, XCH, XB)) + TOP * OG))
                for k in range(TOP):
                    for t in range(g * OG, (g + 1) * OG):
                        x_ = xt(t)
                        ins = dve.scalar_tensor_tensor(x_, yr[k][:, t, 0:D], MV[:, 2 + k, t:t + 1], x_, ALU.mult, ALU.add)
                        if (k, t) != (TOP - 1, g * OG + OG - 1):
                            st.did(ins)
                    if k < TOP - 1:
                        st.wait()
                ins.then_inc(S["x_done"], 1)

        @block.scalar
        def _(act):
            barrier = Barrier(act)
            for name, k in CREDIT["act"].items():
                act.sem_inc(S[name], k)
            act.sem_inc(place_ready, len(away))

            def std(n, dst, src):
                act.wait_ge(var_ready, n)
                act.activation(dst, src, ACT.Sqrt).then_inc(std_ready, 1)

            std(1, MV[:, 2, 0:NT], MV[:, 7, 0:NT])
            barrier()

            def column(n, c, free, count, A, y):
                q, hi, lo = (moves[n][0:EP, ds(c + EC * k, 1)] for k in (0, 2, 3))
                wait_alone(act, place_ready, count)
                act.activation(y[0:EP, :], iota16[0:EP, 0:P], ACT.Abs, bias=q, scale=-1.0).then_inc(abs_ready, 1)
                yield
                wait_alone(act, perm_used, free)
                wait_alone(act, abs_ready, count)
                act.activation(A[0:EP, 0:P], y[0:EP, :], ACT.Relu, bias=hi, scale=minus[n][0][0:EP, ds(c, 1)])
                act.activation(A[0:EP, P:2 * P], y[0:EP, :], ACT.Relu, bias=lo, scale=minus[n][1][0:EP, ds(c, 1)]
                               ).then_inc(place_ready, 1)

            act.wait_ge(moves_ready, 1)
            with act.Fori(0, EC // COLS) as i:
                both = [column(0, i * COLS + s, i * COLS + (s + 1), i * len(SHARED) + (k + 1), permA[s], away[k])
                        for k, s in enumerate(SHARED)]
                for _ in range(2):
                    for shared in both:
                        next(shared, None)
            std(2, sc[:, 1, :], sc[:, 0, :])
            std(3, sc[:, 3, :], sc[:, 2, :])
            barrier()

            def gathering(layer, work):
                for i, here in turns(act):
                    for s in range(CH):
                        beside(work, i, here, s)
                        if layer < 2 and s % 2 and not (layer == 1 and here == 1):
                            m = s // 2
                            c = i * CPT + (C0 * layer + m)
                            for _ in column(1, c, c + (EC + COLS - HCOLS + 1), c + (EC // COLS * len(SHARED) + 1), permA1[m % HCOLS], away[m % 2]):
                                pass

            def kv_in(t, s):
                wait_alone(act, S["c1_T"], t + FREE)
                act.copy(xin[s], XN[:, ds(t * ROW, D)]).then_inc(S["c1_in"], 1)
                act.wait_ge(S["c1_T"], t + READY)
                act.wait_ge(S["c1_p"], t + FREE)
                act.copy(xT[s].rearrange("p a b -> p (a b)"), bank[2][:, 0:D]).then_inc(S["c1_xT"], 1)

            def k_exp(t, s):
                act.wait_ge(S["c1_kb"], t + 1)
                act.wait_ge(S["c1_kf"], t + FREE)
                act.activation(eb[s], kb[s], ACT.Exp).then_inc(S["c1_e"], 1)

            def q_in(t, s):
                wait_alone(act, S["c2_T"], t + FREE)
                act.activation(xin[s], xt(t), ACT.Identity, bias=MV[:, 4, ds(t, 1)], scale=MV[:, 1, ds(t, 1)]
                               ).then_inc(S["c2_in"], 1)
                act.wait_ge(S["c2_T"], t + READY)
                act.wait_ge(S["c2_q"], t + FREE)
                act.copy(xT[s].rearrange("p a b -> p (a b)"), bank[2][:, 0:D]).then_inc(S["c2_xT"], 1)

            def q_exp(t, s):
                act.wait_ge(S["c2_qb"], t + 1)
                act.wait_ge(S["c2_qf"], t + FREE)
                for m in range(2):
                    ins = act.activation(eb[s][:, m * P:(m + 1) * P], bank[2][:, D + m * P:D + (m + 1) * P], ACT.Exp,
                                         bias=bq[:, m:m + 1])
                ins.then_inc(S["c2_e"], 1)

            def q_outT(t, s):
                act.wait_ge(S["c2_oT"], t + READY)
                act.wait_ge(S["c2_y"], t + FREE)
                act.copy(oT[s].rearrange("p a b -> p (a b)"), bank[4][:, 0:D]).then_inc(S["c2_oTs"], 1)

            def attn_in(t, s):
                wait_alone(act, S["i_T"], t + FREE)
                act.copy(xin[s], XN[:, ds(t * ROW, D)]).then_inc(S["i_in"], 1)
                act.wait_ge(S["i_T"], t + READY)
                act.wait_ge(S["i_y"], t + FREE)
                act.copy(xT[s].rearrange("p a b -> p (a b)"), bank[2][:, 0:D]).then_inc(S["i_xT"], 1)

            def dense(layer):
                o = NT * layer

                def load(t, s):
                    wait_alone(act, S["d_T"], t + (o + FREE))
                    act.copy(xin[s], XN[:, ds(t * ROW, D)]).then_inc(S["d_in"], 1)

                load(0, 0)
                for t, s in tiles(act):
                    if not isinstance(t, int):
                        load(t + 1, 1 - s)
                    act.wait_ge(S["d_T"], t + (o + READY))
                    act.wait_ge(S["d_y"], t + (o + FREE))
                    act.copy(cT[s].rearrange("p a b -> p (a b)"), bank[s][:, :]).then_inc(S["d_cT"], 1)

            gathering(0, {0: kv_in, 7: k_exp})
            barrier()
            dense(0)
            barrier()
            barrier()
            gathering(1, {0: q_in, 4: q_exp, 12: q_outT})
            barrier()
            dense(1)
            std(4, MV[:, 2, 0:NT], MV[:, 7, 0:NT])
            barrier()
            for g, T_, next_T in groups(act):
                act.wait_ge(S["f_T"], g + 2)
                act.wait_ge(S["f_l1"], g * 16 + 1)
                for k in range(2):
                    ins = act.copy(xg[:, k, 0:T_ * P], bank[k][:, 0:T_ * P])
                ins.then_inc(S["f_xT"], 1)

                def relu(e, first):
                    lay, h, l_, wait_free = (0, h1, "f_l1", "f_l2") if first else (1, h2, "f_l2", "f_y")
                    for m in range(2):
                        if first:
                            act.wait_ge(S["f_l1"], g * 16 + (2 * e + m + 2))
                            if m == 0:
                                act.wait_ge(S["f_l2"], g * 16 + 2 * e + 1)
                        else:
                            act.wait_ge(S["f_l2"], g * 16 + (2 * e + m + 4))
                            if m == 0:
                                act.wait_ge(S["f_y"], g * NE + (e + FREE))
                        act.activation(h[e % 2][:, m, 0:T_ * P], bank[(2 if first else 0) + m][:, 0:T_ * P], ACT.Relu,
                                       bias=sc[:, 2 * lay + 1, 2 * e + m:2 * e + m + 1],
                                       scale=sc[:, 2 * lay, 2 * e + m:2 * e + m + 1]).then_inc(S["f_h1" if first else "f_h2"], 1)

                relu(0, True)
                for e in range(NE):
                    if e + 1 < NE:
                        relu(e + 1, True)
                    if e == 0:
                        act.wait_ge(S["f_rm"], g + 1)
                        act.activation(rt[:, 3, 0:T_ * NE], rt[:, 2, 0:T_ * NE], ACT.Exp).then_inc(S["f_re"], 1)
                    relu(e, False)
            std(5, MV[:, 2, 0:NT], MV[:, 7, 0:NT])
            barrier()
            def kv_in(t, s):
                wait_alone(act, S["g_T"], t + FREE)
                act.wait_ge(S["g_in"], t + READY)
                act.copy(xin[s], XN[:, ds(t * ROW, D)]).then_inc(S["g_c"], 1)

            def kv_xT(t, s):
                act.wait_ge(S["g_T"], t + READY)
                act.wait_ge(S["g_h"], t * 4 + 1)
                act.copy(xT[s].rearrange("p a b -> p (a b)"), bank[0][:, 0:D]).then_inc(S["g_xT"], 1)

            kv_in(0, 0)
            kv_xT(0, 0)
            for t, s in tiles(act):
                if not isinstance(t, int):
                    kv_in(t + 1, 1 - s)
                act.wait_ge(S["g_kvp"], t + 1)
                act.wait_ge(S["g_var"], t + 1)
                for k in range(2):
                    ins = act.activation(sq[:, k * 512:(k + 1) * 512], bank[6 + k][:, :], ACT.Square)
                ins.then_inc(S["g_sq"], 1)
                act.wait_ge(S["g_dt"], t + 1)
                act.copy(vc, bank[7][:, :]).then_inc(S["g_vc"], 1)
                act.wait_ge(S["g_var"], t + 2)
                act.activation(rs[:, 48:64], rs[:, 16:32], ACT.Sqrt).then_inc(S["g_std"], 1)
                if not isinstance(t, int):
                    kv_xT(t + 1, 1 - s)
                for q in range(2):
                    act.wait_ge(S["g_h"], t * 4 + (q + 1 + 5))
                    if q == 0:
                        act.wait_ge(hall_stored[s], t * 8 + (16 - 8 * s))
                    act.copy(ho[s][:, q * 512:(q + 1) * 512], bank[2 + q][:, :]).then_inc(S["g_ha"], 1)
            barrier()
            gathering(2, {0: attn_in})
            std(6, MV[:, 2, 0:NT], MV[:, 7, 0:NT])
            barrier()

            def gate_in(t, s):
                act.wait_ge(S["r_in"], t + 1)
                wait_alone(act, S["i_T"], t + (NT + FREE))
                act.copy(xin[s], XN[:, ds(t * ROW, D)]).then_inc(S["i_in"], 1)

            gate_in(0, 0)
            for t, s in tiles(act):
                if not isinstance(t, int):
                    gate_in(t + 1, 1 - s)
                act.wait_ge(S["i_T"], t + (NT + READY))
                act.wait_ge(S["i_y"], t + (NT + FREE))
                act.copy(xT[s].rearrange("p a b -> p (a b)"), bank[s][:, 0:D]).then_inc(S["i_xT"], 1)
            act.wait_ge(S["r_d"], 1)
            act.activation(MV[:, 5, 0:NT], MV[:, 4, 0:NT], ACT.Exp).then_inc(S["r_e"], 1)
            barrier()

            def x_T(d, s):
                act.wait_ge(S["e_T"], d + READY)
                act.wait_ge(S["e_l1"], d + FREE)
                act.copy(xT[s].rearrange("p a b -> p (a b)"), bank[s][:, 0:D]).then_inc(S["e_xT"], 1)

            x_T(0, 0)
            for c, s, _, _, _ in chunks(act):
                if not (isinstance(c, int) and c == XCH - 1):
                    x_T(c + 1, 1 - s)
                act.wait_ge(S["e_Th"], c + READY)
                act.wait_ge(S["e_l2"], c + FREE)
                act.activation(hT[s].rearrange("p a b -> p (a b)"), bank[4 + s][:, :], ACT.Relu).then_inc(S["e_hT"], 1)
            barrier()

        @block.tensor
        def _(pe):
            barrier = Barrier(pe)
            for name, k in CREDIT["pe"].items():
                pe.sem_inc(S[name], k)
            pe.sem_inc(perm_used, COLS)
            barrier()
            def close(b, start, stop):
                for k in range(2):
                    mm = pe.matmul(bank[b + k][:, 0:SLOTS], z16[0:EP, :], iota16[0:EP, :], start=start, stop=stop)
                return mm

            def column(c, b, A, R, shared):
                pe.wait_ge(perm_ready, c + 1)
                if shared is not None:
                    pe.wait_ge(place_ready, shared + len(away))
                for k in range(2):
                    mm = pe.matmul(bank[b + k][:, 0:SLOTS], A[0:EP, k * P:(k + 1) * P], R[0:EP, :], start=False, stop=False)
                mm.then_inc(perm_used, 1)

            def starts(n, rows, bins, slots):
                pe.wait_ge(counts_ready, n + 1)
                b0, c = bank[0], small[0:rows, 0:bins]
                pe.matmul(b0[:, 0:bins], tri[0:rows, :], c, start=True, stop=True)
                pe.matmul(b0[:, 32:32 + bins], ones[0:rows, :], c, start=True, stop=True)
                pe.matmul(b0[0:bins, 64:65], c, ones[0:rows, 0:1], start=True, stop=True).then_inc(prefix_ready, 1)
                pe.wait_ge(nch_ready, n + 1)
                pe.matmul(b0[0:bins, 66:67], trin[0:bins, 0:bins], small[0:bins, 224:225], start=True, stop=True
                          ).then_inc(chend_ready, 1)
                pe.wait_ge(ge_ready, n + 1)
                pe.matmul(bank[1][:, 0:slots], ones[0:bins, :], RA[0:bins, 3000:3000 + slots], start=True, stop=True
                          ).then_inc(til_ready, 1)

            for n in range(2):
                starts(n, EP, NT, SLOTS)
                if n == 0:
                    pe.wait_ge(perm_ready, 1)
                    close(2, start=True, stop=False)
                    with pe.Fori(0, EC // COLS) as i:
                        for s in range(COLS):
                            column(i * COLS + s, 2, permA[s], permR[s], i * len(SHARED) + (SHARED.index(s) + 1) if s in SHARED else None)
                    close(2, start=False, stop=True).then_inc(perm_done, 1)
            barrier()

            def transpose(dst, src):
                for k in range(src.shape[-1] // P):
                    mm = pe.transpose(dst[:, k * P:(k + 1) * P], src[:, k * P:(k + 1) * P], ident[:, :])
                return mm

            def kv_T(t, s):
                pe.wait_ge(S["c1_in"], t + READY)
                pe.wait_ge(S["c1_xT"], t + FREE + 1)
                transpose(bank[2], xin[s]).then_inc(S["c1_T"], 1)

            def kv_products(t, s):
                pe.wait_ge(S["c1_xT"], t + READY)
                pe.wait_ge(S["c1_v"], t + FREE + 1)
                for k in range(2):
                    mm = pe.matmul(bank[3][:, :], xT[s][:, k, :], wkv0[:, k, :], start=(k == 0), stop=(k == 1))
                mm.then_inc(S["c1_p"], 1)

            def kv_sums(t, s):
                rows = LAST if isinstance(t, int) else P
                pe.wait_ge(S["c1_kf"], t + READY)
                for h in range(2):
                    mm = pe.matmul(bank[4 + h][:, 0:D + 2], kf[s][0:rows, h * P:(h + 1) * P], vb[s][0:rows, 0:D + 2],
                                   start=False, stop=False)
                mm.then_inc(S["c1_kv"], 1)

            def q_T(t, s):
                pe.wait_ge(S["c2_in"], t + READY)
                pe.wait_ge(S["c2_qf"], t + FREE + 1)
                transpose(bank[2], xin[s]).then_inc(S["c2_T"], 1)

            def q_products(t, s):
                pe.wait_ge(S["c2_xT"], t + READY)
                for m in range(2):
                    for k in range(2):
                        mm = pe.matmul(bank[2][:, D + m * P:D + (m + 1) * P], wq0[:, k, m * P:(m + 1) * P], xT[s][:, k, :],
                                       start=(k == 0), stop=(k == 1))
                mm.then_inc(S["c2_q"], 1)

            def q_kv(t, s):
                pe.wait_ge(S["c2_qf"], t + READY)
                pe.wait_ge(S["c2_o"], t + FREE + 1)
                for m in range(2):
                    mm = pe.matmul(bank[3][:, 0:D + NE], kf[s][:, m * P:(m + 1) * P], kvbd[:, m, :],
                                   start=(m == 0), stop=(m == 1))
                mm.then_inc(S["c2_n"], 1)

            def q_outT(t, s):
                pe.wait_ge(S["c2_o"], t + READY)
                pe.wait_ge(S["c2_x"], t + FREE + 1)
                transpose(bank[4], of[s]).then_inc(S["c2_oT"], 1)

            def q_out(t, s):
                pe.wait_ge(S["c2_oTs"], t + READY)
                for k in range(2):
                    mm = pe.matmul(bank[4][:, D:2 * D], oT[s][:, k, :], wo0[:, k, :], start=(k == 0), stop=False)
                pe.matmul(bank[4][:, D:2 * D], ones[0:1, :], bias[0:1, 2, :], start=False, stop=True).then_inc(S["c2_y"], 1)

            def attn_T(t, s):
                pe.wait_ge(S["i_in"], t + READY)
                pe.wait_ge(S["i_xT"], t + FREE + 1)
                transpose(bank[2], xin[s]).then_inc(S["i_T"], 1)

            def attn_out(t, s):
                pe.wait_ge(S["i_xT"], t + READY)
                pe.wait_ge(S["i_x"], t + FREE + 1)
                for k in range(2):
                    mm = pe.matmul(bank[3][:, 0:D], xT[s][:, k, :], WEFF[:, k, :], start=(k == 0), stop=False)
                pe.matmul(bank[3][:, 0:D], ones[0:1, :], bias[0:1, 7, :], start=False, stop=True).then_inc(S["i_y"], 1)

            def aggregate(layer, cols, banks, work):
                for i, here in turns(pe):
                    for s in range(CH):
                        at = i * CH + (SLOTS * layer + s)
                        pe.wait_ge(hot_ready, at + 1)
                        pe.wait_ge(gathered[s], i * 16 + (TURNS * layer + 1) * 16)
                        pe.wait_ge(added, at + (1 + PSB - len(banks)))
                        pe.matmul(bank[banks[s % len(banks)]][:, 0:cols], hot[:, s % HOTS, :], ring[:, s, 0:cols],
                                  start=True, stop=True).then_inc(summed, 1)
                        beside(work, i, here, s)
                        if layer < 2 and s % 2 and not (layer == 1 and here == 1):
                            if s > 1:
                                m = s // 2 - 1
                                column(i * CPT + (EC + C0 * layer + m), 6, permA1[m % HCOLS], permR1[m % HCOLS],
                                       i * CPT + (EC // COLS * len(SHARED) + C0 * layer + m + 1))
                            if s == CH - 1:
                                m = s // 2
                                column(i * CPT + (EC + C0 * layer + m), 6, permA1[m % HCOLS], permR1[m % HCOLS],
                                       i * CPT + (EC // COLS * len(SHARED) + C0 * layer + m + 1))

            def dense(layer):
                o = NT * layer

                def inT(t, s):
                    pe.wait_ge(S["d_in"], t + (o + READY))
                    pe.wait_ge(S["d_nb"], t + ((NT + 1) * layer + READY))
                    pe.wait_ge(S["d_cT"], t + (o + FREE))
                    transpose(bank[s], xin[s])
                    transpose(bank[s][:, D:2 * D], nb[s]).then_inc(S["d_T"], 1)

                inT(0, 0)
                for t, s in tiles(pe):
                    if not isinstance(t, int):
                        inT(t + 1, 1 - s)
                    pe.wait_ge(S["d_cT"], t + (o + READY))
                    pe.wait_ge(S["d_u"], t + (o + FREE))
                    for k in range(4):
                        pe.matmul(bank[2 + s][:, 0:D], cT[s][:, k, :], gw[layer][:, k, :], start=(k == 0), stop=False)
                    pe.matmul(bank[2 + s][:, 0:D], ones[0:1, :], bias[0:1, 3 + layer, :], start=False, stop=True
                              ).then_inc(S["d_y"], 1)

            close(6, start=True, stop=False)
            for h in range(2):
                pe.matmul(bank[4 + h][:, 0:D + 2], zeros[:, 0:P], zeros[:, 0:D + 2], start=True, stop=False)
            aggregate(0, DS, [0, 1], {1: kv_T, 4: kv_products, 12: kv_sums})
            for h in range(2):
                mm = pe.matmul(bank[4 + h][:, 0:D + 2], zeros[:, 0:P], zeros[:, 0:D + 2], start=False, stop=True)
            mm.then_inc(S["kv_done"], 1)
            barrier()
            dense(0)
            barrier()
            barrier()
            aggregate(1, D, [0, 1], {0: q_T, 2: q_products, 7: q_kv, 11: q_outT, 13: q_out})
            close(6, start=False, stop=True).then_inc(perm_done, 1)
            barrier()
            dense(1)
            barrier()

            def group_T(g, n_tiles):
                pe.wait_ge(S["f_in"], g + 1)
                pe.wait_ge(S["f_h2"], g * 16 + 2)
                for k in range(2):
                    for j in range(n_tiles):
                        mm = pe.transpose(bank[k][:, j * P:(j + 1) * P], xgin[:, j, k * P:(k + 1) * P], ident[:, :])
                mm.then_inc(S["f_T"], 1)

            group_T(0, GT)
            for g, T_, next_T in groups(pe):
                W = T_ * P
                pe.wait_ge(S["f_xT"], g + 1)
                pe.wait_ge(S["f_bx"], g + 1)
                for j in range(T_):
                    for k in range(2):
                        mm = pe.matmul(bank[6][:, j * NE:(j + 1) * NE], xg[:, k, j * P:(j + 1) * P], wr0[:, k, :],
                                       start=(k == 0), stop=(k == 1))
                mm.then_inc(S["f_r"], 1)

                def first(e):
                    for m in range(2):
                        pe.wait_ge(S["f_h1"], g * 16 + (2 * e + m + FREE))
                        for k in range(2):
                            mm = pe.matmul(bank[2 + m][:, 0:W], w1[:, e, k, m * P:(m + 1) * P], xg[:, k, 0:W],
                                           start=(k == 0), stop=(k == 1))
                        mm.then_inc(S["f_l1"], 1)

                def second(e):
                    pe.wait_ge(S["f_h1"], g * 16 + (2 * e + 1 + READY))
                    for m in range(2):
                        pe.wait_ge(S["f_h2"], g * 16 + (2 * e + m + FREE))
                        for k in range(2):
                            mm = pe.matmul(bank[m][:, 0:W], w2[:, e, k, m * P:(m + 1) * P], h1[e % 2][:, k, 0:W],
                                           start=(k == 0), stop=(k == 1))
                        mm.then_inc(S["f_l2"], 1)

                def third(e):
                    pe.wait_ge(S["f_h2"], g * 16 + (2 * e + 1 + READY))
                    pe.wait_ge(S["f_acc"], g * NE + e + 1)
                    for j in range(T_):
                        for k in range(2):
                            mm = pe.matmul(bank[4 + j // 2][:, (j % 2) * D:(j % 2 + 1) * D], h2[e % 2][:, k, j * P:(j + 1) * P],
                                           wo[:, e, k, :], start=(k == 0), stop=(k == 1))
                    mm.then_inc(S["f_y"], 1)

                def gates_T():
                    pe.wait_ge(S["f_w"], g + 1)
                    for j in range(T_):
                        mm = pe.transpose(bank[7][0:NE, j * P:(j + 1) * P], rt[:, 6, j * NE:(j + 1) * NE], ident[:, :])
                    mm.then_inc(S["f_wT"], 1)

                def out_bias():
                    pe.wait_ge(S["f_wTs"], g + 1)
                    for j in range(T_):
                        mm = pe.matmul(bank[6 + j // 2][:, (j % 2) * D:(j % 2 + 1) * D], wT[:, j * P:(j + 1) * P], bo_e[:, :],
                                       start=True, stop=True)
                    mm.then_inc(S["f_b"], 1)

                first(0)
                first(1)
                second(0)
                gates_T()
                for e in range(2, NE):
                    first(e)
                    if e == 2:
                        out_bias()
                    second(e - 1)
                    third(e - 2)
                second(NE - 1)
                third(NE - 2)
                if next_T:
                    group_T(g + 1, next_T)
                third(NE - 1)
            barrier()

            pe.wait_ge(S["wkv_c"], 1)
            pe.matmul(bank[1][:, :], zeros[:, 0:P], zeros[:, :], start=True, stop=False)
            def xn_T(t, s):
                pe.wait_ge(S["g_c"], t + 1)
                pe.wait_ge(S["g_xT"], t + FREE + 1)
                transpose(bank[0], xin[s]).then_inc(S["g_T"], 1)

            xn_T(0, 0)
            for t, s in tiles(pe):
                rows = LAST if isinstance(t, int) else P
                pe.wait_ge(S["g_xT"], t + READY)
                pe.wait_ge(S["g_kc"], t + 1)
                pe.wait_ge(S["g_vc"], t + 1)
                for b in range(2):
                    for k in range(2):
                        mm = pe.matmul(bank[6 + b][:, :], xT[s][:, k, :], wkv1[:, k, b * HW:(b + 1) * HW],
                                       start=(k == 0), stop=(k == 1))
                mm.then_inc(S["g_kvp"], 1)
                pe.wait_ge(S["g_ha"], t * 2 + 1)
                pe.wait_ge(S["g_hd"], t * 2 + 1)
                for q in range(4):
                    if q == 2 and not isinstance(t, int):
                        xn_T(t + 1, 1 - s)
                    for k in range(2):
                        mm = pe.matmul(bank[2 + q][:, :], xT[s][:, k, :], wr[:, k, q * 512:(q + 1) * 512],
                                       start=(k == 0), stop=(k == 1))
                    mm.then_inc(S["g_h"], 1)
                pe.wait_ge(S["g_kc"], t + 2)
                pe.wait_ge(S["g_vc"], t + 2)
                for p in range(4):
                    mm = pe.matmul(bank[1][:, p * P:(p + 1) * P], vc[0:rows, p * P:(p + 1) * P], kc[0:rows, p * P:(p + 1) * P],
                                   start=False, stop=False)
                mm.then_inc(S["g_dt"], 1)
            pe.matmul(bank[1][:, :], zeros[:, 0:P], zeros[:, :], start=False, stop=True).then_inc(S["g_dt"], 1)
            pe.wait_ge(S["g_dtr"], 1)
            pe.wait_ge(S["g_ha"], 2 * NT + 1)
            pe.wait_ge(S["g_hd"], 2 * NT + 1)
            for p in range(4):
                mm = pe.matmul(bank[2 + p // 2][:, (p % 2) * D:(p % 2 + 1) * D], DT[:, p, :], wout1[:, p, :],
                               start=True, stop=True)
            mm.then_inc(S["g_mp"], 1)
            pe.wait_ge(S["g_mps"], 1)
            for m in range(2):
                for p in range(4):
                    mm = pe.matmul(bank[4][:, m * D:(m + 1) * D], wqT1[:, p, m * P:(m + 1) * P], MP[:, p, :],
                                   start=(p == 0), stop=(p == 3))
            mm.then_inc(S["g_we"], 1)
            barrier()
            aggregate(2, D, [0, 1, 4, 5], {1: attn_T, 4: attn_out})
            barrier()
            def gate_T(t, s):
                pe.wait_ge(S["i_in"], t + (NT + READY))
                pe.wait_ge(S["i_xT"], t + (NT + FREE))
                transpose(bank[s], xin[s]).then_inc(S["i_T"], 1)

            gate_T(0, 0)
            for t, s in tiles(pe):
                if not isinstance(t, int):
                    gate_T(t + 1, 1 - s)
                pe.wait_ge(S["i_xT"], t + (NT + READY))
                for k in range(2):
                    mm = pe.matmul(bank[2][:, ds(t * NE, NE)], xT[s][:, k, :], wg1[:, k, :], start=(k == 0), stop=(k == 1))
                mm.then_inc(S["i_y"], 1)
            starts(2, P, NE, XCH)
            pe.matmul(bank[3][:, 0:XCH], zeros[:, 0:P], zeros[:, 0:XCH], start=True, stop=False)
            with pe.Fori(0, NT) as t:
                for k in range(TOP):
                    pe.wait_ge(perm_ready, t * TOP + (2 * EC + k + 1))
                    pe.matmul(bank[3][:, 0:XCH], itemA[k], itemR[k], start=False, stop=False).then_inc(perm_used, 1)
            pe.matmul(bank[3][:, 0:XCH], zeros[:, 0:P], zeros[:, 0:XCH], start=False, stop=True).then_inc(perm_done, 1)
            barrier()

            def xs_T(d, s, b, uses):
                pe.wait_ge(gathered[b], uses * 16 + 16 * (3 * TURNS + 1))
                pe.wait_ge(S["e_xT"], d + FREE)
                transpose(bank[s], xc[b]).then_inc(S["e_T"], 1)

            def second(d, s, start):
                pe.wait_ge(S["e_hT"], d + READY)
                pe.wait_ge(S["e_y"], d + FREE)
                for k in range(4):
                    mm = pe.matmul(bank[6 + s][:, 0:D], hT[s][:, k, :], WA[:, ds(start + (NE * WST + D * k), D)],
                                   start=(k == 0), stop=(k == 3))
                mm.then_inc(S["e_l2"], 1)

            xs_T(0, 0, 0, 0)
            for c, s, _, b, uses in chunks(pe):
                at, span = (0, 1) if isinstance(c, int) and c == 0 else (c - 1, 2)
                _, w = nc.values_load_multi_w_load_instructions(
                    wexp[0:1, ds(at, span)], engines=[mybir.EngineType.PE], min_val=0, max_val=(NE - 1) * WST,
                    skip_runtime_bounds_check_because="a minimum with the last expert's start bounds it")
                pe.wait_ge(S["e_xT"], c + READY)
                pe.wait_ge(S["e_h"], c + FREE)
                for k in range(2):
                    mm = pe.matmul(bank[2 + s][:, :], xT[s][:, k, :], WA[:, ds(w[-1] + HW * k, HW)], start=(k == 0), stop=(k == 1))
                mm.then_inc(S["e_l1"], 1)
                if not (isinstance(c, int) and c == XCH - 1):
                    xs_T(c + 1, 1 - s, b, uses)
                if not (isinstance(c, int) and c == 0):
                    second(c - 1, 1 - s, w[0])
                pe.wait_ge(S["e_h"], c + READY)
                pe.wait_ge(S["e_hT"], c + FREE)
                transpose(bank[4 + s], hs[s]).then_inc(S["e_Th"], 1)
            second(XCH - 1, 1, w[-1])
            barrier()


def kernel(**inputs):
    import numpy as _np
    import concourse.bacc as _bacc
    from concourse import mybir as _mybir
    from concourse.bass_utils import run_bass_kernel_spmd as _run

    a = {k: _np.asarray(v) for k, v in inputs.items()}
    cols = lambda v: v.reshape(-1, P).T
    laid = {k: v for k, v in a.items() if not k.startswith("L0_ffn_") or k[7:] in ("W1", "W2", "Wo", "Wr", "br", "bo")}
    for k in ("L0_gnn_W0", "L0_gnn_W1", "L1_gnn_weight", "L1_mix_w_qkv"):
        del laid[k]
    laid["W0T"], laid["W1T"] = a["L0_gnn_W0"].T, a["L0_gnn_W1"].T
    laid["WrT"] = a["L1_gnn_weight"].reshape(NE * D, D).T
    laid["wkv"], laid["wqT"] = a["L1_mix_w_qkv"][:, HW:], a["L1_mix_w_qkv"][:, :HW].T
    laid["bq"] = cols(laid.pop("L0_mix_bq"))
    laid["bn"] = _np.stack([cols(a["L0_ffn_" + n + k]) for k in "12" for n in ("b", "g", "be", "m", "v")], 1)
    nc = _bacc.Bacc("TRN2", target_bir_lowering=False, num_devices=1)
    arrays, T = {}, {}
    for name, v in laid.items():
        v = _np.ascontiguousarray(v)
        arrays[f"in_{name}"] = v
        T[name] = nc.dram_tensor(f"in_{name}", v.shape, _mybir.dt.from_np(v.dtype), kind="ExternalInput").ap()
    out = nc.dram_tensor("out_0", (N, D), F32, kind="ExternalOutput").ap()
    program(nc, T, out)
    r = _run(nc, [arrays], core_ids=[0])
    return r.results[0]["out_0"]
```

```python
from contextlib import ExitStack

import concourse.bass as bass
from concourse import mybir

P = 128
N = 3125
D = 256
E = 50000
NT = (N + P - 1) // P
LAST = N - (NT - 1) * P
GT = 4
NG = NT // GT
EP = 125
EC = E // EP
CH = 32
PART = 8
HOTS = 16
LOADS = 8
UNIT = CH // 2
NCH = (E + NT * (P - 1)) // P
TURNS = (NCH + CH - 1) // CH
SLOTS = TURNS * CH
ROW = D + 4
DS = D + 2
NE = 8
HW = 512
HEAD0 = D // NE
HEAD1 = HW // NE
PSB = 2
COLS = 5
HCOLS = 2
SHARED = (1, 3)
ROUNDS = 2
CPT = 16
C0 = TURNS * CPT
assert TURNS == NT // 2 + 1 and EC - C0 == (TURNS - 1) * CPT
TOP = 2
ITEMS = TOP * NT
XCH = (TOP * N + NE * (P - 1)) // P
XB = 6
assert XCH % XB == 2
WST = 2 * HW
BST = HW + D
OG = 5
assert NT % OG == 0
LN_EPS = 1e-5
BN_EPS = 1e-3

F32 = mybir.dt.float32
F16 = mybir.dt.float16
I32 = mybir.dt.int32
U32 = mybir.dt.uint32
ALU = mybir.AluOpType
ACT = mybir.ActivationFunctionType
AX = mybir.AxisListType
ds = bass.ds


class Steps:

    def __init__(self, eng, sem):
        self.eng, self.sem, self.base = eng, sem, 0
        self.t = self.per = self.k = 0

    def did(self, ins):
        ins.then_inc(self.sem, 1)
        self.k += 1

    def count(self):
        return self.t * self.per + (self.base + self.k)

    def wait(self, but=0):
        self.eng.wait_ge(self.sem, self.count() - but)

    def link(self, ins):
        self.did(ins)
        self.wait()

    def turn(self, t, per):
        if not self.per:
            self.base, self.k = self.base + self.k, 0
        assert not self.per or self.k == self.per, (self.k, self.per)
        self.t, self.per, self.k = t, per, 0

    def ended(self, turns):
        assert self.k == self.per, (self.k, self.per)
        self.base, self.t, self.per, self.k = self.base + turns * self.per, 0, 0, 0


def tiles(eng):
    with eng.Fori(0, NT // 2) as i:
        for s in range(2):
            yield i * 2 + s, s
    yield NT - 1, 0


def groups(eng):
    with eng.Fori(0, NG - 1) as g:
        yield g, GT, GT
    yield NG - 1, GT, NT - NG * GT
    yield NG, NT - NG * GT, 0


def turns(eng):
    with eng.Fori(0, TURNS - 1) as i:
        yield i, 2
    yield TURNS - 1, 1


def chunks(eng):
    yield 0, 0, 0, 1, 0
    with eng.Fori(0, XCH // XB) as i:
        for u in range(XB):
            yield i * XB + (1 + u), (1 + u) % 2, i * (XB // 2) + u // 2, (2 + u) % XB, i + (2 + u) // XB
    yield XCH - 1, 1, (XCH - 2) // 2, 0, 0


def beside(work, i, tiles_here, s):
    u = s // UNIT
    if u < tiles_here and s % UNIT in work:
        work[s % UNIT](i * 2 + u, u)


def program(nc, T, out):
    with ExitStack() as ctx:
        def sb(name, shape, dt=F32):
            return ctx.enter_context(nc.sbuf_tensor(name, shape, dt))

        def sem(name):
            return ctx.enter_context(nc.semaphore(name))

        def dram(name, shape):
            return nc.dram_tensor(name, shape, F32, kind="Internal").ap()

        bank = [ctx.enter_context(nc.psum_tensor(f"bank{i}", [P, 512], F32)) for i in range(8)]

        table0 = dram("table0", (NT * P, ROW))
        table1 = dram("table1", (NT * P, D))
        hall = dram("hall", (NE * N, D))
        ys = dram("ys", (XCH * P, D))

        X = sb("X", [P, (NT + 1) * D])
        XN = sb("XN", [P, NT * ROW])
        AGG = sb("AGG", [P, (NT + 1) * DS])
        STAT = sb("STAT", [P, NT * 6])
        MV = sb("MV", [P, 8, NT + 1])
        IDX = [sb(f"IDX{i}", [P, SLOTS], I32) for i in range(2)]
        LOC = [sb(f"LOC{i}", [P, SLOTS]) for i in range(2)]
        TIL = [sb(f"TIL{i}", [P, SLOTS], I32) for i in range(2)]
        idxb = sb("idxb", [P, CH], I32)
        ident = sb("ident", [P, P])
        tri = sb("tri", [P, P])
        trin = sb("trin", [P, P])
        ones = sb("ones", [P, P])
        zeros = sb("zeros", [P, 512])
        iotai = sb("iotai", [P, SLOTS], I32)
        iota = sb("iota", [P, SLOTS])
        iota16 = sb("iota16", [P, SLOTS], F16)
        bias = sb("bias", [P, 9, D])
        small = sb("small", [P, 384])
        WA = sb("WA", [P, 16384])
        RA = sb("RA", [P, 7296])

        def view(arena, at, shape):
            n = 1
            for k in shape:
                n *= k
            v = arena[:, at:at + n]
            if len(shape) == 2:
                return v.rearrange("p (a b) -> p a b", b=shape[1])
            if len(shape) == 3:
                return v.rearrange("p (a b c) -> p a b c", b=shape[1], c=shape[2])
            return v

        w1 = view(WA, 0, (NE, 2, D))
        w2 = view(WA, 4096, (NE, 2, D))
        wo = view(WA, 8192, (NE, 2, D))
        gw = [view(WA, 12288 + 1024 * i, (4, D)) for i in range(2)]
        wkv0 = view(WA, 14336, (2, 512))
        wq0 = view(WA, 15360, (2, D))
        wo0 = view(WA, 15872, (2, D))
        wr = view(WA, 12288, (2, NE * D))
        wkv1 = view(AGG, 0, (2, 2 * HW))
        wqT1 = view(AGG, 2048, (4, D))
        wout1 = view(AGG, 3072, (4, D))
        DT = view(AGG, 4096, (4, P))
        MP = view(AGG, 4608, (4, D))
        WEFF = view(AGG, 5632, (2, D))
        v1 = view(WA, 0, (NE, 2, HW))
        v2 = view(WA, 8192, (NE, 4, D))
        bo_e = sb("bo_e", [NE, D])
        wr0 = sb("wr0", [P, 2, NE])
        wg1 = sb("wg1", [P, 2, NE])
        gate_b = sb("gate_b", [P, 3, NE])
        bn = sb("bn", [P, 10, 2 * NE])
        sc = sb("sc", [P, 4, 2 * NE])
        beyond = sb("beyond", [P, 1])
        rowi, rowf = sb("rowi", [P, 1], I32), sb("rowf", [P, 1])
        bq = sb("bq", [P, 2])
        kvbd = sb("kvbd", [P, 2, D + NE])

        pos = AGG[:, 400:800]
        scan = [AGG[:, 800:1200], AGG[:, 1200:1600], IDX[1][:, 0:EC].bitcast(F32)]
        tmpi = [AGG[:, 1600 + 400 * i:2000 + 400 * i].bitcast(I32) for i in range(5)]
        tmpf = [AGG[:, 3600 + 400 * i:4000 + 400 * i] for i in range(6)]
        moves = [AGG[:, 4400:6000], WA[:, 10368:11968]]
        rooms = [(WA, 8320, 9), (RA, 3500, 8), (AGG, 4400, 4), (AGG, 0, 1), (AGG, 6000, 1), (RA, 2560, 1), (LOC[1], 0, 1)]
        oh = [a[:, at + EC * k:at + EC * (k + 1)] for a, at, n in rooms for k in range(n)]
        assert len(oh) == NT
        minus = [[AGG[:, 3600:4000], AGG[:, 4000:4400]], [IDX[1][:, 0:EC].bitcast(F32), LOC[1][:, 0:EC]]]
        away = [RA[:, 6928 + 64 * s:6992 + 64 * s].bitcast(F16) for s in range(2)]
        edges = [RA[:, 400 * i:400 * i + 400].bitcast(I32) for i in range(3)]
        permA = [RA[:, 1200 + 128 * s:1328 + 128 * s].bitcast(F16) for s in range(COLS)]
        permR = [RA[:, 1840 + 208 * s:2048 + 208 * s].bitcast(F16) for s in range(COLS)]
        permA1 = [RA[:, 6192 + 128 * s:6320 + 128 * s].bitcast(F16) for s in range(HCOLS)]
        permR1 = [RA[:, 6448 + 208 * s:6656 + 208 * s].bitcast(F16) for s in range(HCOLS)]
        cnt = small[:, 0:NT]
        z16 = RA[:, 6864:6928].bitcast(F16)
        ring = view(WA, 0, (CH, ROW))
        hot = view(WA, CH * ROW, (HOTS, P))
        xin = [RA[:, 256 * s:256 * s + 256] for s in range(2)]
        xT = [view(RA, 512 + 256 * s, (2, P)) for s in range(2)]
        kb = [RA[:, 1024 + 256 * s:1280 + 256 * s] for s in range(2)]
        eb = [RA[:, 1536 + 256 * s:1792 + 256 * s] for s in range(2)]
        mb = [RA[:, 2048 + 256 * s:2304 + 256 * s] for s in range(2)]
        kf = [RA[:, 2560 + 256 * s:2816 + 256 * s] for s in range(2)]
        vb = [RA[:, 3072 + 258 * s:3330 + 258 * s] for s in range(2)]
        of = [RA[:, 3600 + 256 * s:3856 + 256 * s] for s in range(2)]
        oT = [view(RA, 4112 + 256 * s, (2, P)) for s in range(2)]
        nr = [RA[:, 4624 + 16 * s:4640 + 16 * s] for s in range(2)]
        cT = [view(RA, 4656 + 512 * s, (4, P)) for s in range(2)]
        nb = [RA[:, 5680 + 256 * s:5936 + 256 * s] for s in range(2)]
        ho = [RA[:, 1024 + 2048 * s:3072 + 2048 * s] for s in range(2)]
        sq = RA[:, 5120:6144]
        kc = RA[:, 6144:6656]
        vc = RA[:, 6656:7168]
        rs = RA[:, 7168:7232]
        xg = view(RA, 0, (2, GT * P))
        xgin = view(RA, 1024, (GT, D))
        h1 = [view(RA, 2048 + 1024 * s, (2, GT * P)) for s in range(2)]
        h2 = [view(RA, 4096 + 1024 * s, (2, GT * P)) for s in range(2)]
        rt = view(RA, 6144, (8, GT * NE))
        wT = RA[0:NE, 6400:6400 + GT * P]
        hs = [RA[:, 1024 + 512 * s:1536 + 512 * s] for s in range(2)]
        hT = [view(RA, 2048 + 512 * s, (4, P)) for s in range(2)]
        yo = [RA[:, 3072 + 256 * s:3328 + 256 * s] for s in range(2)]
        logits, best = view(RA, 3600, (NT, NE)), view(RA, 3800, (NT, NE))
        bestat = RA[:, 4000:4200].bitcast(U32).rearrange("p (t e) -> p t e", e=NE)
        chosen = view(RA, 4200, (TOP, NT))
        mask = view(RA, 4300, (NE, ITEMS))
        rank = [RA[:, 4700 + 50 * s:4700 + 50 * s + ITEMS] for s in range(2)]
        ipos = RA[:, 4800:4800 + ITEMS]
        slot_token = IDX[0][:, 0:XCH]
        item_slot = IDX[0][:, 64:64 + ITEMS]
        itemi = [RA[:, 5360 + 50 * k:5360 + 50 * k + ITEMS].bitcast(I32) for k in range(3)]
        itemf = [RA[:, 5520 + 50 * k:5520 + 50 * k + ITEMS] for k in range(2)]
        tokens = RA[:, 5620:5620 + NT]
        itemA = [RA[:, 4860 + P * k:4860 + P * (k + 1)] for k in range(TOP)]
        itemR = [RA[:, 5120 + 64 * k:5120 + 64 * k + XCH] for k in range(TOP)]
        xc = [RA[:, 3600 + 256 * b:3856 + 256 * b] for b in range(XB)]
        wexp, bexp = TIL[0], TIL[1]
        eb1 = view(AGG, 0, (NE, BST))
        yr = [view(XN, 0, (NT, ROW)), view(RA, 0, (NT, D))]

        def xt(t):
            return X[:, ds(t * D, D)]

        consts = sem("consts")
        pool_step, dve_step = sem("pool_step"), sem("dve_step")
        phase = sem("phase")
        x_in = sem("x_in")
        edges_in = sem("edges_in")
        w_in = sem("w_in")
        stored = sem("stored")
        hall_stored = [sem(f"hall_stored{s}") for s in range(2)]
        out_stored = sem("out_stored")
        x_pad = sem("x_pad")
        ys_stored = [sem(f"ys_stored{s}") for s in range(2)]
        var_ready, std_ready = sem("var_ready"), sem("std_ready")
        counts_ready, prefix_ready = sem("counts_ready"), sem("prefix_ready")
        nch_ready, chend_ready, ge_ready, til_ready = (sem(n) for n in ("nch_ready", "chend_ready", "ge_ready", "til_ready"))
        perm_ready, perm_used, perm_done = sem("perm_ready"), sem("perm_used"), sem("perm_done")
        moves_ready, abs_ready, place_ready = sem("moves_ready"), sem("abs_ready"), sem("place_ready")
        idx_ready, hot_ready = sem("idx_ready"), sem("hot_ready")
        gathered = [sem(f"gathered{s}") for s in range(CH)]
        summed = sem("summed")
        added = sem("added")

        class Barrier:
            def __init__(self, eng):
                self.eng, self.n = eng, 0

            def __call__(self, wait=True):
                self.n += 1
                self.eng.drain().then_inc(phase, 1)
                if wait:
                    self.eng.wait_ge(phase, 5 * self.n)

        S = {n: sem(n) for n in (
            "stats_ready kv_k_exp_capped q_reciprocal q_denominator kv_x_loaded kv_x_transposed kv_xT_copied "
            "kv_products kv_v_biased kv_k_biased kv_k_exp kv_k_feature kv_tile_summed kv_done q_x_loaded "
            "q_x_transposed q_xT_copied q_products q_biased q_exp q_feature_ready q_kv_products q_normalised "
            "q_out_transposed q_outT_copied q_out_products q_added gnn_x_loaded gnn_mean_ready "
            "gnn_transposed gnn_copied gnn_products gnn_row_ready ffn_x_normalised ffn_x_transposed "
            "ffn_xT_copied ffn_gate_products ffn_gate_less_max ffn_gate_exp ffn_gates_ready "
            "ffn_gates_transposed ffn_gatesT_copied ffn_bias_products ffn_bias_added ffn_first_products "
            "ffn_first_relu ffn_second_products ffn_second_relu ffn_third_products ffn_expert_added "
            "kv1_weights_centred kv1_x_normalised kv1_x_loaded kv1_x_transposed kv1_xT_copied kv1_products "
            "hall_products hall_copied_by_act hall_copied_by_dve kv1_squared kv1_var_ready kv1_std_ready "
            "kv1_k_scaled kv1_v_copied kv1_tile_summed fold_kv_ready fold_first_products fold_first_copied "
            "fold_second_products tile_x_loaded tile_x_transposed tile_xT_copied tile_products attn1_added "
            "gate_x_normalised gate_difference gate_exp chunk_x_transposed chunk_xT_copied "
            "chunk_first_products chunk_first_biased chunk_h_transposed chunk_hT_copied "
            "chunk_second_products chunk_output_ready output_ready").split()}
        CREDIT = {
            "act": {"kv_x_loaded": 2, "kv_xT_copied": 2, "kv_k_exp": 2, "q_x_loaded": 2, "q_xT_copied": 2,
                    "q_outT_copied": 2, "gnn_x_loaded": 2, "gnn_copied": 2, "ffn_first_relu": 2,
                    "ffn_second_relu": 2, "kv1_v_copied": 1, "hall_copied_by_act": 1, "kv1_xT_copied": 2,
                    "tile_x_loaded": 2, "tile_xT_copied": 2, "chunk_xT_copied": 2, "chunk_hT_copied": 2},
            "pe": {"kv_x_transposed": 2, "kv_products": 2, "kv_tile_summed": 2, "q_x_transposed": 2,
                    "q_products": 2, "q_kv_products": 2, "q_out_transposed": 2, "q_out_products": 2,
                    "gnn_transposed": 2, "gnn_products": 2, "ffn_second_products": 3, "ffn_x_transposed": 1,
                    "kv1_tile_summed": 1, "hall_products": 5, "ffn_first_products": 1, "ffn_third_products": 2,
                    "kv1_x_transposed": 2, "tile_x_transposed": 2, "tile_products": 2, "chunk_x_transposed": 2,
                    "chunk_first_products": 2, "chunk_h_transposed": 2, "chunk_second_products": 2},
            "dve": {"kv_v_biased": 2, "kv_k_feature": 2, "q_feature_ready": 2, "q_normalised": 2, "q_added": 2,
                    "gnn_mean_ready": 2, "gnn_row_ready": 2, "kv1_x_normalised": 2, "kv1_var_ready": 1,
                    "ffn_bias_added": 1, "ffn_expert_added": 1, "kv1_k_scaled": 1, "hall_copied_by_dve": 1,
                    "chunk_first_biased": 2, "chunk_output_ready": 2, "attn1_added": 2},
        }
        FREE, READY = 1, 3

        def wait_alone(eng, signal, value):
            if not isinstance(value, int):
                value = eng.to_reg(value)
                eng.wait_ge(consts, 6)
            eng.wait_ge(signal, value)

        block = ctx.enter_context(nc.Block())

        @block.sync
        def _(sp):
            barrier = Barrier(sp)
            for s in range(2):
                sp.sem_inc(hall_stored[s], 16)
            sp.wait_ge(x_pad, 1)
            sp.dma_start(X[:, 0:(NT - 1) * D].rearrange("p (t d) -> p t d", d=D),
                         T["x"][0:(NT - 1) * P, :].rearrange("(t p) d -> p t d", p=P)).then_inc(x_in, 16)
            sp.dma_start(X[0:LAST, (NT - 1) * D:NT * D], T["x"][(NT - 1) * P:N, :]).then_inc(x_in, 16)
            for i, n in enumerate(("src", "dst", "edge_type_8")):
                sp.dma_start(edges[i][0:EP, :], T[n].rearrange("(p c) -> p c", c=EC)).then_inc(edges_in, 16)
            for i, n in enumerate(("L0_mix_bk", "L0_mix_bv", "L0_mix_bo", "L0_gnn_b0", "L0_gnn_b1", "L1_gnn_bias", "L1_mix_b_out")):
                sp.dma_start(bias[:, i, :], T[n].partition_broadcast(P)).then_inc(w_in, 16)
            sp.dma_start(bq[:, :], T["bq"]).then_inc(w_in, 16)
            for i, n in enumerate(("L0_ffn_br", "L1_ffn_bg", "L1_ffn_bias")):
                sp.dma_start(gate_b[:, i, :], T[n].partition_broadcast(P)).then_inc(w_in, 16)
            sp.dma_start(bn[:, :, :], T["bn"]).then_inc(w_in, 16)
            sp.dma_start(bo_e[:, :], T["L0_ffn_bo"]).then_inc(w_in, 16)
            sp.dma_start(wr0[:, :, :], T["L0_ffn_Wr"].rearrange("(k p) n -> p k n", p=P)).then_inc(w_in, 16)
            sp.dma_start(wg1[:, :, :], T["L1_ffn_Wg"].rearrange("(k p) n -> p k n", p=P)).then_inc(w_in, 16)
            for dst, n in ((gw[0], "W0T"), (gw[1], "W1T"), (wkv0[:, :, 0:D], "L0_mix_wk"), (wkv0[:, :, D:2 * D], "L0_mix_wv"),
                           (wq0, "L0_mix_wq"), (wo0, "L0_mix_wo")):
                sp.dma_start(dst, T[n].rearrange("(k p) n -> p k n", p=P)).then_inc(w_in, 16)
            barrier()
            sp.dma_start(table0.rearrange("(t p) d -> p t d", p=P),
                         XN[:, :].rearrange("p (t d) -> p t d", d=ROW)).then_inc(stored, 16)
            sp.wait_ge(stored, 16)
            barrier()
            barrier()
            barrier()
            sp.dma_start(table1.rearrange("(t p) d -> p t d", p=P),
                         XN[:, :].rearrange("p (t d) -> p t d", d=ROW)[:, :, 0:D]).then_inc(stored, 16)
            sp.wait_ge(stored, 32)
            barrier()
            barrier()
            for e in range(NE):
                for dst, n in ((w1, "L0_ffn_W1"), (w2, "L0_ffn_W2"), (wo, "L0_ffn_Wo")):
                    sp.dma_start(dst[:, e, :, :], T[n][e].rearrange("(k p) n -> p k n", p=P)).then_inc(w_in, 16)
            sp.wait_ge(w_in, 16 * (21 + 3 * NE))
            barrier()
            for dst, n in ((wr, "WrT"), (wkv1, "wkv"), (wqT1, "wqT"), (wout1, "L1_mix_w_out")):
                sp.dma_start(dst, T[n].rearrange("(k p) n -> p k n", p=P)).then_inc(w_in, 16)
            sp.wait_ge(w_in, 16 * (25 + 3 * NE))
            barrier()
            hall_v = hall.rearrange("(r n) d -> n r d", n=N)
            for t, s in tiles(sp):
                rows = LAST if isinstance(t, int) else P
                sp.wait_ge(S["hall_copied_by_act"], t * 2 + 2 + 1)
                sp.wait_ge(S["hall_copied_by_dve"], t * 2 + 2 + 1)
                if rows == P:
                    src = hall_v[ds(t * P, P), :, :]
                else:
                    src = hall_v[(NT - 1) * P:N, :, :]
                sp.dma_start(src, ho[s][0:rows, :].rearrange("p (r d) -> p r d", r=NE)).then_inc(hall_stored[s], 16)
            sp.wait_ge(hall_stored[0], 16 * 14)
            sp.wait_ge(hall_stored[1], 16 * 13)
            barrier()
            barrier()
            for e in range(NE):
                sp.dma_start(v1[:, e, :, :], T["L1_ffn_W1"][e].rearrange("(k p) n -> p k n", p=P)).then_inc(w_in, 16)
                sp.dma_start(v2[:, e, :, :], T["L1_ffn_W2"][e].rearrange("(k p) n -> p k n", p=P)).then_inc(w_in, 16)
                sp.dma_start(eb1[:, e, 0:HW], T["L1_ffn_b1"][e].partition_broadcast(P)).then_inc(w_in, 16)
                sp.dma_start(eb1[:, e, HW:BST], T["L1_ffn_b2"][e].partition_broadcast(P)).then_inc(w_in, 16)
            sp.wait_ge(S["gate_x_normalised"], NT)
            sp.dma_start(table1.rearrange("(t p) d -> p t d", p=P),
                         XN[:, :].rearrange("p (t d) -> p t d", d=ROW)[:, :, 0:D]).then_inc(stored, 16)
            sp.wait_ge(stored, 48)
            sp.wait_ge(w_in, 16 * (25 + 7 * NE))
            barrier()
            for s in range(2):
                sp.sem_inc(ys_stored[s], 16)
            for c, s, before, _, _ in chunks(sp):
                if not (isinstance(c, int) and c == 0):
                    sp.wait_ge(S["chunk_output_ready"], c + (READY - 1))
                    sp.dma_start(ys[ds(c * P - P, P), :], yo[1 - s]).then_inc(ys_stored[1 - s], 16)
            sp.wait_ge(S["chunk_output_ready"], XCH - 1 + READY)
            sp.dma_start(ys[(XCH - 1) * P:XCH * P, :], yo[1]).then_inc(ys_stored[1], 16)
            for s in range(2):
                sp.wait_ge(ys_stored[s], 16 * (XCH // 2 + 1))
            barrier()
            for g in range(NT // OG):
                sp.wait_ge(S["output_ready"], g + 1)
                a, b = g * OG, min((g + 1) * OG, NT - 1)
                sp.dma_start(out[a * P:b * P, :].rearrange("(t p) d -> p t d", p=P),
                             X[:, a * D:b * D].rearrange("p (t d) -> p t d", d=D)).then_inc(out_stored, 16)
            sp.dma_start(out[(NT - 1) * P:N, :], X[0:LAST, (NT - 1) * D:NT * D]).then_inc(out_stored, 16)
            sp.wait_ge(out_stored, 16 * (NT // OG + 1))

        @block.gpsimd
        def _(pool):
            barrier = Barrier(pool)
            pool.memset(X[:, (NT - 1) * D:(NT + 1) * D], 0.0).then_inc(x_pad, 1)
            pool.memset(ident[:, :], 0.0).then_inc(pool_step, 1)
            pool.memset(ones[:, :], 1.0).then_inc(pool_step, 1)
            pool.memset(zeros[:, :], 0.0).then_inc(consts, 1)
            pool.iota(rowi[:, :], pattern=[[0, 1]], base=0, channel_multiplier=1).then_inc(pool_step, 1)
            pool.memset(XN[:, :].rearrange("p (t d) -> p t d", d=ROW)[:, :, D:ROW], 1.0).then_inc(consts, 1)
            pool.iota(iotai[:, :], pattern=[[1, SLOTS]], base=0, channel_multiplier=0).then_inc(consts, 1)
            pool.wait_ge(pool_step, 3)
            pool.affine_select(out=ident[:, :], in_=ident[:, :], compare_op=ALU.not_equal, fill=1.0, base=0,
                               pattern=[[-1, P]], channel_multiplier=1).then_inc(consts, 1)
            pool.affine_select(out=tri[:, :], in_=ones[:, :], compare_op=ALU.is_gt, fill=0.0, base=0,
                               pattern=[[1, P]], channel_multiplier=-1).then_inc(consts, 1)
            pool.affine_select(out=trin[:, :], in_=ones[:, :], compare_op=ALU.is_ge, fill=0.0, base=0,
                               pattern=[[1, P]], channel_multiplier=-1).then_inc(consts, 1)
            barrier()
            barrier(wait=False)
            pool.wait_ge(stored, 16)

            def gather(layer, table, cols):
                with pool.Fori(0, TURNS) as i:
                    for q in range(CH // PART):
                        wait_alone(pool, idx_ready, (i + TURNS * layer) * (CH // PART) + (q + 1))
                        for s in range(q * PART, (q + 1) * PART):
                            pool.indirect_dma_start(out=ring[:, s, 0:cols], out_offset=None, in_=table,
                                                    in_offset=bass.IndirectOffsetOnAxis(ap=idxb[:, s:s + 1], axis=0)
                                                    ).then_inc(gathered[s], 16)

            gather(0, table0[:, :], ROW)
            barrier()
            barrier()
            barrier()
            gather(1, table1[:, :], D)
            for _ in range(4):
                barrier()
            gather(2, hall[:, :], D)
            barrier()
            barrier()
            for c in range(XCH):
                if c >= XB:
                    pool.wait_ge(S["chunk_x_transposed"], c - XB + READY)
                pool.indirect_dma_start(out=xc[c % XB], out_offset=None, in_=table1,
                                        in_offset=bass.IndirectOffsetOnAxis(ap=slot_token[:, c:c + 1], axis=0)
                                        ).then_inc(gathered[c % XB], 16)
            barrier()
            for g in range(NT // OG):
                for t in range(g * OG, (g + 1) * OG):
                    for k in range(TOP):
                        pool.indirect_dma_start(out=yr[k][:, t, 0:D], out_offset=None, in_=ys,
                                                in_offset=bass.IndirectOffsetOnAxis(ap=item_slot[:, k * NT + t:k * NT + t + 1], axis=0)
                                                ).then_inc(gathered[g], 16)

        @block.vector
        def _(dve):
            barrier = Barrier(dve)
            st = Steps(dve, dve_step)
            for name, k in CREDIT["dve"].items():
                dve.sem_inc(S[name], k)
            dve.sem_inc(added, PSB)

            def moments(t):
                return dve.bn_stats(STAT[:, ds(t * 6, 6)], xt(t))

            def all_moments():
                with dve.Fori(0, NT // OG) as i:
                    st.turn(i, OG)
                    for j in range(OG):
                        st.did(moments(i * OG + j))
                st.ended(NT // OG)

            def stats(n):
                st.wait()
                f = STAT[:, :].rearrange("p (t c) -> p c t", c=6)
                st.did(dve.tensor_tensor(MV[:, 2, 0:NT], f[:, 1, :], f[:, 4, :], ALU.add))
                st.did(dve.tensor_tensor(MV[:, 3, 0:NT], f[:, 1, :], f[:, 4, :], ALU.subtract))
                st.link(dve.tensor_tensor(MV[:, 4, 0:NT], f[:, 2, :], f[:, 5, :], ALU.add))
                st.did(dve.tensor_scalar(MV[:, 0, 0:NT], MV[:, 2, 0:NT], 0.5, None, ALU.mult))
                st.link(dve.scalar_tensor_tensor(MV[:, 5, 0:NT], MV[:, 3, 0:NT], 0.25, MV[:, 3, 0:NT], ALU.mult, ALU.mult))
                st.link(dve.scalar_tensor_tensor(MV[:, 6, 0:NT], MV[:, 4, 0:NT], 1.0 / D, MV[:, 5, 0:NT], ALU.mult, ALU.add))
                dve.tensor_scalar(MV[:, 7, 0:NT], MV[:, 6, 0:NT], LN_EPS, None, ALU.add).then_inc(var_ready, 1)
                dve.wait_ge(std_ready, n)
                st.link(dve.reciprocal(MV[:, 1, 0:NT], MV[:, 2, 0:NT]))
                st.did(dve.scalar_tensor_tensor(MV[:, 4, 0:NT], MV[:, 0, 0:NT], -1.0, MV[:, 1, 0:NT], ALU.mult, ALU.mult))

            def norm(dst, t):
                return dve.tensor_scalar(dst, xt(t), MV[:, 0, ds(t, 1)], MV[:, 1, ds(t, 1)], ALU.subtract, ALU.mult)

            dve.wait_ge(consts, 6)
            st.did(dve.tensor_copy(iota[:, :], iotai[:, :]))
            st.did(dve.tensor_copy(iota16[:, :], iotai[:, :]))
            dve.wait_ge(pool_step, 3)
            st.did(dve.tensor_copy(rowf[:, :], rowi[:, :]))
            st.link(dve.tensor_scalar(beyond[:, :], rowi[:, :], float(LAST), 16.0, ALU.is_ge, ALU.mult))
            dve.wait_ge(x_in, 32)
            all_moments()
            stats(1)
            st.wait()
            dve.drain().then_inc(S["stats_ready"], 1)
            barrier(wait=False)

            def indices(n, i, q):
                dve.tensor_copy(idxb[:, q * PART:(q + 1) * PART], IDX[n][:, ds(i * CH + q * PART, PART)]
                                ).then_inc(idx_ready, 1)

            def starts(n, bins, slots):
                c = [small[:, 32 * k:32 * k + bins] for k in range(1, 6)]
                ci = [small[:, 256 + 32 * k:256 + 32 * k + bins].bitcast(I32) for k in range(2)]
                r, ri = small[0:bins, 224:226], small[0:bins, 320:322].bitcast(I32)
                st.wait()
                dve.drain().then_inc(counts_ready, 1)
                dve.wait_ge(prefix_ready, n + 1)
                st.link(dve.tensor_scalar(ci[0], bank[0][:, 32:32 + bins], float(P - 1), None, ALU.add))
                st.link(dve.tensor_scalar(ci[1], ci[0], 7, None, ALU.logical_shift_right))
                st.link(dve.tensor_copy(c[0], ci[1]))
                st.link(dve.tensor_tensor_scan(c[1], c[0], zeros[:, 0:bins], 0.0, ALU.add, ALU.add))
                st.link(dve.tensor_tensor(c[2], c[1], c[0], ALU.subtract))
                st.link(dve.scalar_tensor_tensor(c[3], c[2], float(P), bank[0][:, 0:bins], ALU.mult, ALU.add))
                st.link(dve.tensor_scalar(c[4], c[3], -1.0, None, ALU.add))
                st.link(dve.tensor_scalar(ri[:, 0:1], bank[0][0:bins, 64:65], float(P - 1), None, ALU.add))
                st.link(dve.tensor_scalar(ri[:, 1:2], ri[:, 0:1], 7, None, ALU.logical_shift_right))
                dve.tensor_copy(r[:, 0:1], ri[:, 1:2]).then_inc(nch_ready, 1)
                dve.wait_ge(chend_ready, n + 1)
                st.link(dve.tensor_copy(r[:, 1:2], bank[0][0:bins, 66:67]))
                dve.tensor_scalar(RA[0:bins, 3000:3000 + slots], iota[0:bins, 0:slots], r[:, 1:2], None,
                                  ALU.is_ge).then_inc(ge_ready, 1)
                dve.wait_ge(til_ready, n + 1)
                return c[4]

            def place(n):
                key, other = edges[n][0:EP, :], edges[1 - n][0:EP, :]
                f = [a[0:EP, :] for a in tmpf]
                m = [moves[n][0:EP, EC * k:EC * (k + 1)] for k in range(4)]
                g = [a[0:EP, :] for a in tmpi]
                st.did(dve.tensor_scalar(g[0], key, 7, None, ALU.logical_shift_right))
                st.link(dve.tensor_scalar(g[1], key, P - 1, None, ALU.bitwise_and))
                st.did(dve.tensor_copy(f[0], g[0]))
                st.link(dve.tensor_copy(f[1], g[1]))
                for b in range(NT):
                    st.did(dve.tensor_scalar(oh[b][0:EP, :], f[0], float(b), 0.0, ALU.is_equal, ALU.add,
                                             accum_out=cnt[0:EP, b:b + 1]))
                c = starts(n, NT, SLOTS)
                st.did(dve.tensor_scalar(TIL[n][:, :], bank[1][:, 0:SLOTS], float((DS, D)[n]), None, ALU.mult))
                st.link(dve.memset(pos, 0.0))

                def count(b):
                    st.did(dve.tensor_tensor_scan(scan[b % 3][0:EP, :], oh[b][0:EP, :], zeros[0:EP, 0:EC],
                                                  c[0:EP, b:b + 1], ALU.add, ALU.add))

                count(0)
                for b in range(NT):
                    if b + 1 < NT:
                        count(b + 1)
                    st.wait(but=int(b + 1 < NT))
                    st.did(dve.copy_predicated(pos[0:EP, :], oh[b][0:EP, :].bitcast(I32), scan[b % 3][0:EP, :]))
                st.wait()
                st.link(dve.tensor_copy(g[2], pos[0:EP, :]))
                st.did(dve.tensor_scalar(g[3], g[2], P - 1, None, ALU.bitwise_and))
                st.link(dve.tensor_scalar(g[4], g[2], 7, None, ALU.logical_shift_right))
                st.did(dve.tensor_copy(m[0], g[3]))
                st.did(dve.tensor_copy(m[1], g[4]))
                if n == 0:
                    st.link(dve.tensor_copy(m[2], other))
                else:
                    st.link(dve.scalar_tensor_tensor(m[2], edges[2][0:EP, :], float(N), other, ALU.mult, ALU.add))
                st.link(dve.tensor_scalar(m[3], m[2], 1.0, float(P), ALU.add, ALU.mult))
                st.link(dve.tensor_tensor(g[0], m[3], f[1], ALU.add))
                st.did(dve.tensor_scalar(g[1], g[0], 11, None, ALU.logical_shift_right))
                st.link(dve.tensor_scalar(g[2], g[0], 2047, None, ALU.bitwise_and))
                st.did(dve.tensor_copy(m[2], g[1]))
                st.link(dve.tensor_copy(m[3], g[2]))
                for k in range(2):
                    ins = dve.tensor_scalar(minus[n][k][0:EP, :], m[2 + k], -1.0, None, ALU.mult)
                ins.then_inc(moves_ready, 1)
                dve.wait_ge(moves_ready, n + 1)
                if n == 0:
                    st.link(dve.memset(z16, 0.0))

            def column(n, c, free, A, R, shared):
                q, r, hi, lo = (moves[n][0:EP, ds(c + EC * k, 1)] for k in range(4))
                dve.wait_ge(perm_used, free)
                if not shared:
                    dve.tensor_scalar(A[0:EP, 0:P], iota16[0:EP, 0:P], q, hi, ALU.is_equal, ALU.mult)
                    dve.tensor_scalar(A[0:EP, P:2 * P], iota16[0:EP, 0:P], q, lo, ALU.is_equal, ALU.mult)
                dve.tensor_scalar(R[0:EP, :], iota16[0:EP, :], r, None, ALU.is_equal).then_inc(perm_ready, 1)

            def moved(n, bank_hi, bank_lo):
                dve.wait_ge(perm_done, n + 1)
                hif, lof, vf = RA[:, 3500:3500 + SLOTS], RA[:, 3916:3916 + SLOTS], RA[:, 4332:4332 + SLOTS]
                vi, ri, li = (RA[:, 4748 + SLOTS * k:4748 + SLOTS * (k + 1)].bitcast(I32) for k in range(3))
                st.link(dve.tensor_copy(lof, bank_lo[:, 0:SLOTS]))
                st.link(dve.scalar_tensor_tensor(vf, bank_hi[:, 0:SLOTS], 2048.0, lof, ALU.mult, ALU.add))
                st.link(dve.tensor_copy(vi, vf))
                st.did(dve.tensor_scalar(ri, vi, 7, None, ALU.logical_shift_right))
                st.did(dve.tensor_scalar(li, vi, P - 1, None, ALU.bitwise_and))
                st.link(dve.tensor_scalar(hif, vf, float(P), None, ALU.is_lt))
                st.link(dve.tensor_scalar(IDX[n][:, :], ri, -1.0, 0.0, ALU.add, ALU.max))
                st.link(dve.tensor_tensor(LOC[n][:, :], li, hif, ALU.subtract))

            dve.wait_ge(edges_in, 48)
            place(0)
            with dve.Fori(0, EC // (COLS * ROUNDS)) as i:
                for m in range(COLS * ROUNDS):
                    c, s = i * (COLS * ROUNDS), m % COLS
                    column(0, c + m, c + (m + 1), permA[s], permR[s], s in SHARED)
            moved(0, bank[2], bank[3])
            for q in range(CH // PART):
                indices(0, 0, q)
            place(1)

            dve.wait_ge(w_in, 16 * 21)
            for k in range(2):
                b, g, be, m, v = (bn[:, 5 * k + j, :] for j in range(5))
                dve.tensor_scalar(sc[:, 2 * k, :], v, BN_EPS, None, ALU.add).then_inc(var_ready, 1)
                dve.wait_ge(std_ready, 2 + k)
                st.link(dve.reciprocal(sc[:, 2 * k, :], sc[:, 2 * k + 1, :]))
                st.did(dve.tensor_tensor(sc[:, 2 * k, :], sc[:, 2 * k, :], g, ALU.mult))
                st.link(dve.tensor_tensor(sc[:, 2 * k + 1, :], b, m, ALU.subtract))
                st.link(dve.tensor_tensor(sc[:, 2 * k + 1, :], sc[:, 2 * k + 1, :], sc[:, 2 * k, :], ALU.mult))
                st.link(dve.tensor_tensor(sc[:, 2 * k + 1, :], sc[:, 2 * k + 1, :], be, ALU.add))
            st.did(dve.tensor_tensor(bias[:, 7, :], bias[:, 5, :], bias[:, 6, :], ALU.add))
            st.did(dve.tensor_tensor(gate_b[:, 1, :], gate_b[:, 1, :], gate_b[:, 2, :], ALU.add))
            for s in range(2):
                st.did(dve.memset(vb[s][:, D:D + 2], 1.0))
            st.link(dve.memset(kvbd[:, :, :], 0.0))
            barrier()

            def onehot(n, i, s):
                dve.tensor_scalar(hot[:, s % HOTS, :], iota[:, 0:P], LOC[n][:, ds(i * CH + s, 1)], None, ALU.is_equal
                                  ).then_inc(hot_ready, 1)

            def aggregate(layer, dst, stride, cols, banks, work, after=None):
                n, parts = (0 if layer < 2 else 1), CH // PART
                if layer:
                    for q in range(parts):
                        indices(n, 0, q)
                for s in range(HOTS):
                    onehot(n, 0, s)
                for i, here in turns(dve):
                    for s in range(CH):
                        at = i * CH + (SLOTS * layer + s)
                        if s % LOADS == 0:
                            _, starts = nc.values_load_multi_w_load_instructions(
                                TIL[n][0:1, ds(i * CH + s, LOADS)], engines=[mybir.EngineType.DVE], min_val=0, max_val=NT * stride,
                                skip_runtime_bounds_check_because="the sort writes the starts of its tiles, of which there are NT + 1")
                        dve.wait_ge(summed, at + 1)
                        dve.wait_ge(added, at + PSB)
                        if after and s % UNIT == after[0] + 1 and s // UNIT < here:
                            dve.wait_ge(after[1], i * 2 + (s // UNIT + READY))
                        a = dst[:, ds(starts[s % LOADS], cols)]
                        dve.tensor_tensor(a, a, bank[banks[s % len(banks)]][:, 0:cols], ALU.add).then_inc(added, 1)
                        beside(work, i, here, s)
                        if layer < 2 and s % 2 and not (layer == 1 and here == 1):
                            c = i * CPT + (C0 * layer + s // 2)
                            column(1, c, c + (EC + COLS - HCOLS + 1), permA1[s // 2 % HCOLS], permR1[s // 2 % HCOLS], True)
                        if s + HOTS < CH:
                            onehot(n, i, s + HOTS)
                        elif here == 2:
                            onehot(n, i + 1, s + HOTS - CH)
                        if s % PART == PART - 1 and here == 2:
                            indices(n, i + 1, s // PART)

            def kv_bias(t, s):
                dve.wait_ge(S["kv_products"], t + READY)
                dve.wait_ge(S["kv_tile_summed"], t + FREE)
                p = bank[3]
                dve.tensor_tensor(kb[s], p[:, 0:D], bias[:, 0, :], ALU.add).then_inc(S["kv_k_biased"], 1)
                dve.tensor_tensor(vb[s][:, 0:D], p[:, D:2 * D], bias[:, 1, :], ALU.add).then_inc(S["kv_v_biased"], 1)

            def k_feature(t, s):
                dve.wait_ge(S["kv_k_exp"], t + READY)
                dve.tensor_scalar(mb[s], eb[s], 1.0, None, ALU.min).then_inc(S["kv_k_exp_capped"], 1)
                dve.wait_ge(S["kv_k_exp_capped"], t + 1)
                dve.scalar_tensor_tensor(kf[s], kb[s], 0.0, mb[s], ALU.max, ALU.add).then_inc(S["kv_k_feature"], 1)

            def q_bias(t, s):
                dve.wait_ge(S["q_products"], t + READY)
                dve.wait_ge(S["q_kv_products"], t + FREE)
                p = bank[2][:, D:2 * D]
                for m in range(2):
                    ins = dve.tensor_scalar(kb[s][:, m * P:(m + 1) * P], p[:, m * P:(m + 1) * P], bq[:, m:m + 1], 0.0,
                                            ALU.add, ALU.max)
                ins.then_inc(S["q_biased"], 1)

            def q_feature(t, s):
                dve.wait_ge(S["q_exp"], t + 1)
                dve.scalar_tensor_tensor(kf[s], eb[s], 1.0, kb[s], ALU.min, ALU.add).then_inc(S["q_feature_ready"], 1)

            def q_normalise(t, s):
                dve.wait_ge(S["q_kv_products"], t + READY)
                n = bank[3]
                dve.tensor_scalar(nr[s][:, 0:NE], n[:, D:D + NE], 1e-6, None, ALU.add).then_inc(S["q_denominator"], 1)
                wait_alone(dve, S["q_denominator"], t + 1)
                dve.reciprocal(nr[s][:, NE:2 * NE], nr[s][:, 0:NE]).then_inc(S["q_reciprocal"], 1)
                dve.wait_ge(S["q_reciprocal"], t + 1)
                dve.wait_ge(S["q_out_transposed"], t + FREE)
                dve.tensor_tensor(of[s].rearrange("p (h e) -> p h e", h=NE), n[:, 0:D].rearrange("p (h e) -> p h e", h=NE),
                                  nr[s][:, NE:2 * NE].unsqueeze(2).to_broadcast([P, NE, HEAD0]), ALU.mult
                                  ).then_inc(S["q_normalised"], 1)

            def q_out(t, s):
                dve.wait_ge(S["q_out_products"], t + READY)
                dve.tensor_tensor(xt(t), xt(t), bank[4][:, D:2 * D], ALU.add).then_inc(S["q_added"], 1)

            def x_plus(t, s):
                dve.wait_ge(S["tile_products"], t + READY)
                dve.wait_ge(added, t * UNIT + (SLOTS * 2 + 6 + 1 + PSB))
                dve.tensor_tensor(xt(t), xt(t), bank[3][:, 0:D], ALU.add).then_inc(S["attn1_added"], 1)

            def dense(layer):
                if layer == 0:
                    st.link(dve.tensor_scalar(MV[:, 2, 0:NT], AGG[:, 0:NT * DS].rearrange("p (t c) -> p c t", c=DS)[:, D, :], 1.0,
                                              None, ALU.max))
                    st.did(dve.memset(MV[:, 3, NT:NT + 1], 0.0))
                    st.link(dve.reciprocal(MV[:, 3, 0:NT], MV[:, 2, 0:NT]))

                def mean(t, s, free):
                    dve.wait_ge(S["gnn_transposed"], free)
                    dve.tensor_scalar(nb[s], AGG[:, ds(t * DS, D)], MV[:, 3, ds(t, 1)], None, ALU.mult).then_inc(S["gnn_mean_ready"], 1)

                o = NT * layer
                mean(0, 0, o + FREE)
                mean(1, 1, o + FREE + 1)
                for t, s in tiles(dve):
                    if layer:
                        st.turn(t, 1)
                    if not isinstance(t, int):
                        mean(t + 2, s, t + (o + FREE + 2))
                    dve.wait_ge(S["gnn_products"], t + (o + READY))
                    if layer == 0:
                        dve.tensor_scalar(XN[:, ds(t * ROW, D)], bank[2 + s][:, 0:D], 0.0, None, ALU.max).then_inc(S["gnn_row_ready"], 1)
                    else:
                        dve.scalar_tensor_tensor(xt(t), bank[2 + s][:, 0:D], 0.0, xt(t), ALU.max, ALU.add).then_inc(S["gnn_row_ready"], 1)
                        wait_alone(dve, S["gnn_row_ready"], t + (o + READY))
                        st.did(moments(t))
                if layer:
                    st.ended(NT)

            st.link(dve.memset(AGG[:, :], 0.0))
            aggregate(0, AGG, DS, DS, [0, 1], {6: kv_bias, 9: k_feature})
            dve.wait_ge(S["kv_done"], 1)
            for h in range(2):
                for a in range(4):
                    hd = 4 * h + a
                    r = slice(32 * a, 32 * a + 32)
                    st.did(dve.tensor_copy(kvbd[r, h, hd * HEAD0:(hd + 1) * HEAD0],
                                           bank[4 + h][r, hd * HEAD0:(hd + 1) * HEAD0]))
                    st.did(dve.tensor_copy(kvbd[r, h, D + hd:D + hd + 1], bank[4 + h][r, D:D + 1]))
            barrier()
            dense(0)
            dve.wait_ge(S["gnn_mean_ready"], NT + 1 + 2)
            st.did(dve.memset(AGG[:, :], 0.0))
            barrier()
            barrier()
            aggregate(1, AGG, DS, D, [0, 1], {3: q_bias, 5: q_feature, 9: q_normalise, 14: q_out})
            moved(1, bank[6], bank[7])
            barrier()
            dense(1)
            stats(4)
            barrier()

            def x_add(g, n_tiles, e, scale, psum_banks, sig_y, sig_acc, sig_b):
                dve.wait_ge(S[sig_y], g * NE + (e + READY))
                if e == 0:
                    dve.wait_ge(S[sig_b], g + 2)
                else:
                    dve.wait_ge(S[sig_acc], g * NE + (e + 1))
                for j in range(n_tiles):
                    x_ = xt(g * GT + j)
                    ins = dve.scalar_tensor_tensor(x_, bank[psum_banks + j // 2][:, (j % 2) * D:(j % 2 + 1) * D],
                                                   scale[:, j * NE + e:j * NE + e + 1], x_, ALU.mult, ALU.add)
                ins.then_inc(S[sig_acc], 1)

            def norm_group(g, n_tiles):
                dve.wait_ge(S["ffn_x_transposed"], g + 1)
                for j in range(n_tiles):
                    ins = norm(xgin[:, j, :], g * GT + j)
                ins.then_inc(S["ffn_x_normalised"], 1)

            norm_group(0, GT)
            for g, T_, next_T in groups(dve):
                st.turn(g, 5)
                dve.wait_ge(S["ffn_gate_products"], g + 1)
                n = T_ * NE
                v = [rt[:, k, 0:n].rearrange("p (t e) -> p t e", e=NE) for k in range(8)]
                st.link(dve.tensor_tensor(v[0], bank[6][:, 0:n].rearrange("p (t e) -> p t e", e=NE),
                                          gate_b[:, 0:1, :].to_broadcast([P, T_, NE]), ALU.add))
                st.link(dve.tensor_reduce(rt[:, 1, 0:T_], v[0], AX.X, ALU.max))
                dve.tensor_tensor(v[2], v[0], rt[:, 1, 0:T_].unsqueeze(2).to_broadcast([P, T_, NE]), ALU.subtract
                                  ).then_inc(S["ffn_gate_less_max"], 1)
                dve.wait_ge(S["ffn_gate_exp"], g + 1)
                st.link(dve.tensor_reduce(rt[:, 4, 0:T_], v[3], AX.X, ALU.add))
                st.link(dve.reciprocal(rt[:, 5, 0:T_], rt[:, 4, 0:T_]))
                dve.tensor_tensor(v[6], v[3], rt[:, 5, 0:T_].unsqueeze(2).to_broadcast([P, T_, NE]), ALU.mult
                                  ).then_inc(S["ffn_gates_ready"], 1)
                dve.wait_ge(S["ffn_gates_transposed"], g + 1)
                dve.tensor_copy(wT[:, 0:T_ * P], bank[7][0:NE, 0:T_ * P]).then_inc(S["ffn_gatesT_copied"], 1)
                dve.wait_ge(S["ffn_bias_products"], g + 1)
                for j in range(T_):
                    x_ = xt(g * GT + j)
                    ins = dve.tensor_tensor(x_, x_, bank[6 + j // 2][:, (j % 2) * D:(j % 2 + 1) * D], ALU.add)
                ins.then_inc(S["ffn_bias_added"], 1)
                if next_T:
                    norm_group(g + 1, next_T)
                for e in range(NE):
                    x_add(g, T_, e, rt[:, 6, :], 4, "ffn_third_products", "ffn_expert_added", "ffn_bias_added")
                wait_alone(dve, S["ffn_expert_added"], g * NE + (NE + 1))
                for j in range(T_):
                    ins = moments(g * GT + j)
                st.did(ins)
            st.ended(NG + 1)
            stats(5)
            barrier()

            st.did(dve.memset(DT[:, :, :], 0.0))
            hv = wkv1.rearrange("p k n -> p (k n)").rearrange("p (h e) -> p h e", e=HEAD1)
            st.link(dve.tensor_reduce(rs[:, 0:32], hv, AX.X, ALU.add))
            st.link(dve.tensor_scalar(rs[:, 32:64], rs[:, 0:32], 1.0 / HEAD1, None, ALU.mult))
            dve.tensor_tensor(hv, hv, rs[:, 32:64].unsqueeze(2).to_broadcast([P, 32, HEAD1]), ALU.subtract
                              ).then_inc(S["kv1_weights_centred"], 1)
            norm(XN[:, 0:D], 0).then_inc(S["kv1_x_normalised"], 1)
            for t, s in tiles(dve):
                st.turn(t, 3)
                if not isinstance(t, int):
                    norm(XN[:, ds(t * ROW + ROW, D)], t + 1).then_inc(S["kv1_x_normalised"], 1)
                dve.wait_ge(S["kv1_squared"], t + 1)
                st.link(dve.tensor_reduce(rs[:, 0:16], sq.rearrange("p (h e) -> p h e", e=HEAD1), AX.X, ALU.add))
                dve.tensor_scalar(rs[:, 16:32], rs[:, 0:16], 1.0 / HEAD1, LN_EPS, ALU.mult, ALU.add).then_inc(S["kv1_var_ready"], 1)
                dve.wait_ge(S["kv1_std_ready"], t + 1)
                st.link(dve.reciprocal(rs[:, 32:48], rs[:, 48:64]))
                st.link(dve.tensor_tensor(rs[:, 0:8], rs[:, 32:40], rs[:, 40:48], ALU.mult))
                dve.wait_ge(S["kv1_tile_summed"], t + 1)
                dve.tensor_tensor(kc.rearrange("p (h e) -> p h e", e=HEAD1), bank[6][:, :].rearrange("p (h e) -> p h e", e=HEAD1),
                                  rs[:, 0:8].unsqueeze(2).to_broadcast([P, NE, HEAD1]), ALU.mult).then_inc(S["kv1_k_scaled"], 1)
                for q in range(2, 4):
                    dve.wait_ge(S["hall_products"], t * 4 + (q + 1 + 5))
                    if q == 2:
                        dve.wait_ge(hall_stored[s], t * 8 + (16 - 8 * s))
                    dve.tensor_copy(ho[s][:, q * 512:(q + 1) * 512], bank[2 + q][:, :]).then_inc(S["hall_copied_by_dve"], 1)
            st.ended(NT)
            dve.wait_ge(S["kv1_tile_summed"], NT + 2)
            b1 = bank[1][:, :].rearrange("p (a b) -> p a b", b=P)
            st.did(dve.tensor_scalar(DT[0:64, :, 0:64], b1[0:64, :, 0:64], 1.0 / N, None, ALU.mult))
            dve.tensor_scalar(DT[64:P, :, 64:P], b1[64:P, :, 64:P], 1.0 / N, None, ALU.mult).then_inc(S["fold_kv_ready"], 1)
            dve.wait_ge(S["fold_first_products"], 1)
            for h in range(2):
                ins = dve.tensor_copy(MP[:, 2 * h:2 * h + 2, :].rearrange("p a b -> p (a b)"), bank[2 + h][:, :])
            ins.then_inc(S["fold_first_copied"], 1)
            dve.wait_ge(S["fold_second_products"], 1)
            dve.tensor_copy(WEFF.rearrange("p a b -> p (a b)"), bank[4][:, :])
            barrier()
            aggregate(2, X, D, D, [0, 1, 4, 5], {6: x_plus}, (6, S["attn1_added"]))
            dve.wait_ge(added, 3 * SLOTS + PSB)
            all_moments()
            stats(6)
            barrier()

            with dve.Fori(0, NT // OG) as i:
                for j in range(OG):
                    norm(XN[:, ds(i * OG * ROW + j * ROW, D)], i * OG + j).then_inc(S["gate_x_normalised"], 1)
            dve.wait_ge(S["tile_products"], 2 * NT + 2)
            st.link(dve.tensor_tensor(logits, bank[2][:, 0:NT * NE].rearrange("p (t e) -> p t e", e=NE),
                                      gate_b[:, 1:2, :].to_broadcast([P, NT, NE]), ALU.add))
            for t in range(NT):
                st.did(dve.max(best[:, t, :], logits[:, t, :]))
            st.wait()
            for t in range(NT):
                st.did(dve.max_index(bestat[:, t, :], best[:, t, :], logits[:, t, :]))
            dve.tensor_tensor(MV[:, 4, 0:NT], best[:, :, 1], best[:, :, 0], ALU.subtract).then_inc(S["gate_difference"], 1)
            st.wait()
            for k in range(TOP):
                st.did(dve.tensor_copy(chosen[:, k, :], bestat[:, :, k]))
            st.wait()
            st.link(dve.tensor_tensor(chosen[:, :, NT - 1], chosen[:, :, NT - 1], beyond[:, :].to_broadcast([P, TOP]), ALU.add))
            dve.wait_ge(S["gate_exp"], 1)
            st.link(dve.tensor_scalar(MV[:, 6, 0:NT], MV[:, 5, 0:NT], 1.0, None, ALU.add))
            st.link(dve.reciprocal(MV[:, 2, 0:NT], MV[:, 6, 0:NT]))
            st.did(dve.tensor_tensor(MV[:, 3, 0:NT], MV[:, 2, 0:NT], MV[:, 5, 0:NT], ALU.mult))
            items = chosen.rearrange("p k t -> p (k t)")
            for e in range(NE):
                st.did(dve.tensor_scalar(mask[:, e, :], items, float(e), 0.0, ALU.is_equal, ALU.add, accum_out=small[:, e:e + 1]))
            c = starts(2, NE, XCH)
            st.did(dve.tensor_scalar(wexp[:, 0:XCH], bank[1][:, 0:XCH], float(NE - 1), float(WST), ALU.min, ALU.mult))
            st.did(dve.tensor_scalar(bexp[:, 0:XCH], bank[1][:, 0:XCH], float(NE - 1), float(BST), ALU.min, ALU.mult))
            st.link(dve.memset(ipos, -1.0))
            for e in range(NE):
                st.link(dve.tensor_tensor_scan(rank[e % 2], mask[:, e, :], zeros[:, 0:ITEMS], c[:, e:e + 1], ALU.add, ALU.add))
                st.link(dve.copy_predicated(ipos, mask[:, e, :].bitcast(I32), rank[e % 2]))
            st.did(dve.tensor_scalar(item_slot, ipos, 0.0, None, ALU.max))
            st.did(dve.tensor_scalar(tokens, iota[:, 0:NT], float(P), rowf[:, :], ALU.mult, ALU.add))
            st.link(dve.tensor_copy(itemi[0], ipos))
            st.did(dve.tensor_scalar(itemi[1], itemi[0], P - 1, None, ALU.bitwise_and))
            st.did(dve.tensor_scalar(itemi[2], itemi[0], 7, None, ALU.arith_shift_right))
            st.wait()
            for k in range(2):
                st.did(dve.tensor_copy(itemf[k], itemi[1 + k]))
            st.wait()
            with dve.Fori(0, NT // OG) as i:
                for m in range(OG * TOP):
                    j, k = divmod(m, TOP)
                    q, r = (a[:, ds(i * OG + (j + k * NT), 1)] for a in itemf)
                    dve.wait_ge(perm_used, i * (OG * TOP) + (2 * EC + m + 1 + COLS - TOP))
                    dve.tensor_scalar(itemA[k], iota[:, 0:P], q, tokens[:, ds(i * OG + j, 1)], ALU.is_equal, ALU.mult)
                    dve.tensor_scalar(itemR[k], iota[:, 0:XCH], r, None, ALU.is_equal).then_inc(perm_ready, 1)
            dve.wait_ge(perm_done, 3)
            st.did(dve.tensor_copy(slot_token, bank[3][:, 0:XCH]))
            barrier()

            def out_bias(d, s, before, start):
                dve.wait_ge(S["chunk_second_products"], d + READY)
                dve.wait_ge(ys_stored[s], before * 16 + 16)
                dve.tensor_tensor(yo[s], bank[6 + s][:, 0:D], AGG[:, ds(start + HW, D)], ALU.add).then_inc(S["chunk_output_ready"], 1)

            for c, s, before, _, _ in chunks(dve):
                at, span = (0, 1) if isinstance(c, int) and c == 0 else (c - 1, 2)
                _, b = nc.values_load_multi_w_load_instructions(
                    bexp[0:1, ds(at, span)], engines=[mybir.EngineType.DVE], min_val=0, max_val=(NE - 1) * BST,
                    skip_runtime_bounds_check_because="a minimum with the last expert's start bounds it")
                dve.wait_ge(S["chunk_first_products"], c + READY)
                dve.wait_ge(S["chunk_h_transposed"], c + FREE)
                dve.tensor_tensor(hs[s], bank[2 + s][:, :], AGG[:, ds(b[-1], HW)], ALU.add).then_inc(S["chunk_first_biased"], 1)
                if not (isinstance(c, int) and c == 0):
                    out_bias(c - 1, 1 - s, before, b[0])
            out_bias(XCH - 1, 1, XCH // 2 - 1, b[-1])
            barrier()

            for g in range(NT // OG):
                dve.wait_ge(gathered[g], 16 * (3 * TURNS + len(range(g, XCH, XB)) + TOP * OG))
                for k in range(TOP):
                    for t in range(g * OG, (g + 1) * OG):
                        x_ = xt(t)
                        ins = dve.scalar_tensor_tensor(x_, yr[k][:, t, 0:D], MV[:, 2 + k, t:t + 1], x_, ALU.mult, ALU.add)
                        if (k, t) != (TOP - 1, g * OG + OG - 1):
                            st.did(ins)
                    if k < TOP - 1:
                        st.wait()
                ins.then_inc(S["output_ready"], 1)

        @block.scalar
        def _(act):
            barrier = Barrier(act)
            for name, k in CREDIT["act"].items():
                act.sem_inc(S[name], k)
            act.sem_inc(place_ready, len(away))

            def std(n, dst, src):
                act.wait_ge(var_ready, n)
                act.activation(dst, src, ACT.Sqrt).then_inc(std_ready, 1)

            std(1, MV[:, 2, 0:NT], MV[:, 7, 0:NT])
            act.wait_ge(S["stats_ready"], 1)
            with act.Fori(0, NT // OG) as i:
                for j in range(OG):
                    t = i * OG + j
                    act.activation(XN[:, ds(i * OG * ROW + j * ROW, D)], xt(t), ACT.Identity, bias=MV[:, 4, ds(t, 1)],
                                   scale=MV[:, 1, ds(t, 1)])
            barrier()

            def distance(n, c, count, y):
                wait_alone(act, place_ready, count)
                act.activation(y[0:EP, :], iota16[0:EP, 0:P], ACT.Abs, bias=moves[n][0:EP, ds(c, 1)], scale=-1.0
                               ).then_inc(abs_ready, 1)

            def places(n, c, free, count, A, y):
                hi, lo = (moves[n][0:EP, ds(c + EC * k, 1)] for k in (2, 3))
                wait_alone(act, perm_used, free)
                wait_alone(act, abs_ready, count)
                act.activation(A[0:EP, 0:P], y[0:EP, :], ACT.Relu, bias=hi, scale=minus[n][0][0:EP, ds(c, 1)])
                act.activation(A[0:EP, P:2 * P], y[0:EP, :], ACT.Relu, bias=lo, scale=minus[n][1][0:EP, ds(c, 1)]
                               ).then_inc(place_ready, 1)

            act.wait_ge(moves_ready, 1)
            with act.Fori(0, EC // (COLS * ROUNDS)) as i:
                for u in range(ROUNDS):
                    c, done = i * (COLS * ROUNDS), i * (len(SHARED) * ROUNDS)
                    for k, s in enumerate(SHARED):
                        distance(0, c + (u * COLS + s), done + (u * len(SHARED) + k + 1), away[k])
                    for k, s in enumerate(SHARED):
                        places(0, c + (u * COLS + s), c + (u * COLS + s + 1), done + (u * len(SHARED) + k + 1), permA[s], away[k])
            std(2, sc[:, 1, :], sc[:, 0, :])
            std(3, sc[:, 3, :], sc[:, 2, :])
            barrier()

            def gathering(layer, work):
                for i, here in turns(act):
                    for s in range(CH):
                        beside(work, i, here, s)
                        if layer < 2 and s % 2 and not (layer == 1 and here == 1):
                            m = s // 2
                            c = i * CPT + (C0 * layer + m)
                            done = c + (EC // COLS * len(SHARED) + 1)
                            distance(1, c, done, away[m % 2])
                            places(1, c, c + (EC + COLS - HCOLS + 1), done, permA1[m % HCOLS], away[m % 2])

            def kv_in(t, s):
                wait_alone(act, S["kv_x_transposed"], t + FREE)
                act.copy(xin[s], XN[:, ds(t * ROW, D)]).then_inc(S["kv_x_loaded"], 1)
                act.wait_ge(S["kv_x_transposed"], t + READY)
                act.wait_ge(S["kv_products"], t + FREE)
                act.copy(xT[s].rearrange("p a b -> p (a b)"), bank[2][:, 0:D]).then_inc(S["kv_xT_copied"], 1)

            def k_exp(t, s):
                act.wait_ge(S["kv_k_biased"], t + 1)
                act.wait_ge(S["kv_k_feature"], t + FREE)
                act.activation(eb[s], kb[s], ACT.Exp).then_inc(S["kv_k_exp"], 1)

            def q_in(t, s):
                wait_alone(act, S["q_x_transposed"], t + FREE)
                act.activation(xin[s], xt(t), ACT.Identity, bias=MV[:, 4, ds(t, 1)], scale=MV[:, 1, ds(t, 1)]
                               ).then_inc(S["q_x_loaded"], 1)
                act.wait_ge(S["q_x_transposed"], t + READY)
                act.wait_ge(S["q_products"], t + FREE)
                act.copy(xT[s].rearrange("p a b -> p (a b)"), bank[2][:, 0:D]).then_inc(S["q_xT_copied"], 1)

            def q_exp(t, s):
                act.wait_ge(S["q_biased"], t + 1)
                act.wait_ge(S["q_feature_ready"], t + FREE)
                for m in range(2):
                    ins = act.activation(eb[s][:, m * P:(m + 1) * P], bank[2][:, D + m * P:D + (m + 1) * P], ACT.Exp,
                                         bias=bq[:, m:m + 1])
                ins.then_inc(S["q_exp"], 1)

            def q_outT(t, s):
                act.wait_ge(S["q_out_transposed"], t + READY)
                act.wait_ge(S["q_out_products"], t + FREE)
                act.copy(oT[s].rearrange("p a b -> p (a b)"), bank[4][:, 0:D]).then_inc(S["q_outT_copied"], 1)

            def attn_in(t, s):
                wait_alone(act, S["tile_x_transposed"], t + FREE)
                act.copy(xin[s], XN[:, ds(t * ROW, D)]).then_inc(S["tile_x_loaded"], 1)
                act.wait_ge(S["tile_x_transposed"], t + READY)
                act.wait_ge(S["tile_products"], t + FREE)
                act.copy(xT[s].rearrange("p a b -> p (a b)"), bank[2][:, 0:D]).then_inc(S["tile_xT_copied"], 1)

            def dense(layer):
                o = NT * layer

                def load(t, s):
                    wait_alone(act, S["gnn_transposed"], t + (o + FREE))
                    act.copy(xin[s], XN[:, ds(t * ROW, D)]).then_inc(S["gnn_x_loaded"], 1)

                load(0, 0)
                for t, s in tiles(act):
                    if not isinstance(t, int):
                        load(t + 1, 1 - s)
                    act.wait_ge(S["gnn_transposed"], t + (o + READY))
                    act.wait_ge(S["gnn_products"], t + (o + FREE))
                    act.copy(cT[s].rearrange("p a b -> p (a b)"), bank[s][:, :]).then_inc(S["gnn_copied"], 1)

            gathering(0, {0: kv_in, 7: k_exp})
            barrier()
            dense(0)
            barrier()
            barrier()
            gathering(1, {0: q_in, 4: q_exp, 12: q_outT})
            barrier()
            dense(1)
            std(4, MV[:, 2, 0:NT], MV[:, 7, 0:NT])
            barrier()
            for g, T_, next_T in groups(act):
                act.wait_ge(S["ffn_x_transposed"], g + 2)
                act.wait_ge(S["ffn_first_products"], g * 16 + 1)
                for k in range(2):
                    ins = act.copy(xg[:, k, 0:T_ * P], bank[k][:, 0:T_ * P])
                ins.then_inc(S["ffn_xT_copied"], 1)

                def relu(e, first):
                    lay, h = (0, h1) if first else (1, h2)
                    for m in range(2):
                        if first:
                            act.wait_ge(S["ffn_first_products"], g * 16 + (2 * e + m + 2))
                            if m == 0:
                                act.wait_ge(S["ffn_second_products"], g * 16 + 2 * e + 1)
                        else:
                            act.wait_ge(S["ffn_second_products"], g * 16 + (2 * e + m + 4))
                            if m == 0:
                                act.wait_ge(S["ffn_third_products"], g * NE + (e + FREE))
                        act.activation(h[e % 2][:, m, 0:T_ * P], bank[(2 if first else 0) + m][:, 0:T_ * P], ACT.Relu,
                                       bias=sc[:, 2 * lay + 1, 2 * e + m:2 * e + m + 1],
                                       scale=sc[:, 2 * lay, 2 * e + m:2 * e + m + 1]).then_inc(S["ffn_first_relu" if first else "ffn_second_relu"], 1)

                relu(0, True)
                for e in range(NE):
                    if e + 1 < NE:
                        relu(e + 1, True)
                    if e == 0:
                        act.wait_ge(S["ffn_gate_less_max"], g + 1)
                        act.activation(rt[:, 3, 0:T_ * NE], rt[:, 2, 0:T_ * NE], ACT.Exp).then_inc(S["ffn_gate_exp"], 1)
                    relu(e, False)
            std(5, MV[:, 2, 0:NT], MV[:, 7, 0:NT])
            barrier()
            def kv_in(t, s):
                wait_alone(act, S["kv1_x_transposed"], t + FREE)
                act.wait_ge(S["kv1_x_normalised"], t + READY)
                act.copy(xin[s], XN[:, ds(t * ROW, D)]).then_inc(S["kv1_x_loaded"], 1)

            def kv_xT(t, s):
                act.wait_ge(S["kv1_x_transposed"], t + READY)
                act.wait_ge(S["hall_products"], t * 4 + 1)
                act.copy(xT[s].rearrange("p a b -> p (a b)"), bank[0][:, 0:D]).then_inc(S["kv1_xT_copied"], 1)

            kv_in(0, 0)
            kv_xT(0, 0)
            for t, s in tiles(act):
                if not isinstance(t, int):
                    kv_in(t + 1, 1 - s)
                act.wait_ge(S["kv1_products"], t + 1)
                act.wait_ge(S["kv1_var_ready"], t + 1)
                for k in range(2):
                    ins = act.activation(sq[:, k * 512:(k + 1) * 512], bank[6 + k][:, :], ACT.Square)
                ins.then_inc(S["kv1_squared"], 1)
                act.wait_ge(S["kv1_tile_summed"], t + 1)
                act.copy(vc, bank[7][:, :]).then_inc(S["kv1_v_copied"], 1)
                act.wait_ge(S["kv1_var_ready"], t + 2)
                act.activation(rs[:, 48:64], rs[:, 16:32], ACT.Sqrt).then_inc(S["kv1_std_ready"], 1)
                if not isinstance(t, int):
                    kv_xT(t + 1, 1 - s)
                for q in range(2):
                    act.wait_ge(S["hall_products"], t * 4 + (q + 1 + 5))
                    if q == 0:
                        act.wait_ge(hall_stored[s], t * 8 + (16 - 8 * s))
                    act.copy(ho[s][:, q * 512:(q + 1) * 512], bank[2 + q][:, :]).then_inc(S["hall_copied_by_act"], 1)
            barrier()
            gathering(2, {0: attn_in})
            std(6, MV[:, 2, 0:NT], MV[:, 7, 0:NT])
            barrier()

            def gate_in(t, s):
                act.wait_ge(S["gate_x_normalised"], t + 1)
                wait_alone(act, S["tile_x_transposed"], t + (NT + FREE))
                act.copy(xin[s], XN[:, ds(t * ROW, D)]).then_inc(S["tile_x_loaded"], 1)

            gate_in(0, 0)
            for t, s in tiles(act):
                if not isinstance(t, int):
                    gate_in(t + 1, 1 - s)
                act.wait_ge(S["tile_x_transposed"], t + (NT + READY))
                act.wait_ge(S["tile_products"], t + (NT + FREE))
                act.copy(xT[s].rearrange("p a b -> p (a b)"), bank[s][:, 0:D]).then_inc(S["tile_xT_copied"], 1)
            act.wait_ge(S["gate_difference"], 1)
            act.activation(MV[:, 5, 0:NT], MV[:, 4, 0:NT], ACT.Exp).then_inc(S["gate_exp"], 1)
            barrier()

            def x_T(d, s):
                act.wait_ge(S["chunk_x_transposed"], d + READY)
                act.wait_ge(S["chunk_first_products"], d + FREE)
                act.copy(xT[s].rearrange("p a b -> p (a b)"), bank[s][:, 0:D]).then_inc(S["chunk_xT_copied"], 1)

            x_T(0, 0)
            for c, s, _, _, _ in chunks(act):
                if not (isinstance(c, int) and c == XCH - 1):
                    x_T(c + 1, 1 - s)
                act.wait_ge(S["chunk_h_transposed"], c + READY)
                act.wait_ge(S["chunk_second_products"], c + FREE)
                act.activation(hT[s].rearrange("p a b -> p (a b)"), bank[4 + s][:, :], ACT.Relu).then_inc(S["chunk_hT_copied"], 1)
            barrier()

        @block.tensor
        def _(pe):
            barrier = Barrier(pe)
            for name, k in CREDIT["pe"].items():
                pe.sem_inc(S[name], k)
            pe.sem_inc(perm_used, COLS)
            barrier()
            def close(b, start, stop):
                for k in range(2):
                    mm = pe.matmul(bank[b + k][:, 0:SLOTS], z16[0:EP, :], iota16[0:EP, :], start=start, stop=stop)
                return mm

            def column(c, b, A, R, shared):
                pe.wait_ge(perm_ready, c + 1)
                if shared is not None:
                    pe.wait_ge(place_ready, shared + len(away))
                for k in range(2):
                    mm = pe.matmul(bank[b + k][:, 0:SLOTS], A[0:EP, k * P:(k + 1) * P], R[0:EP, :], start=False, stop=False)
                mm.then_inc(perm_used, 1)

            def starts(n, rows, bins, slots):
                pe.wait_ge(counts_ready, n + 1)
                b0, c = bank[0], small[0:rows, 0:bins]
                pe.matmul(b0[:, 0:bins], tri[0:rows, :], c, start=True, stop=True)
                pe.matmul(b0[:, 32:32 + bins], ones[0:rows, :], c, start=True, stop=True)
                pe.matmul(b0[0:bins, 64:65], c, ones[0:rows, 0:1], start=True, stop=True).then_inc(prefix_ready, 1)
                pe.wait_ge(nch_ready, n + 1)
                pe.matmul(b0[0:bins, 66:67], trin[0:bins, 0:bins], small[0:bins, 224:225], start=True, stop=True
                          ).then_inc(chend_ready, 1)
                pe.wait_ge(ge_ready, n + 1)
                pe.matmul(bank[1][:, 0:slots], ones[0:bins, :], RA[0:bins, 3000:3000 + slots], start=True, stop=True
                          ).then_inc(til_ready, 1)

            for n in range(2):
                starts(n, EP, NT, SLOTS)
                if n == 0:
                    pe.wait_ge(perm_ready, 1)
                    close(2, start=True, stop=False)
                    with pe.Fori(0, EC // (COLS * ROUNDS)) as i:
                        for m in range(COLS * ROUNDS):
                            u, s = divmod(m, COLS)
                            shared = i * (len(SHARED) * ROUNDS) + (u * len(SHARED) + SHARED.index(s) + 1) if s in SHARED else None
                            column(i * (COLS * ROUNDS) + m, 2, permA[s], permR[s], shared)
                    close(2, start=False, stop=True).then_inc(perm_done, 1)
            barrier()

            def transpose(dst, src):
                for k in range(src.shape[-1] // P):
                    mm = pe.transpose(dst[:, k * P:(k + 1) * P], src[:, k * P:(k + 1) * P], ident[:, :])
                return mm

            def kv_T(t, s):
                pe.wait_ge(S["kv_x_loaded"], t + READY)
                pe.wait_ge(S["kv_xT_copied"], t + FREE + 1)
                transpose(bank[2], xin[s]).then_inc(S["kv_x_transposed"], 1)

            def kv_products(t, s):
                pe.wait_ge(S["kv_xT_copied"], t + READY)
                pe.wait_ge(S["kv_v_biased"], t + FREE + 1)
                for k in range(2):
                    mm = pe.matmul(bank[3][:, :], xT[s][:, k, :], wkv0[:, k, :], start=(k == 0), stop=(k == 1))
                mm.then_inc(S["kv_products"], 1)

            def kv_sums(t, s):
                rows = LAST if isinstance(t, int) else P
                pe.wait_ge(S["kv_k_feature"], t + READY)
                for h in range(2):
                    mm = pe.matmul(bank[4 + h][:, 0:D + 2], kf[s][0:rows, h * P:(h + 1) * P], vb[s][0:rows, 0:D + 2],
                                   start=False, stop=False)
                mm.then_inc(S["kv_tile_summed"], 1)

            def q_T(t, s):
                pe.wait_ge(S["q_x_loaded"], t + READY)
                pe.wait_ge(S["q_feature_ready"], t + FREE + 1)
                transpose(bank[2], xin[s]).then_inc(S["q_x_transposed"], 1)

            def q_products(t, s):
                pe.wait_ge(S["q_xT_copied"], t + READY)
                for m in range(2):
                    for k in range(2):
                        mm = pe.matmul(bank[2][:, D + m * P:D + (m + 1) * P], wq0[:, k, m * P:(m + 1) * P], xT[s][:, k, :],
                                       start=(k == 0), stop=(k == 1))
                mm.then_inc(S["q_products"], 1)

            def q_kv(t, s):
                pe.wait_ge(S["q_feature_ready"], t + READY)
                pe.wait_ge(S["q_normalised"], t + FREE + 1)
                for m in range(2):
                    mm = pe.matmul(bank[3][:, 0:D + NE], kf[s][:, m * P:(m + 1) * P], kvbd[:, m, :],
                                   start=(m == 0), stop=(m == 1))
                mm.then_inc(S["q_kv_products"], 1)

            def q_outT(t, s):
                pe.wait_ge(S["q_normalised"], t + READY)
                pe.wait_ge(S["q_added"], t + FREE + 1)
                transpose(bank[4], of[s]).then_inc(S["q_out_transposed"], 1)

            def q_out(t, s):
                pe.wait_ge(S["q_outT_copied"], t + READY)
                for k in range(2):
                    mm = pe.matmul(bank[4][:, D:2 * D], oT[s][:, k, :], wo0[:, k, :], start=(k == 0), stop=False)
                pe.matmul(bank[4][:, D:2 * D], ones[0:1, :], bias[0:1, 2, :], start=False, stop=True).then_inc(S["q_out_products"], 1)

            def attn_T(t, s):
                pe.wait_ge(S["tile_x_loaded"], t + READY)
                pe.wait_ge(S["tile_xT_copied"], t + FREE + 1)
                transpose(bank[2], xin[s]).then_inc(S["tile_x_transposed"], 1)

            def attn_out(t, s):
                pe.wait_ge(S["tile_xT_copied"], t + READY)
                pe.wait_ge(S["attn1_added"], t + FREE + 1)
                for k in range(2):
                    mm = pe.matmul(bank[3][:, 0:D], xT[s][:, k, :], WEFF[:, k, :], start=(k == 0), stop=False)
                pe.matmul(bank[3][:, 0:D], ones[0:1, :], bias[0:1, 7, :], start=False, stop=True).then_inc(S["tile_products"], 1)

            def aggregate(layer, cols, banks, work):
                for i, here in turns(pe):
                    for s in range(CH):
                        at = i * CH + (SLOTS * layer + s)
                        pe.wait_ge(hot_ready, at + 1)
                        pe.wait_ge(gathered[s], i * 16 + (TURNS * layer + 1) * 16)
                        pe.wait_ge(added, at + (1 + PSB - len(banks)))
                        pe.matmul(bank[banks[s % len(banks)]][:, 0:cols], hot[:, s % HOTS, :], ring[:, s, 0:cols],
                                  start=True, stop=True).then_inc(summed, 1)
                        beside(work, i, here, s)
                        if layer < 2 and s % 2 and not (layer == 1 and here == 1):
                            if s > 1:
                                m = s // 2 - 1
                                column(i * CPT + (EC + C0 * layer + m), 6, permA1[m % HCOLS], permR1[m % HCOLS],
                                       i * CPT + (EC // COLS * len(SHARED) + C0 * layer + m + 1))
                            if s == CH - 1:
                                m = s // 2
                                column(i * CPT + (EC + C0 * layer + m), 6, permA1[m % HCOLS], permR1[m % HCOLS],
                                       i * CPT + (EC // COLS * len(SHARED) + C0 * layer + m + 1))

            def dense(layer):
                o = NT * layer

                def inT(t, s):
                    pe.wait_ge(S["gnn_x_loaded"], t + (o + READY))
                    pe.wait_ge(S["gnn_mean_ready"], t + ((NT + 1) * layer + READY))
                    pe.wait_ge(S["gnn_copied"], t + (o + FREE))
                    transpose(bank[s], xin[s])
                    transpose(bank[s][:, D:2 * D], nb[s]).then_inc(S["gnn_transposed"], 1)

                inT(0, 0)
                for t, s in tiles(pe):
                    if not isinstance(t, int):
                        inT(t + 1, 1 - s)
                    pe.wait_ge(S["gnn_copied"], t + (o + READY))
                    pe.wait_ge(S["gnn_row_ready"], t + (o + FREE))
                    for k in range(4):
                        pe.matmul(bank[2 + s][:, 0:D], cT[s][:, k, :], gw[layer][:, k, :], start=(k == 0), stop=False)
                    pe.matmul(bank[2 + s][:, 0:D], ones[0:1, :], bias[0:1, 3 + layer, :], start=False, stop=True
                              ).then_inc(S["gnn_products"], 1)

            close(6, start=True, stop=False)
            for h in range(2):
                pe.matmul(bank[4 + h][:, 0:D + 2], zeros[:, 0:P], zeros[:, 0:D + 2], start=True, stop=False)
            aggregate(0, DS, [0, 1], {1: kv_T, 4: kv_products, 12: kv_sums})
            for h in range(2):
                mm = pe.matmul(bank[4 + h][:, 0:D + 2], zeros[:, 0:P], zeros[:, 0:D + 2], start=False, stop=True)
            mm.then_inc(S["kv_done"], 1)
            barrier()
            dense(0)
            barrier()
            barrier()
            aggregate(1, D, [0, 1], {0: q_T, 2: q_products, 7: q_kv, 11: q_outT, 13: q_out})
            close(6, start=False, stop=True).then_inc(perm_done, 1)
            barrier()
            dense(1)
            barrier()

            def group_T(g, n_tiles):
                pe.wait_ge(S["ffn_x_normalised"], g + 1)
                pe.wait_ge(S["ffn_second_relu"], g * 16 + 2)
                for k in range(2):
                    for j in range(n_tiles):
                        mm = pe.transpose(bank[k][:, j * P:(j + 1) * P], xgin[:, j, k * P:(k + 1) * P], ident[:, :])
                mm.then_inc(S["ffn_x_transposed"], 1)

            group_T(0, GT)
            for g, T_, next_T in groups(pe):
                W = T_ * P
                pe.wait_ge(S["ffn_xT_copied"], g + 1)
                pe.wait_ge(S["ffn_bias_added"], g + 1)
                for j in range(T_):
                    for k in range(2):
                        mm = pe.matmul(bank[6][:, j * NE:(j + 1) * NE], xg[:, k, j * P:(j + 1) * P], wr0[:, k, :],
                                       start=(k == 0), stop=(k == 1))
                mm.then_inc(S["ffn_gate_products"], 1)

                def first(e):
                    for m in range(2):
                        pe.wait_ge(S["ffn_first_relu"], g * 16 + (2 * e + m + FREE))
                        for k in range(2):
                            mm = pe.matmul(bank[2 + m][:, 0:W], w1[:, e, k, m * P:(m + 1) * P], xg[:, k, 0:W],
                                           start=(k == 0), stop=(k == 1))
                        mm.then_inc(S["ffn_first_products"], 1)

                def second(e):
                    pe.wait_ge(S["ffn_first_relu"], g * 16 + (2 * e + 1 + READY))
                    for m in range(2):
                        pe.wait_ge(S["ffn_second_relu"], g * 16 + (2 * e + m + FREE))
                        for k in range(2):
                            mm = pe.matmul(bank[m][:, 0:W], w2[:, e, k, m * P:(m + 1) * P], h1[e % 2][:, k, 0:W],
                                           start=(k == 0), stop=(k == 1))
                        mm.then_inc(S["ffn_second_products"], 1)

                def third(e):
                    pe.wait_ge(S["ffn_second_relu"], g * 16 + (2 * e + 1 + READY))
                    pe.wait_ge(S["ffn_expert_added"], g * NE + e + 1)
                    for j in range(T_):
                        for k in range(2):
                            mm = pe.matmul(bank[4 + j // 2][:, (j % 2) * D:(j % 2 + 1) * D], h2[e % 2][:, k, j * P:(j + 1) * P],
                                           wo[:, e, k, :], start=(k == 0), stop=(k == 1))
                    mm.then_inc(S["ffn_third_products"], 1)

                def gates_T():
                    pe.wait_ge(S["ffn_gates_ready"], g + 1)
                    for j in range(T_):
                        mm = pe.transpose(bank[7][0:NE, j * P:(j + 1) * P], rt[:, 6, j * NE:(j + 1) * NE], ident[:, :])
                    mm.then_inc(S["ffn_gates_transposed"], 1)

                def out_bias():
                    pe.wait_ge(S["ffn_gatesT_copied"], g + 1)
                    for j in range(T_):
                        mm = pe.matmul(bank[6 + j // 2][:, (j % 2) * D:(j % 2 + 1) * D], wT[:, j * P:(j + 1) * P], bo_e[:, :],
                                       start=True, stop=True)
                    mm.then_inc(S["ffn_bias_products"], 1)

                first(0)
                first(1)
                second(0)
                gates_T()
                for e in range(2, NE):
                    first(e)
                    if e == 2:
                        out_bias()
                    second(e - 1)
                    third(e - 2)
                second(NE - 1)
                third(NE - 2)
                if next_T:
                    group_T(g + 1, next_T)
                third(NE - 1)
            barrier()

            pe.wait_ge(S["kv1_weights_centred"], 1)
            pe.matmul(bank[1][:, :], zeros[:, 0:P], zeros[:, :], start=True, stop=False)
            def xn_T(t, s):
                pe.wait_ge(S["kv1_x_loaded"], t + 1)
                pe.wait_ge(S["kv1_xT_copied"], t + FREE + 1)
                transpose(bank[0], xin[s]).then_inc(S["kv1_x_transposed"], 1)

            xn_T(0, 0)
            for t, s in tiles(pe):
                rows = LAST if isinstance(t, int) else P
                pe.wait_ge(S["kv1_xT_copied"], t + READY)
                pe.wait_ge(S["kv1_k_scaled"], t + 1)
                pe.wait_ge(S["kv1_v_copied"], t + 1)
                for b in range(2):
                    for k in range(2):
                        mm = pe.matmul(bank[6 + b][:, :], xT[s][:, k, :], wkv1[:, k, b * HW:(b + 1) * HW],
                                       start=(k == 0), stop=(k == 1))
                mm.then_inc(S["kv1_products"], 1)
                pe.wait_ge(S["hall_copied_by_act"], t * 2 + 1)
                pe.wait_ge(S["hall_copied_by_dve"], t * 2 + 1)
                for q in range(4):
                    if q == 2 and not isinstance(t, int):
                        xn_T(t + 1, 1 - s)
                    for k in range(2):
                        mm = pe.matmul(bank[2 + q][:, :], xT[s][:, k, :], wr[:, k, q * 512:(q + 1) * 512],
                                       start=(k == 0), stop=(k == 1))
                    mm.then_inc(S["hall_products"], 1)
                pe.wait_ge(S["kv1_k_scaled"], t + 2)
                pe.wait_ge(S["kv1_v_copied"], t + 2)
                for p in range(4):
                    mm = pe.matmul(bank[1][:, p * P:(p + 1) * P], vc[0:rows, p * P:(p + 1) * P], kc[0:rows, p * P:(p + 1) * P],
                                   start=False, stop=False)
                mm.then_inc(S["kv1_tile_summed"], 1)
            pe.matmul(bank[1][:, :], zeros[:, 0:P], zeros[:, :], start=False, stop=True).then_inc(S["kv1_tile_summed"], 1)
            pe.wait_ge(S["fold_kv_ready"], 1)
            pe.wait_ge(S["hall_copied_by_act"], 2 * NT + 1)
            pe.wait_ge(S["hall_copied_by_dve"], 2 * NT + 1)
            for p in range(4):
                mm = pe.matmul(bank[2 + p // 2][:, (p % 2) * D:(p % 2 + 1) * D], DT[:, p, :], wout1[:, p, :],
                               start=True, stop=True)
            mm.then_inc(S["fold_first_products"], 1)
            pe.wait_ge(S["fold_first_copied"], 1)
            for m in range(2):
                for p in range(4):
                    mm = pe.matmul(bank[4][:, m * D:(m + 1) * D], wqT1[:, p, m * P:(m + 1) * P], MP[:, p, :],
                                   start=(p == 0), stop=(p == 3))
            mm.then_inc(S["fold_second_products"], 1)
            barrier()
            aggregate(2, D, [0, 1, 4, 5], {1: attn_T, 4: attn_out})
            barrier()
            def gate_T(t, s):
                pe.wait_ge(S["tile_x_loaded"], t + (NT + READY))
                pe.wait_ge(S["tile_xT_copied"], t + (NT + FREE))
                transpose(bank[s], xin[s]).then_inc(S["tile_x_transposed"], 1)

            gate_T(0, 0)
            for t, s in tiles(pe):
                if not isinstance(t, int):
                    gate_T(t + 1, 1 - s)
                pe.wait_ge(S["tile_xT_copied"], t + (NT + READY))
                for k in range(2):
                    mm = pe.matmul(bank[2][:, ds(t * NE, NE)], xT[s][:, k, :], wg1[:, k, :], start=(k == 0), stop=(k == 1))
                mm.then_inc(S["tile_products"], 1)
            starts(2, P, NE, XCH)
            pe.matmul(bank[3][:, 0:XCH], zeros[:, 0:P], zeros[:, 0:XCH], start=True, stop=False)
            with pe.Fori(0, NT // OG) as i:
                for m in range(OG * TOP):
                    k = m % TOP
                    pe.wait_ge(perm_ready, i * (OG * TOP) + (2 * EC + m + 1))
                    pe.matmul(bank[3][:, 0:XCH], itemA[k], itemR[k], start=False, stop=False).then_inc(perm_used, 1)
            pe.matmul(bank[3][:, 0:XCH], zeros[:, 0:P], zeros[:, 0:XCH], start=False, stop=True).then_inc(perm_done, 1)
            barrier()

            def xs_T(d, s, b, uses):
                pe.wait_ge(gathered[b], uses * 16 + 16 * (3 * TURNS + 1))
                pe.wait_ge(S["chunk_xT_copied"], d + FREE)
                transpose(bank[s], xc[b]).then_inc(S["chunk_x_transposed"], 1)

            def second(d, s, start):
                pe.wait_ge(S["chunk_hT_copied"], d + READY)
                pe.wait_ge(S["chunk_output_ready"], d + FREE)
                for k in range(4):
                    mm = pe.matmul(bank[6 + s][:, 0:D], hT[s][:, k, :], WA[:, ds(start + (NE * WST + D * k), D)],
                                   start=(k == 0), stop=(k == 3))
                mm.then_inc(S["chunk_second_products"], 1)

            xs_T(0, 0, 0, 0)
            for c, s, _, b, uses in chunks(pe):
                at, span = (0, 1) if isinstance(c, int) and c == 0 else (c - 1, 2)
                _, w = nc.values_load_multi_w_load_instructions(
                    wexp[0:1, ds(at, span)], engines=[mybir.EngineType.PE], min_val=0, max_val=(NE - 1) * WST,
                    skip_runtime_bounds_check_because="a minimum with the last expert's start bounds it")
                pe.wait_ge(S["chunk_xT_copied"], c + READY)
                pe.wait_ge(S["chunk_first_biased"], c + FREE)
                for k in range(2):
                    mm = pe.matmul(bank[2 + s][:, :], xT[s][:, k, :], WA[:, ds(w[-1] + HW * k, HW)], start=(k == 0), stop=(k == 1))
                mm.then_inc(S["chunk_first_products"], 1)
                if not (isinstance(c, int) and c == XCH - 1):
                    xs_T(c + 1, 1 - s, b, uses)
                if not (isinstance(c, int) and c == 0):
                    second(c - 1, 1 - s, w[0])
                pe.wait_ge(S["chunk_first_biased"], c + READY)
                pe.wait_ge(S["chunk_hT_copied"], c + FREE)
                transpose(bank[4 + s], hs[s]).then_inc(S["chunk_h_transposed"], 1)
            second(XCH - 1, 1, w[-1])
            barrier()


def kernel(**inputs):
    import numpy as _np
    import concourse.bacc as _bacc
    from concourse import mybir as _mybir
    from concourse.bass_utils import run_bass_kernel_spmd as _run

    a = {k: _np.asarray(v) for k, v in inputs.items()}
    cols = lambda v: v.reshape(-1, P).T
    laid = {k: v for k, v in a.items() if not k.startswith("L0_ffn_") or k[7:] in ("W1", "W2", "Wo", "Wr", "br", "bo")}
    for k in ("L0_gnn_W0", "L0_gnn_W1", "L1_gnn_weight", "L1_mix_w_qkv"):
        del laid[k]
    laid["W0T"], laid["W1T"] = a["L0_gnn_W0"].T, a["L0_gnn_W1"].T
    laid["WrT"] = a["L1_gnn_weight"].reshape(NE * D, D).T
    laid["wkv"], laid["wqT"] = a["L1_mix_w_qkv"][:, HW:], a["L1_mix_w_qkv"][:, :HW].T
    laid["bq"] = cols(laid.pop("L0_mix_bq"))
    laid["bn"] = _np.stack([cols(a["L0_ffn_" + n + k]) for k in "12" for n in ("b", "g", "be", "m", "v")], 1)
    nc = _bacc.Bacc("TRN2", target_bir_lowering=False, num_devices=1)
    arrays, T = {}, {}
    for name, v in laid.items():
        v = _np.ascontiguousarray(v)
        arrays[f"in_{name}"] = v
        T[name] = nc.dram_tensor(f"in_{name}", v.shape, _mybir.dt.from_np(v.dtype), kind="ExternalInput").ap()
    out = nc.dram_tensor("out_0", (N, D), F32, kind="ExternalOutput").ap()
    program(nc, T, out)
    r = _run(nc, [arrays], core_ids=[0])
    return r.results[0]["out_0"]
```
